# Optimizing a Trainium2 kernel written in Bass

```python
import numpy as np
import jax
import jax.numpy as jnp

def _softmax(x, axis=-1):
    return jax.nn.softmax(x, axis=axis)

def _gelu(x):
    return jax.nn.gelu(x, approximate=True)

def _silu(x):
    return jax.nn.silu(x)

def _sigmoid(x):
    return jax.nn.sigmoid(x)

def _layernorm(x, axis=-1, eps=1e-05):
    m = jnp.mean(x, axis=axis, keepdims=True)
    v = jnp.var(x, axis=axis, keepdims=True)
    return (x - m) / jnp.sqrt(v + eps)

def _scatter_add(tgt, idx, src, axis=0):
    return tgt.at[idx].add(src)

def _segment_sum(src, seg, n):
    return jax.ops.segment_sum(src, seg, n)
kernel_name = 'mk_xattn_ffn_d2_seqx_r8_2553f0'

def setup_inputs(seed: int=0):
    np.random.seed(seed)
    _w = jnp.asarray

    def _rec_inputs():
        import jax
        import jax.numpy as jnp
        _rk = jax.random.key(seed)
        x = 7.22e-05 + 1 * jax.random.normal(jax.random.fold_in(_rk, 1), (16, 64, 256), jnp.float32)
        _lenS = 64 - jax.random.randint(jax.random.fold_in(_rk, 7), (16,), 0, max(1, 64 // 4) + 1, jnp.int32)
        _lenS2 = 64 - jax.random.randint(jax.random.fold_in(_rk, 8), (16,), 0, max(1, 64 // 4) + 1, jnp.int32)
        _ctx_512P = jax.random.normal(jax.random.fold_in(_rk, 11), (16, 16, 64), jnp.float32)
        _ctx_512c = jax.random.dirichlet(jax.random.fold_in(_rk, 511), 0.3 * jnp.ones((16,), jnp.float32), (16, 64))
        _ctx_512t = jnp.einsum('bsk,bkd->bsd', _ctx_512c, _ctx_512P)
        _ctx_512t = _ctx_512t * jax.lax.rsqrt(jnp.mean(jnp.square(_ctx_512t)) + 1e-12) * 0.953939
        ctx_512 = -0.000514642 + 1.00011 * (_ctx_512t + 0.3 * jax.random.normal(jax.random.fold_in(_rk, 611), (16, 64, 64), jnp.float32))
        return (x, ctx_512)
    x, ctx_512 = _rec_inputs()

    def _L0_xattn_setup():
        import jax, jax.numpy as jnp
        import numpy as np
        B, S, E = (2, 256, 256)
        QH, KVH = (32, 8)
        D = E // QH
        G = QH // KVH
        DROPOUT = 1.0
        key = jax.random.key(seed)
        k1, k2, k3 = jax.random.split(key, 3)
        q = jax.random.normal(k1, (B, S, E), dtype=jnp.float32)
        k = jax.random.normal(k2, (B, S, E // G), dtype=jnp.float32)
        v = jax.random.normal(k3, (B, S, E // G), dtype=jnp.float32)
        return {'q': q, 'k': k, 'v': v}
    _L0_xattn_all = _L0_xattn_setup()
    _L0_xattn_in = {k: v for k, v in _L0_xattn_all.items() if k in ()}
    del _L0_xattn_all

    def _L0_ffn_setup():
        import jax, jax.numpy as jnp
        import numpy as np
        EPS = 1e-05
        TOP_K = 2

        def weight_quant(w):
            scale = 1.0 / jnp.maximum(jnp.mean(jnp.abs(w)), EPS)
            return jnp.clip(jnp.round(w * scale), -1.0, 1.0) / scale

        def activation_quant(x):
            scale = 127.0 / jnp.maximum(jnp.max(jnp.abs(x), axis=-1, keepdims=True), EPS)
            return jnp.clip(jnp.round(x * scale), -128.0, 127.0) / scale

        def bitlinear(x, w):
            w_q = w + jax.lax.stop_gradient(weight_quant(w) - w)
            x_q = x + jax.lax.stop_gradient(activation_quant(x) - x)
            return x_q @ w_q.T

        def expert_ffn(x, gw, uw, dw):
            gate = bitlinear(x, gw)
            up = bitlinear(x, uw)
            activated = up * jnp.square(jax.nn.relu(gate))
            return bitlinear(activated, dw)
        key = jax.random.key(seed)
        ks = jax.random.split(key, 5)
        B, S, H, I, E = (2, 256, 256, 512, 8)
        return {'hidden_states': jax.random.normal(ks[0], (B, S, H), dtype=jnp.float32), 'router_w': jax.random.normal(ks[1], (E, H), dtype=jnp.float32) * 0.02, 'gate_w': jax.random.normal(ks[2], (E, I, H), dtype=jnp.float32) * 0.02, 'up_w': jax.random.normal(ks[3], (E, I, H), dtype=jnp.float32) * 0.02, 'down_w': jax.random.normal(ks[4], (E, H, I), dtype=jnp.float32) * 0.02}
    _L0_ffn_all = _L0_ffn_setup()
    _L0_ffn_in = {k: v for k, v in _L0_ffn_all.items() if k in ('router_w', 'gate_w', 'up_w', 'down_w')}
    del _L0_ffn_all

    def _L1_xattn_setup():
        import jax, jax.numpy as jnp
        import numpy as np
        B, S, L = (2, 128, 128)
        DIM_Q, H, K, D_C, D_CQ, R = (256, 16, 128, 64, 192, 64)

        def _rope_tables(length, dim):
            inv = 1.0 / 10000.0 ** (jnp.arange(0, dim, 2, dtype=jnp.float32) / dim)
            f = jnp.arange(length, dtype=jnp.float32)[:, None] * inv[None, :]
            sin = jnp.repeat(jnp.sin(f), 2, axis=-1)
            cos = jnp.repeat(jnp.cos(f), 2, axis=-1)
            return (sin, cos)

        def _rotate_half(x):
            half = x.shape[-1] // 2
            return jnp.concatenate([-x[..., half:], x[..., :half]], axis=-1)

        def _apply_rope(x, sin, cos):
            return x * cos + _rotate_half(x) * sin
        key = jax.random.key(seed)
        ks = jax.random.split(key, 8)
        return {'hidden_q': jax.random.normal(ks[0], (B, S, DIM_Q), jnp.float32), 'kv_c': jax.random.normal(ks[1], (B, L, D_C), jnp.float32), 'Wq': jax.random.normal(ks[2], (H * K, DIM_Q), jnp.float32) / np.sqrt(DIM_Q).astype(np.float32), 'w_kc_q': jax.random.normal(ks[3], (H, K, D_CQ), jnp.float32) / np.sqrt(K).astype(np.float32), 'w_kc_kv': jax.random.normal(ks[4], (H, K, D_C), jnp.float32) / np.sqrt(K).astype(np.float32), 'W_qr': jax.random.normal(ks[5], (H, D_CQ, R), jnp.float32) / np.float32(np.sqrt(D_CQ) * np.sqrt(R)), 'W_kr': jax.random.normal(ks[6], (H, D_C, R), jnp.float32) / np.sqrt(D_C).astype(np.float32), 'Wo': jax.random.normal(ks[7], (DIM_Q, H * K), jnp.float32) / np.sqrt(H * K).astype(np.float32)}
    _L1_xattn_all = _L1_xattn_setup()
    _L1_xattn_in = {k: v for k, v in _L1_xattn_all.items() if k in ('Wq', 'w_kc_q', 'w_kc_kv', 'W_qr', 'W_kr', 'Wo')}
    del _L1_xattn_all

    def _L1_ffn_setup():
        import jax, jax.numpy as jnp
        import numpy as np
        B, S, D_IN, D_OUT, E = (4, 128, 256, 256, 32)
        MASK_DENSITY = 0.3
        THRESH = 0.5
        key = jax.random.key(seed)
        k_x, k_w, k_m, k_r = jax.random.split(key, 4)
        x = jax.random.normal(k_x, (B, S, D_IN), dtype=jnp.float32)
        bound = np.sqrt(1.0 / D_IN) * np.sqrt(3.0)
        weight = jax.random.uniform(k_w, (D_OUT, D_IN), minval=-bound, maxval=bound, dtype=jnp.float32)
        scale = jnp.ones((D_OUT,), dtype=jnp.float32)
        expert_masks = (jax.random.uniform(k_m, (E, D_OUT, D_IN)) < MASK_DENSITY).astype(jnp.float32)
        router_w = 0.01 * jax.random.normal(k_r, (E, D_IN), dtype=jnp.float32)
        return {'x': x, 'weight': weight, 'scale': scale, 'expert_masks': expert_masks, 'router_w': router_w}
    _L1_ffn_all = _L1_ffn_setup()
    _L1_ffn_in = {k: v for k, v in _L1_ffn_all.items() if k in ('weight', 'scale', 'expert_masks', 'router_w')}
    del _L1_ffn_all
    return {'x': x, 'ctx_512': ctx_512, 'L0_ffn_router_w': _L0_ffn_in['router_w'], 'L0_ffn_gate_w': _L0_ffn_in['gate_w'], 'L0_ffn_up_w': _L0_ffn_in['up_w'], 'L0_ffn_down_w': _L0_ffn_in['down_w'], 'L1_xattn_Wq': _L1_xattn_in['Wq'], 'L1_xattn_w_kc_q': _L1_xattn_in['w_kc_q'], 'L1_xattn_w_kc_kv': _L1_xattn_in['w_kc_kv'], 'L1_xattn_W_qr': _L1_xattn_in['W_qr'], 'L1_xattn_W_kr': _L1_xattn_in['W_kr'], 'L1_xattn_Wo': _L1_xattn_in['Wo'], 'L1_ffn_weight': _L1_ffn_in['weight'], 'L1_ffn_scale': _L1_ffn_in['scale'], 'L1_ffn_expert_masks': _L1_ffn_in['expert_masks'], 'L1_ffn_router_w': _L1_ffn_in['router_w']}

def reference(x, ctx_512, L0_ffn_router_w, L0_ffn_gate_w, L0_ffn_up_w, L0_ffn_down_w, L1_xattn_Wq, L1_xattn_w_kc_q, L1_xattn_w_kc_kv, L1_xattn_W_qr, L1_xattn_W_kr, L1_xattn_Wo, L1_ffn_weight, L1_ffn_scale, L1_ffn_expert_masks, L1_ffn_router_w):
    import jax
    import jax.numpy as jnp

    def _L0_xattn_ref(q, k, v):
        import jax, jax.numpy as jnp
        import numpy as np
        B, S, E = (2, 256, 256)
        QH, KVH = (32, 8)
        D = E // QH
        G = QH // KVH
        DROPOUT = 1.0
        b, s, _ = q.shape
        qh = q.reshape(b, s, KVH, G, D).transpose(0, 2, 3, 1, 4)
        kh = k.reshape(b, s, KVH, D).transpose(0, 2, 1, 3)
        vh = v.reshape(b, s, KVH, D).transpose(0, 2, 1, 3)
        scale = 1.0 / jnp.sqrt(jnp.float32(D))
        scores = jnp.einsum('bkgsd,bktd->bkgst', qh, kh) * scale
        attn = jax.nn.softmax(scores, axis=-1) / DROPOUT
        out = jnp.einsum('bkgst,bktd->bkgsd', attn, vh)
        return out.transpose(0, 3, 1, 2, 4).reshape(b, s, E)

    def _L0_ffn_ref(hidden_states, router_w, gate_w, up_w, down_w):
        import jax, jax.numpy as jnp
        import numpy as np
        EPS = 1e-05
        TOP_K = 2

        def weight_quant(w):
            scale = 1.0 / jnp.maximum(jnp.mean(jnp.abs(w)), EPS)
            return jnp.clip(jnp.round(w * scale), -1.0, 1.0) / scale

        def activation_quant(x):
            scale = 127.0 / jnp.maximum(jnp.max(jnp.abs(x), axis=-1, keepdims=True), EPS)
            return jnp.clip(jnp.round(x * scale), -128.0, 127.0) / scale

        def bitlinear(x, w):
            w_q = w + jax.lax.stop_gradient(weight_quant(w) - w)
            x_q = x + jax.lax.stop_gradient(activation_quant(x) - x)
            return x_q @ w_q.T

        def expert_ffn(x, gw, uw, dw):
            gate = bitlinear(x, gw)
            up = bitlinear(x, uw)
            activated = up * jnp.square(jax.nn.relu(gate))
            return bitlinear(activated, dw)
        B, S, H = hidden_states.shape
        E = router_w.shape[0]
        x = hidden_states.reshape(-1, H)
        logits = x @ router_w.T
        probs = jax.nn.softmax(logits, axis=-1)
        top_w, top_i = jax.lax.top_k(probs, TOP_K)
        top_w = top_w / jnp.sum(top_w, axis=-1, keepdims=True)
        combine = jnp.sum(top_w[..., None] * jax.nn.one_hot(top_i, E, dtype=x.dtype), axis=1)
        out = jnp.zeros_like(x)
        for e in range(E):
            y_e = expert_ffn(x, gate_w[e], up_w[e], down_w[e])
            out = out + combine[:, e:e + 1] * y_e
        return out.reshape(B, S, H)

    def _L1_xattn_ref(hidden_q, kv_c, Wq, w_kc_q, w_kc_kv, W_qr, W_kr, Wo):
        import jax, jax.numpy as jnp
        import numpy as np
        B, S, L = (2, 128, 128)
        DIM_Q, H, K, D_C, D_CQ, R = (256, 16, 128, 64, 192, 64)

        def _rope_tables(length, dim):
            inv = 1.0 / 10000.0 ** (jnp.arange(0, dim, 2, dtype=jnp.float32) / dim)
            f = jnp.arange(length, dtype=jnp.float32)[:, None] * inv[None, :]
            sin = jnp.repeat(jnp.sin(f), 2, axis=-1)
            cos = jnp.repeat(jnp.cos(f), 2, axis=-1)
            return (sin, cos)

        def _rotate_half(x):
            half = x.shape[-1] // 2
            return jnp.concatenate([-x[..., half:], x[..., :half]], axis=-1)

        def _apply_rope(x, sin, cos):
            return x * cos + _rotate_half(x) * sin
        Bv, Sv, _ = hidden_q.shape
        _, Lv, _ = kv_c.shape
        q_hk = (hidden_q @ Wq.T).reshape(Bv, Sv, H, K)
        q_big = jnp.einsum('bshk,hkq->bshq', q_hk, w_kc_q)
        sin_q, cos_q = _rope_tables(Sv, D_CQ)
        q_big = _apply_rope(q_big, sin_q[None, :, None, :], cos_q[None, :, None, :])
        sin_k, cos_k = _rope_tables(Lv, D_C)
        kv_r = _apply_rope(kv_c, sin_k[None], cos_k[None])
        q_r = jnp.einsum('bshq,hqr->bhsr', q_big, W_qr)
        k_r = jnp.einsum('bld,hdr->bhlr', kv_r, W_kr)
        scores = jnp.einsum('bhsr,bhlr->bhsl', q_r, k_r)
        attn = jax.nn.softmax(scores, axis=-1)
        ctx_c = jnp.einsum('bhsl,bld->bhsd', attn, kv_r)
        ctx_lat = jnp.einsum('bhsd,hkd->bhsk', ctx_c, w_kc_kv)
        ctx = ctx_lat.transpose(0, 2, 1, 3).reshape(Bv, Sv, H * K)
        return ctx @ Wo.T

    def _L1_ffn_ref(x, weight, scale, expert_masks, router_w):
        import jax, jax.numpy as jnp
        import numpy as np
        B, S, D_IN, D_OUT, E = (4, 128, 256, 256, 32)
        MASK_DENSITY = 0.3
        THRESH = 0.5
        logits = jnp.einsum('bsd,ed->bse', x, router_w)
        probs = jax.nn.softmax(logits, axis=-1)
        top1_w = jnp.max(probs, axis=-1)
        top1_idx = jnp.argmax(probs, axis=-1)
        w_q = jnp.clip(jnp.round(weight / THRESH), -1.0, 1.0)
        w_scaled = w_q * scale[:, None]
        out0 = jnp.zeros((x.shape[0], x.shape[1], weight.shape[0]), dtype=x.dtype)

        def body(out, inputs):
            e_idx, mask_e = inputs
            y = jnp.einsum('bsi,oi->bso', x, w_scaled * mask_e)
            sel = (top1_idx == e_idx)[..., None]
            out = jnp.where(sel, y * top1_w[..., None], out)
            return (out, None)
        out, _ = jax.lax.scan(body, out0, (jnp.arange(E), expert_masks))
        return out
    x = x + _L0_xattn_ref(_layernorm(x, axis=-1), ctx_512, ctx_512)
    x = x + _L0_ffn_ref(_layernorm(x, axis=-1), L0_ffn_router_w, L0_ffn_gate_w, L0_ffn_up_w, L0_ffn_down_w)
    x = x + _L1_xattn_ref(_layernorm(x, axis=-1), ctx_512, L1_xattn_Wq, L1_xattn_w_kc_q, L1_xattn_w_kc_kv, L1_xattn_W_qr, L1_xattn_W_kr, L1_xattn_Wo)
    x = x + _L1_ffn_ref(_layernorm(x, axis=-1), L1_ffn_weight, L1_ffn_scale, L1_ffn_expert_masks, L1_ffn_router_w)
    return x

_drawn_inputs = setup_inputs


def setup_inputs(seed=0):
    import zlib

    import numpy as np

    out = dict(_drawn_inputs(seed))
    spreads = {'L1_ffn_scale': (1.0, 0.2)}
    factors = {'L0_ffn_router_w': 8.0,
     'L0_ffn_gate_w': 8.0,
     'L0_ffn_up_w': 8.0,
     'L0_ffn_down_w': 8.0,
     'L1_xattn_Wq': 4.464,
     'L1_xattn_w_kc_q': 4.484,
     'L1_xattn_W_qr': 4.456,
     'L1_xattn_W_kr': 4.399}
    for name, (base, spread) in spreads.items():
        noise = np.random.default_rng([zlib.crc32(name.encode()), seed]).standard_normal(out[name].shape)
        drawn = base * np.exp(spread * noise) if base else spread * noise
        out[name] = jnp.asarray(drawn.astype(out[name].dtype))
    for name, factor in factors.items():
        out[name] = (out[name] * factor).astype(out[name].dtype)
    return out
```

```python
from contextlib import ExitStack

import numpy as np

import concourse.bass as bass
from concourse import mybir

F32, BF16, I32, U32 = mybir.dt.float32, mybir.dt.bfloat16, mybir.dt.int32, mybir.dt.uint32
ALU, ACT, AX = mybir.AluOpType, mybir.ActivationFunctionType, mybir.AxisListType
P = 128
NT = 8
H = 256
S = 64
NPAIR = 16
NKV = 8
HD = 8
NTERM = 6
KROWS = NTERM * 2 * HD
EPS = 1e-5
MAGIC = 1.5 * 2.0 ** 23
NE = 8
FF = 512
NBLK = 24
XROW = 258
QMAX = 127.0
NE_D = 32
NBLK_D = 40

NH = 16
NU = NH // 2
KD = 128
QD = 192
NUNIT = 6
UNITS = [(0, 0), (0, 1), (2, 0), (2, 1), (1, 0), (1, 1)]
SBUF_BASE, SBUF_END = 16512, 229344

C_HEAD, C_HALF, C_IOTA, C_TOKEN, C_KCOS, C_KSIN, C_QCOS = 0, 2, 4, 52, 64, 128, 192
C_W = C_QCOS + 3 * 2 * S
Q_SCALE = float(np.float32(1.0) / np.sqrt(np.float32(HD)))


class Chain:

    def __init__(self, eng, sem):
        self.eng, self.sem, self.base, self.n = eng, sem, 0, 0

    def __call__(self, ins):
        self.n += 1
        ins.then_inc(self.sem, 1)
        self.eng.wait_ge(self.sem, self.base + self.n)

    def enter(self, i, per):
        self.start = self.base + self.n
        self.base, self.n = self.start + i * per, 0

    def leave(self, trips, per):
        assert self.n == per, (self.n, per)
        self.base, self.n = self.start + trips * per, 0


class Routing:

    def __init__(self, sb, s, n_e, n_blk, choices):
        n = choices * NT
        self.n_e, self.n_blk, self.choices = n_e, n_blk, choices
        self.logits = sb(f"logits{s}", [P, NT, n_e])
        self.top = sb(f"top{s}", [P, NT, 8])
        self.top_i = sb(f"top_i{s}", [P, NT, 8], U32)
        self.top_f = sb(f"top_f{s}", [P, NT, choices])
        self.hot = sb(f"hot{s}", [P, choices, NT, n_e])
        self.hot_b = sb(f"hot_b{s}", [P, NT, n_e], BF16)
        self.rank = sb(f"rank{s}", [P, NT, n_e])
        self.tots = sb(f"tots{s}", [P, NT, n_e])
        self.counts = sb(f"counts{s}", [P, 4, n_e])
        self.counts_i = sb(f"counts_i{s}", [P, n_e], I32)
        self.picked = sb(f"picked{s}", [P, 2, NT, n_e])
        self.spot = sb(f"spot{s}", [P, 6, n])
        self.spot_i = sb(f"spot_i{s}", [P, n], I32)
        self.y_index = sb(f"y_index{s}", [P, n], U32)
        self.inv_index = sb(f"inv_index{s}", [P, n], U32)
        self.owner = sb(f"owner{s}", [P, n_blk], U32)
        self.below = sb(f"below{s}", [P, n_blk, n_e])
        self.block_e = sb(f"block_e{s}", [P, n_blk])
        self.block_ei = sb(f"block_ei{s}", [P, n_blk], U32)


def build(nc, x, ctx_in, cst_in, router_w, gate_w, up_w, down_w, wq, w_kc_q, w_kc_kv, w_qr, w_kr, wo,
          weight, scale, masks, router_d, out):
    with ExitStack() as ctx:
        place = [SBUF_BASE]

        def sb(name, shape, dt=F32):
            n = int(np.prod(shape[1:])) * (2 if dt == BF16 else 4)
            at = place[0]
            place[0] = (at + n + 31) // 32 * 32
            return nc.alloc_sbuf_tensor_at(name, shape, dt, offset=at)

        def sem(name):
            return ctx.enter_context(nc.semaphore(name))

        bank = [ctx.enter_context(nc.psum_tensor(f"bank{i}", [P, 512], F32)) for i in range(8)]
        X = sb("X", [P, NT, H])
        ctxn = sb("ctxn", [P, NT, S])
        ctx2 = sb("ctx2", [P, 2 * NT, S])
        cst = sb("cst", [P, C_W])
        ident = sb("ident", [P, P], BF16)
        token = sb("token", [P, NT], U32)
        zeros = sb("zeros", [P, NBLK + NBLK_D])

        stats = sb("stats", [P, NT, 6])
        mv = sb("mv", [P, NT, 2])
        var = sb("var", [P, NT])
        half_bits = sb("half_bits", [P, NT], I32)
        rstd = sb("rstd", [P, NT])
        root_tmp = sb("root_tmp", [P, 2, NT])
        identf = sb("identf", [P, P])
        ones = sb("ones", [P, P])
        ones_b = sb("ones_b", [P, P], BF16)
        before = sb("before", [P, P], BF16)
        row_max = sb("row_max", [P, 4, NT])
        mask_m = sb("mask_m", [P, 2 * P])
        kvr = sb("kvr", [P, NT, 2, S])
        kvr2 = sb("kvr2", [P, 2 * NT, S])
        rot = sb("rot", [P, 2 * NT, S])
        kvrT = sb("kvrT", [P, NT * P])
        b_place = place[0]
        raw = [sb(f"raw{i}", [P, 3, 4 * H]) for i in range(2)]
        w_junk = sb("w_junk", [P, 3, 4 * H], BF16)
        w_sum = [sb(f"w_sum{i}", [P, 3]) for i in range(2)]
        w_sum2 = sb("w_sum2", [P, 3])
        magic = sb("magic", [P, 1])
        w_rec = [sb(f"w_rec{i}", [P, 3]) for i in range(2)]
        w_mean = sb("w_mean", [P, NE, 3])
        tern = [sb(f"tern{i}", [P, 3, 4 * H], BF16) for i in range(2)]
        WGU = sb("WGU", [P, NE, 2, 2, FF], BF16)
        WD = sb("WD", [P, NE, 4, H], BF16)
        r_raw = sb("r_raw", [NE, H])
        rT = sb("rT", [P, 2, NE])
        RB = Routing(sb, "_b", NE, NBLK, 2)
        gate = sb("gate", [P, 2, NT])
        below2 = sb("below2", [P, NBLK, NE])
        block_w = sb("block_w", [P, 2, NBLK])
        w_prod = sb("w_prod", [P, 2, NE])
        hs = [sb(f"hs{i}", [P, 6]) for i in range(2)]
        a_place = place[0]
        qn = sb("qn", [P, H])
        q_parts = [sb(f"q_parts{i}", [P, NPAIR, NTERM, 2 * HD], BF16) for i in range(2)]
        k_parts = [sb(f"k_parts{i}", [P, NKV, NTERM, 2, HD], BF16) for i in range(2)]
        q_rest = sb("q_rest", [P, H])
        k_rest = sb("k_rest", [P, NT, S])
        k_split = sb("k_split", [P, NT, 3, S], BF16)
        k_all = sb("k_all", [P, NT, NKV, NTERM, 2, HD], BF16)
        v_all = sb("v_all", [P, 2 * NT, NKV, 2, HD + 1])
        qT = [sb(f"qT{i}", [KROWS, NPAIR * P], BF16) for i in range(2)]
        kT = [sb(f"kT{i}", [KROWS, NKV, 2, 2, S], BF16) for i in range(2)]
        negsel = sb("negsel", [96, NPAIR, 2, S], BF16)
        v_blk = [sb(f"v_blk{i}", [P, 2, NKV, 2, HD + 1]) for i in range(2)]
        mx = sb("mx", [P, 32])
        mx_rest = sb("mx_rest", [P, 2, 32])
        mx_parts = sb("mx_parts", [P, 3, 32], BF16)
        mxT = [sb(f"mxT{i}", [96, P], BF16) for i in range(2)]
        pT = [sb(f"pT{i}", [P, 512]) for i in range(4)]
        den_rec = sb("den_rec", [P, 32])
        att = sb("att", [P, H])
        place[0] = a_place
        xq32 = sb("xq32", [P, NT, H])
        xrow = sb("xrow", [P, NT, XROW], BF16)
        xg = [sb(f"xg{i}", [P, XROW], BF16) for i in range(4)]
        xgT = [sb(f"xgT{i}", [P, H], BF16) for i in range(2)]
        relu = [sb(f"relu{i}", [P, FF]) for i in range(2)]
        hid = [sb(f"hid{i}", [P, FF]) for i in range(2)]
        hid_q = [sb(f"hid_q{i}", [P, FF], BF16) for i in range(2)]
        hidT = [sb(f"hidT{i}", [P, FF], BF16) for i in range(2)]
        y = [sb(f"y{i}", [P, H]) for i in range(2)]
        yg = sb("yg", [P, NT, 2, H])
        assert place[0] <= SBUF_END - 2 * 4 * NT * H
        place[0] = SBUF_END - 2 * 4 * NT * H
        XN = sb("XN", [P, NT, H])
        XNT = sb("XNT", [P, 2, NT * P])
        place[0] = b_place
        f_wq = [sb(f"f_wq{i}", [P, 2, H]) for i in range(2)]
        f_kcq = [sb(f"f_kcq{i}", [P, 2, QD]) for i in range(2)]
        f_wo = [sb(f"f_wo{i}", [P, 2, 2 * KD]) for i in range(2)]
        f_kv = [sb(f"f_kv{i}", [P, 2, S]) for i in range(2)]
        f_qr = [sb(f"f_qr{i}", [P, 3, S]) for i in range(2)]
        f_kr = [sb(f"f_kr{i}", [P, S]) for i in range(2)]
        woT = sb("woT", [P, 2, H])
        qrwT = sb("qrwT", [S, 2, 2, QD])
        krT = sb("krT", [S, P])
        AW = [sb(f"AW{i}", [P, 2, 2 * QD]) for i in range(2)]
        MW = [sb(f"MW{i}", [P, 2, 2 * P]) for i in range(2)]
        VW = sb("VW", [P, NU, H])
        roped = [sb(f"roped{i}", [P, 2, 512]) for i in range(NUNIT)]
        qrT = sb("qrT", [P, NT * P])
        prob = sb("prob", [P, NT, 2, S])
        probT = sb("probT", [P, NT * P])
        s_stat = sb("s_stat", [P, 2, 3, NT])
        ctxT = sb("ctxT", [P, NU, NT * P])
        c_end = place[0]
        m_raw = [sb(f"m_raw{i}", [P, 4, 2, H]) for i in range(4)]
        w_raw = sb("w_raw", [P, 2, H])
        o_scale = sb("o_scale", [P, 2])
        rd_raw = sb("rd_raw", [NE_D, H])
        assert place[0] <= SBUF_END - 2 * 4 * NT * H
        place[0] = b_place
        WE = sb("WE", [P, NE_D, 2, H])
        wT = sb("wT", [P, 2, H])
        rdT = sb("rdT", [P, 2, NE_D])
        RD = Routing(sb, "_d", NE_D, NBLK_D, 1)
        l_exp = sb("l_exp", [P, NT, NE_D])
        top_w = sb("top_w", [P, 2, NT])
        dg = [sb(f"dg{i}", [P, H]) for i in range(4)]
        dgT = [sb(f"dgT{i}", [P, H]) for i in range(2)]
        z = [sb(f"z{i}", [P, H]) for i in range(2)]
        zg = sb("zg", [P, NT, H])
        assert place[0] <= c_end
        n_rows = nc.dram_tensor("n_rows", (NT * P, H), F32).ap()
        owners_d = nc.dram_tensor("owners_d", (P * NBLK_D, 1), U32).ap()
        z_rows = nc.dram_tensor("z_rows", (NBLK_D * P, H), F32).ap()
        x_rows = nc.dram_tensor("x_rows", (NT * P, XROW // 2), U32).ap()
        owners = nc.dram_tensor("owners", (P * NBLK, 1), U32).ap()
        y_rows = nc.dram_tensor("y_rows", (NBLK * P, H), F32).ap()

        x_loaded, ctx_loaded, out_stored = sem("x_loaded"), sem("ctx_loaded"), sem("out_stored")
        consts_built = sem("consts_built")
        stats_ready, rstd_ready = sem("stats_ready"), sem("rstd_ready")
        bconsts_built, negsel_built, v_all_ready = sem("bconsts_built"), sem("negsel_built"), sem("v_all_ready")
        parts_ready, v_ready = sem("parts_ready"), sem("v_ready")
        turned, k_unturned, q_unturned = sem("turned"), sem("k_unturned"), sem("q_unturned")
        nat_ready, nat_read = sem("nat_ready"), sem("nat_read")
        mx_ready, mx_turned, mxT_ready = sem("mx_ready"), sem("mx_turned"), sem("mxT_ready")
        scores_ready, probs_ready, probs_used = sem("scores_ready"), sem("probs_ready"), sem("probs_used")
        att_read, x1_ready = sem("att_read"), sem("x1_ready")
        dve_chain, pool_chain = sem("dve_chain"), sem("pool_chain")

        raw_loaded = [sem(f"raw_loaded{i}") for i in range(2)]
        raw_used, w_summed, w_total, w_rec_ready, w_scaled = (sem(n) for n in ("raw_used", "w_summed", "w_total", "w_rec_ready", "w_scaled"))
        tern_ready, tern_turned, tern_done = sem("tern_ready"), sem("tern_turned"), sem("tern_done")
        magic_set = sem("magic_set")
        r_loaded, r_turned, r_ready = sem("r_loaded"), sem("r_turned"), sem("r_ready")
        XN_ready, XN_turned, XNT_ready, logits_ready = sem("XN_ready"), sem("XN_turned"), sem("XNT_ready"), sem("logits_ready")
        xs_ready, xq_ready, xrow_ready, xrow_stored = sem("xs_ready"), sem("xq_ready"), sem("xrow_ready"), sem("xrow_stored")
        gap_ready, gate_exp, hot_ready, counted = sem("gap_ready"), sem("gate_exp"), sem("hot_ready"), sem("counted")
        spots_ready, owner_zeroed, owner_stored, owner_loaded = sem("spots_ready"), sem("owner_zeroed"), sem("owner_stored"), sem("owner_loaded")
        block_e_ready, rank_read = sem("block_e_ready"), sem("rank_read")
        gathered = [sem(f"gathered{i}") for i in range(4)]
        xg_turned, xgT_ready, xg_read, gu_ready, relu_ready = (sem(n) for n in ("xg_turned", "xgT_ready", "xg_read", "gu_ready", "relu_ready"))
        hid_done, hq_ready, h_turned, hT_ready, y_ready, y_copied = (sem(n) for n in ("hid_done", "hq_ready", "h_turned", "hT_ready", "y_ready", "y_copied"))
        y_stored = [sem(f"y_stored{i}") for i in range(2)]
        y_back, x2_ready = sem("y_back"), sem("x2_ready")
        kv_rotated, kv_turned, kvrT_ready, mask_built = sem("kv_rotated"), sem("kv_turned"), sem("kvrT_ready"), sem("mask_built")
        f_loaded = [sem(f"f_loaded{i}") for i in range(2)]
        A_ready, A_done, wo_turned, woT_done = (sem(n) for n in ("A_ready", "A_done", "wo_turned", "woT_done"))
        qr_turned, qrwT_done, V_ready, V_done, M_ready, M_done = (sem(n) for n in ("qr_turned", "qrwT_done", "V_ready", "V_done", "M_ready", "M_done"))
        q_ready, roped_ready, keyed, qrT_ready = (sem(n) for n in ("q_ready", "roped_ready", "keyed", "qrT_ready"))
        s_ready, s_less, s_exp, prob_ready = (sem(n) for n in ("s_ready", "s_less", "s_exp", "prob_ready"))
        prob_turned, probT_ready, c_ready, ctxT_ready = (sem(n) for n in ("prob_turned", "probT_ready", "c_ready", "ctxT_ready"))
        o_ready, x3_ready, pe_waited = sem("o_ready"), sem("x3_ready"), sem("pe_waited")
        m_loaded = [sem(f"m_loaded{i}") for i in range(4)]
        d_loaded, w_scaled_d, w_turned_d, wT_ready, rdT_ready = (sem(n) for n in ("d_loaded", "w_scaled_d", "w_turned_d", "wT_ready", "rdT_ready"))
        m_turned, WE_ready, n_stored, less_ready, l_exp_ready = (sem(n) for n in ("m_turned", "WE_ready", "n_stored", "less_ready", "l_exp_ready"))
        d_gathered = [sem(f"d_gathered{i}") for i in range(4)]
        dg_turned, dgT_ready, z_ready, z_copied, z_back, x4_ready = (sem(n) for n in ("dg_turned", "dgT_ready", "z_ready", "z_copied", "z_back", "x4_ready"))
        z_stored = [sem(f"z_stored{i}") for i in range(2)]

        block = ctx.enter_context(nc.Block())

        def row(a, t):
            return a[:, bass.ds(t, 1), :].rearrange("p a d -> p (a d)")

        def inverse_root(pool, link, c):
            y, v = rstd[:, c], var[:, c]
            a, b = root_tmp[:, 0, c], root_tmp[:, 1, c]
            link(pool.tensor_scalar(y.bitcast(I32), half_bits[:, c], -1.0, float(0x5F3759DF), ALU.mult, ALU.add))
            for _ in range(3):
                link(pool.tensor_tensor(a, y, y, ALU.mult))
                link(pool.tensor_tensor(b, a, v, ALU.mult))
                link(pool.tensor_scalar(a, b, -0.5, 1.5, ALU.mult, ALU.add))
                link(pool.tensor_tensor(y, y, a, ALU.mult))

        def positions(dve, link, R, nth):
            n_e, n_blk = R.n_e, R.n_blk
            for t in range(1, NT):
                link(dve.tensor_tensor(R.rank[:, t, :], R.rank[:, t, :], R.tots[:, t - 1, :], ALU.add))
                link(dve.tensor_tensor(R.tots[:, t, :], R.tots[:, t, :], R.tots[:, t - 1, :], ALU.add))
            nb, upto, start = (R.counts[:, i, :] for i in range(3))
            link(dve.tensor_scalar(R.counts_i[:], R.tots[:, NT - 1, :], float(P - 1), None, ALU.add))
            link(dve.tensor_scalar(R.counts_i[:], R.counts_i[:], 7, None, ALU.arith_shift_right))
            link(dve.tensor_copy(nb, R.counts_i[:]))
            link(dve.tensor_tensor_scan(upto, ones[:, 0:n_e], nb, 0.0, ALU.mult, ALU.add))
            link(dve.tensor_tensor(start, upto, nb, ALU.subtract))
            for k in range(R.choices):
                c = slice(k * NT, (k + 1) * NT)
                link(dve.tensor_tensor(R.picked[:, 0], R.hot[:, k], R.rank[:], ALU.mult))
                link(dve.tensor_reduce(R.spot[:, 0, c], R.picked[:, 0], AX.X, ALU.add))
                link(dve.tensor_tensor(R.picked[:, 1], R.hot[:, k], start[:, None, :].to_broadcast([P, NT, n_e]), ALU.mult))
                link(dve.tensor_reduce(R.spot[:, 1, c], R.picked[:, 1], AX.X, ALU.add))
            rank, first, hi, lo, blk = (R.spot[:, i, :] for i in range(5))
            link(dve.tensor_copy(R.spot_i[:], rank))
            link(dve.tensor_scalar(R.spot_i[:], R.spot_i[:], 7, None, ALU.arith_shift_right))
            link(dve.tensor_copy(hi, R.spot_i[:]))
            link(dve.scalar_tensor_tensor(lo, hi, -float(P), rank, ALU.mult, ALU.add))
            link(dve.tensor_tensor(blk, first, hi, ALU.add))
            link(dve.scalar_tensor_tensor(R.inv_index[:], lo, float(n_blk), blk, ALU.mult, ALU.add))
            dve.scalar_tensor_tensor(R.y_index[:], blk, float(P), lo, ALU.mult, ALU.add).then_inc(spots_ready, 1)
            link(dve.tensor_tensor(R.below[:], upto[:, None, :].to_broadcast([P, n_blk, n_e]),
                                   cst[:, C_IOTA:C_IOTA + n_blk, None].to_broadcast([P, n_blk, n_e]), ALU.is_le))
            link(dve.tensor_reduce(R.block_e[:], R.below[:], AX.X, ALU.add))
            link(dve.tensor_scalar(R.block_e[:], R.block_e[:], float(n_e - 1), None, ALU.min))
            dve.tensor_copy(R.block_ei[:], R.block_e[:]).then_inc(block_e_ready, 1)
            dve.wait_ge(block_e_ready, nth)

        def best(dve, link, R):
            for t in range(NT):
                link(dve.max(R.top[:, t, :], R.logits[:, t, :]))
                ins = dve.max_index(R.top_i[:, t, :], R.top[:, t, :], R.logits[:, t, :])
            link(ins)

        def mark(dve, link, R):
            link(dve.tensor_copy(R.top_f[:], R.top_i[:, :, 0:R.choices]))
            for k in range(R.choices):
                link(dve.tensor_tensor(R.hot[:, k], R.top_f[:, :, k:k + 1].to_broadcast([P, NT, R.n_e]),
                                       cst[:, None, C_IOTA:C_IOTA + R.n_e].to_broadcast([P, NT, R.n_e]), ALU.is_equal))

        @block.sync
        def _(sp):
            sp.dma_start(X[:], x.rearrange("(t p) d -> p t d", p=P)).then_inc(x_loaded, 16)
            sp.dma_start(ctxn[:], ctx_in.rearrange("(t p) d -> p t d", p=P)).then_inc(ctx_loaded, 16)
            for g in range(2):
                sp.dma_start(ctx2[64 * g:64 * g + 64], ctx_in.rearrange("(b s) d -> s b d", s=S)).then_inc(ctx_loaded, 16)
            sp.dma_start(cst[:], cst_in).then_inc(ctx_loaded, 16)
            sp.dma_start(r_raw[:], router_w).then_inc(r_loaded, 16)
            with sp.Fori(0, NE // 2) as i:
                for par in range(2):
                    sp.wait_ge(raw_used, 2 * i + par + 1)
                    for m, w in enumerate((gate_w, up_w, down_w)):
                        sp.dma_start(raw[par][:, m, :].rearrange("p (c h) -> p c h", h=w.shape[2]),
                                     w[bass.ds(2 * i + par, 1)].rearrange("a (c p) h -> p (a c) h", p=P)).then_inc(raw_loaded[par], 16)
            sp.wait_ge(xrow_ready, 1)
            sp.dma_start(x_rows.rearrange("(t p) d -> p t d", p=P), xrow[:].bitcast(U32)).then_inc(xrow_stored, 16)
            sp.wait_ge(owner_stored, 16 * 2 * NT)
            sp.dma_start(RB.owner[:], owners.rearrange("(p j) a -> p (j a)", p=P)).then_inc(owner_loaded, 16)
            for par in range(2):
                sp.sem_inc(y_stored[par], 16)
            with sp.Fori(0, NBLK // 2) as i:
                for par in range(2):
                    sp.wait_ge(y_copied, 2 * i + par + 2)
                    sp.dma_start(y_rows[bass.ds((2 * i + par) * P, P), :], y[par][:]).then_inc(y_stored[par], 16)
            sp.wait_ge(x2_ready, NT)
            for c, (dst, src) in enumerate(((w_raw, weight.rearrange("(c p) i -> p c i", p=P)), (o_scale, scale), (rd_raw, router_d))):
                sp.dma_start(dst[:], src).then_inc(d_loaded, 16)
            with sp.Fori(0, NU // 2) as i:
                for par in range(2):
                    u = 2 * i + par
                    sp.wait_ge(V_ready, u + 1)
                    for dst, src in ((f_wq, wq.rearrange("(h k) i -> k h i", k=KD)[:, bass.ds(2 * u, 2), :]),
                                     (f_kcq, w_kc_q.rearrange("h k q -> k h q")[:, bass.ds(2 * u, 2), :]),
                                     (f_wo, wo.rearrange("(c o) n -> o c n", o=P)[:, :, bass.ds(2 * KD * u, 2 * KD)]),
                                     (f_kv, w_kc_kv.rearrange("h k d -> k h d")[:, bass.ds(2 * u, 2), :]),
                                     (f_qr, w_qr.rearrange("(u c p) r -> u p c r", c=3, p=P)[bass.ds(u, 1)].rearrange("a p c r -> p (a c) r")),
                                     (f_kr, w_kr[bass.ds(P * u, P), :])):
                        sp.dma_start(dst[par][:], src).then_inc(f_loaded[par], 16)
            def load_masks(g):
                sp.dma_start(m_raw[g % 4][:], masks[4 * g:4 * g + 4].rearrange("e (c p) i -> p e c i", p=P)).then_inc(m_loaded[g % 4], 16)

            for g in range(4):
                load_masks(g)
            sp.wait_ge(XN_ready, 3)
            sp.dma_start(n_rows.rearrange("(t p) d -> p t d", p=P), XN[:]).then_inc(n_stored, 16)
            sp.wait_ge(owner_stored, 16 * 3 * NT)
            sp.dma_start(RD.owner[:], owners_d.rearrange("(p j) a -> p (j a)", p=P)).then_inc(owner_loaded, 16)
            for g in range(4, 8):
                sp.wait_ge(m_turned, 4 * (g - 3) + 4)
                load_masks(g)
            for par in range(2):
                sp.sem_inc(z_stored[par], 16)
            with sp.Fori(0, NBLK_D // 2) as i:
                for par in range(2):
                    sp.wait_ge(z_copied, 2 * i + par + 3)
                    sp.dma_start(z_rows[bass.ds((2 * i + par) * P, P), :], z[par][:]).then_inc(z_stored[par], 16)
            for t in range(NT):
                sp.wait_ge(x4_ready, t + 1)
                sp.dma_start(out[t * P:(t + 1) * P, :], X[:, t, :]).then_inc(out_stored, 16)
            sp.wait_ge(out_stored, 16 * NT)

        @block.gpsimd
        def _(pool):
            link = Chain(pool, pool_chain)
            link(pool.memset(ident[:], 0.0))
            pool.affine_select(out=ident[:], in_=ident[:], compare_op=ALU.not_equal, fill=1.0, base=0,
                               pattern=[[-1, P]], channel_multiplier=1).then_inc(consts_built, 1)
            pool.wait_ge(stats_ready, 1)
            inverse_root(pool, link, slice(0, NT))
            pool.tensor_scalar(rstd[:], rstd[:], Q_SCALE, None, ALU.mult).then_inc(rstd_ready, 1)
            pool.wait_ge(ctx_loaded, 64)
            for g in range(2):
                pool.tensor_tensor(v_all[:, :, :, g, 0:HD], ctx2[:].rearrange("p b (k d) -> p b k d", d=HD),
                                   cst[:, 2 + g:3 + g, None, None].to_broadcast([P, 2 * NT, NKV, HD]), ALU.mult).then_inc(v_all_ready, 1)
                pool.tensor_copy(v_all[:, :, :, g, HD], cst[:, 2 + g:3 + g, None].to_broadcast([P, 2 * NT, NKV])).then_inc(v_all_ready, 1)
            link(pool.memset(negsel[:], 0.0))
            for s in range(3):
                link(pool.affine_select(out=negsel[32 * s:32 * s + 32], in_=negsel[32 * s:32 * s + 32],
                                        compare_op=ALU.not_equal, fill=-1.0, base=0,
                                        pattern=[[-2, NPAIR], [-1, 2], [0, S]], channel_multiplier=1))
            pool.nop().then_inc(negsel_built, 1)
            pool.memset(ones[:], 1.0).then_inc(bconsts_built, 1)
            pool.memset(ones_b[:], 1.0).then_inc(bconsts_built, 1)
            link(pool.memset(identf[:], 0.0))
            pool.affine_select(out=identf[:], in_=identf[:], compare_op=ALU.not_equal, fill=1.0, base=0,
                               pattern=[[-1, P]], channel_multiplier=1).then_inc(bconsts_built, 1)
            link(pool.memset(before[:], 0.0))
            pool.affine_select(out=before[:], in_=before[:], compare_op=ALU.is_ge, fill=1.0, base=0,
                               pattern=[[-1, P]], channel_multiplier=1).then_inc(bconsts_built, 1)
            link(pool.memset(zeros[:], 0.0))
            pool.dma_start(owners.rearrange("(p j) a -> p (j a)", p=P), zeros[:, 0:NBLK].bitcast(U32)).then_inc(owner_zeroed, 16)
            pool.dma_start(owners_d.rearrange("(p j) a -> p (j a)", p=P), zeros[:, NBLK:NBLK + NBLK_D].bitcast(U32)).then_inc(owner_zeroed, 16)
            pool.tensor_copy(token[:], cst[:, C_TOKEN:C_TOKEN + NT]).then_inc(bconsts_built, 1)
            link(pool.memset(mask_m[:], 1.0))
            link(pool.memset(mask_m[0:64, P:P + 64], 0.0))
            link(pool.memset(mask_m[64:P, 64:P], 0.0))
            for dst, src in ((kvr2[:], ctx2[:]), (kvr[:, :, 0, :], ctxn[:])):
                n = src.shape[1]
                r = rot[:, 0:n, :]
                cos = cst[:, None, C_KCOS:C_KCOS + S].to_broadcast([P, n, S])
                sin = cst[:, None, C_KSIN:C_KSIN + S].to_broadcast([P, n, S])
                link(pool.tensor_tensor(dst, src, cos, ALU.mult))
                link(pool.tensor_tensor(r[:, :, 0:32], src[:, :, 32:64], sin[:, :, 0:32], ALU.mult))
                link(pool.tensor_tensor(r[:, :, 32:64], src[:, :, 0:32], sin[:, :, 32:64], ALU.mult))
                link(pool.tensor_tensor(dst, dst, r, ALU.add))
            pool.tensor_copy(kvr[:, :, 1, :], kvr[:, :, 0, :]).then_inc(kv_rotated, 1)
            pool.wait_ge(stats_ready, 2)
            inverse_root(pool, link, slice(0, NT))
            pool.nop().then_inc(rstd_ready, 1)
            pool.wait_ge(owner_zeroed, 32)
            pool.wait_ge(spots_ready, 1)
            for t in range(NT):
                for k in range(2):
                    c = k * NT + t
                    pool.indirect_dma_start(out=owners, out_offset=bass.IndirectOffsetOnAxis(ap=RB.inv_index[:, c:c + 1], axis=0),
                                            in_=token[:, t:t + 1], in_offset=None).then_inc(owner_stored, 16)
            pool.wait_ge(xrow_stored, 16)
            pool.wait_ge(owner_loaded, 16)
            for j in range(NBLK):
                if j >= 4:
                    pool.wait_ge(xg_turned, j - 3)
                    pool.wait_ge(xg_read, j - 3)
                    pool.wait_ge(gathered[j % 4], 16 * (j // 4))
                pool.indirect_dma_start(out=xg[j % 4][:].bitcast(U32), out_offset=None, in_=x_rows,
                                        in_offset=bass.IndirectOffsetOnAxis(ap=RB.owner[:, j:j + 1], axis=0)).then_inc(gathered[j % 4], 16)
            for par in range(2):
                pool.wait_ge(y_stored[par], 16 * (NBLK // 2) + 16)
            for t in range(NT):
                for k in range(2):
                    c = k * NT + t
                    pool.indirect_dma_start(out=yg[:, t, k, :], out_offset=None, in_=y_rows,
                                            in_offset=bass.IndirectOffsetOnAxis(ap=RB.y_index[:, c:c + 1], axis=0)).then_inc(y_back, 16)
            for n in (3, 4):
                pool.wait_ge(stats_ready, n)
                inverse_root(pool, link, slice(0, NT))
                pool.nop().then_inc(rstd_ready, 1)
            pool.wait_ge(spots_ready, 2)
            for t in range(NT):
                pool.indirect_dma_start(out=owners_d, out_offset=bass.IndirectOffsetOnAxis(ap=RD.inv_index[:, t:t + 1], axis=0),
                                        in_=token[:, t:t + 1], in_offset=None).then_inc(owner_stored, 16)
            pool.wait_ge(n_stored, 16)
            pool.wait_ge(owner_loaded, 32)
            for j in range(NBLK_D):
                if j >= 4:
                    pool.wait_ge(dg_turned, j - 3)
                pool.indirect_dma_start(out=dg[j % 4][:], out_offset=None, in_=n_rows,
                                        in_offset=bass.IndirectOffsetOnAxis(ap=RD.owner[:, j:j + 1], axis=0)).then_inc(d_gathered[j % 4], 16)
            for par in range(2):
                pool.wait_ge(z_stored[par], 16 * (NBLK_D // 2) + 16)
            for t in range(NT):
                pool.indirect_dma_start(out=zg[:, t, :], out_offset=None, in_=z_rows,
                                        in_offset=bass.IndirectOffsetOnAxis(ap=RD.y_index[:, t:t + 1], axis=0)).then_inc(z_back, 16)

        @block.tensor
        def _(pe):
            pe.sem_inc(turned, 6)
            pe.sem_inc(scores_ready, 8)
            pe.sem_inc(probs_used, 8)
            pe.wait_ge(consts_built, 1)

            def turn(t, par):
                pe.wait_ge(parts_ready, t + 1)
                k = k_parts[par][:].rearrange("p k a g d -> p k (a g d)")
                q = q_parts[par][:].rearrange("p r a e -> p r (a e)")
                for u, src in enumerate((k, q[:, 0:8, :], q[:, 8:16, :])):
                    T = bank[(3 * par + u) % 2].bitcast(BF16)
                    if u < 2:
                        pe.wait_ge(q_unturned, 2 * t + u + 1)
                    else:
                        pe.wait_ge(k_unturned, t + 1)
                    for j in range(8):
                        mm = pe.transpose(T[0:KROWS, j * P:(j + 1) * P], src[:, j, :], ident[:])
                    mm.then_inc(turned, 1)

            def natural(t, par):
                pe.wait_ge(k_unturned, t + 1)
                pe.wait_ge(q_unturned, 2 * t + 4)
                for q in range(4):
                    pe.wait_ge(nat_read, 4 * t + q + 1)
                    for j in range(4):
                        for b in range(2):
                            r = 4 * q + j
                            mm = pe.matmul(bank[2 + q % 2][64 * b:64 * b + 64, j * P:(j + 1) * P],
                                           qT[par][:, r * P + 64 * b:r * P + 64 * b + 64],
                                           kT[par][:, r // 2, b, :, :].rearrange("p g s -> p (g s)"), start=True, stop=True)
                    mm.then_inc(nat_ready, 1)

            def turn_max(t):
                pe.wait_ge(mx_ready, t + 1)
                pe.transpose(bank[6].bitcast(BF16)[0:96, 0:P], mx_parts[:].rearrange("p a h -> p (a h)"),
                             ident[:]).then_inc(mx_turned, 1)

            def attend(t, par, units):
                pe.wait_ge(mxT_ready, t + 1)
                for q in units:
                    if q < 4:
                        B = bank[4 + q % 2]
                        pe.wait_ge(probs_ready, 4 * t + q + 1)
                        for j in range(4):
                            for b in range(2):
                                r = 4 * q + j
                                o = B[:, (2 * j + b) * 64:(2 * j + b) * 64 + 64]
                                pe.matmul(o, kT[par][:, r // 2, b, :, :].rearrange("p g s -> p (g s)"),
                                          qT[par][:, r * P + 64 * b:r * P + 64 * b + 64], start=True, stop=False)
                                mm = pe.matmul(o, negsel[:, r, :, :].rearrange("p g s -> p (g s)"),
                                               mxT[par][:, 64 * b:64 * b + 64], start=False, stop=True)
                        mm.then_inc(scores_ready, 1)
                    if q == 1:
                        pe.wait_ge(att_read, t + 1)
                        pe.wait_ge(v_ready, t + 1)
                    if q >= 1:
                        pe.wait_ge(probs_ready, 4 * t + q + 2)
                        for j in range(4):
                            for b in range(2):
                                r = 4 * (q - 1) + j
                                mm = pe.matmul(bank[7][64 * b:64 * b + 64, r * 18:r * 18 + 18],
                                               pT[q - 1][:, (2 * j + b) * 64:(2 * j + b) * 64 + 64],
                                               v_blk[par][:, b, r // 2, :, :].rearrange("p g e -> p (g e)"), start=True, stop=True)
                        mm.then_inc(probs_used, 1)

            turn(0, 0)
            natural(0, 0)
            turn_max(0)
            pe.wait_ge(negsel_built, 1)
            with pe.Fori(0, NT // 2 - 1) as i:
                for t, par in ((2 * i, 0), (2 * i + 1, 1)):
                    turn(t + 1, 1 - par)
                    attend(t, par, (0, 1))
                    natural(t + 1, 1 - par)
                    attend(t, par, (2, 3, 4))
                    turn_max(t + 1)
            turn(NT - 1, 1)
            attend(NT - 2, 0, (0, 1))
            natural(NT - 1, 1)
            attend(NT - 2, 0, (2, 3, 4))
            turn_max(NT - 1)
            attend(NT - 1, 1, range(5))

            pe.wait_ge(bconsts_built, 5)
            pe.wait_ge(x1_ready, NT)
            pe.sem_inc(tern_turned, 6)
            pe.sem_inc(w_total, 2)

            def weights(e, par):
                pe.wait_ge(w_summed, e + 1)
                if par == 0:
                    pe.wait_ge(tern_done, 3 * e + 1)
                pe.wait_ge(w_rec_ready, e + 1)
                pe.matmul(bank[7][:, 0:3], ones[:], w_sum[par][:], start=True, stop=True).then_inc(w_total, 1)
                for m in range(3):
                    pe.wait_ge(tern_ready, 3 * e + m + 1)
                    pe.wait_ge(tern_done, 3 * e + m + 1)
                    B = bank[m].bitcast(BF16)
                    for c in range(4 if m < 2 else 2):
                        for k in range(2 if m < 2 else 4):
                            src = tern[par][:, m, (c * 2 + k if m < 2 else c * 4 + k) * P:][:, 0:P]
                            o = k * FF + c * P if m < 2 else k * H + c * P
                            mm = pe.transpose(B[:, o:o + P], src, ident[:])
                    mm.then_inc(tern_turned, 1)

            with pe.Fori(0, NE // 2) as i:
                weights(2 * i, 0)
                weights(2 * i + 1, 1)

            pe.wait_ge(r_loaded, 16)
            for k in range(2):
                mm = pe.transpose(bank[3][:, k * NE:(k + 1) * NE], r_raw[:, k * P:(k + 1) * P], identf[0:NE, 0:NE])
            mm.then_inc(r_turned, 1)
            pe.wait_ge(XN_ready, 1)
            for h in range(NT // 2):
                for k in range(2):
                    for t in range(2):
                        mm = pe.transpose(bank[4 + h % 4][:, (2 * k + t) * P:(2 * k + t + 1) * P],
                                          XN[:, 2 * h + t, k * P:(k + 1) * P], identf[:])
                mm.then_inc(XN_turned, 1)
            pe.wait_ge(r_ready, 1)
            for t in range(NT):
                pe.wait_ge(XNT_ready, t // 2 + 1)
                for k in range(2):
                    mm = pe.matmul(bank[3][:, 64 + t * NE:64 + (t + 1) * NE], XNT[:, k, t * P:(t + 1) * P], rT[:, k, :],
                                   start=k == 0, stop=k == 1)
            mm.then_inc(logits_ready, 1)
            pe.wait_ge(hot_ready, 1)
            pe.matmul(bank[4][:, 0:NT * NE], before[:], RB.hot_b[:].rearrange("p t e -> p (t e)"), start=True, stop=True)
            pe.matmul(bank[4][:, 64:64 + NT * NE], ones_b[:], RB.hot_b[:].rearrange("p t e -> p (t e)"),
                      start=True, stop=True).then_inc(counted, 1)

            pe.wait_ge(block_e_ready, 1)
            pe.wait_ge(rank_read, 1)

            def turn_rows(j, q, r):
                pe.wait_ge(gathered[r], 16 * q + 16)
                pe.wait_ge(xgT_ready, j + 1)
                for k in range(2):
                    mm = pe.transpose(bank[0].bitcast(BF16)[:, k * P:(k + 1) * P], xg[r][:, k * P:(k + 1) * P], ident[:])
                mm.then_inc(xg_turned, 1)

            def gate_up(j, par):
                e = pe.value_load(RB.block_ei[0:1, bass.ds(j, 1)], min_val=0, max_val=NE - 1)
                pe.wait_ge(xgT_ready, j + 2)
                pe.wait_ge(hid_done, j + 1)
                for k in range(2):
                    for m in range(2):
                        mm = pe.matmul(bank[1 + 2 * m + par][:], xgT[par][:, k * P:(k + 1) * P],
                                       WGU[:, bass.ds(e, 1), k, m, :].rearrange("p a i -> p (a i)"), start=k == 0, stop=k == 1)
                mm.then_inc(gu_ready, 1)

            def turn_hidden(j, par):
                pe.wait_ge(hq_ready, j + 1)
                pe.wait_ge(hT_ready, j + 1)
                for k in range(4):
                    mm = pe.transpose(bank[5].bitcast(BF16)[:, k * P:(k + 1) * P], hid_q[par][:, k * P:(k + 1) * P], ident[:])
                mm.then_inc(h_turned, 1)

            def down(j, par):
                e = pe.value_load(RB.block_ei[0:1, bass.ds(j, 1)], min_val=0, max_val=NE - 1)
                pe.wait_ge(hT_ready, j + 2)
                pe.wait_ge(y_copied, j + 1)
                for k in range(4):
                    mm = pe.matmul(bank[6][:, 0:H], hidT[par][:, k * P:(k + 1) * P],
                                   WD[:, bass.ds(e, 1), k, :].rearrange("p a o -> p (a o)"), start=k == 0, stop=k == 3)
                mm.then_inc(y_ready, 1)

            turn_rows(0, 0, 0)
            turn_rows(1, 0, 1)
            gate_up(0, 0)
            with pe.Fori(0, NBLK // 4 - 1) as i:
                for r in range(4):
                    j = 4 * i + r
                    turn_rows(j + 2, i + (r + 2) // 4, (r + 2) % 4)
                    turn_hidden(j, r % 2)
                    gate_up(j + 1, (r + 1) % 2)
                    down(j, r % 2)
            for j in range(NBLK - 4, NBLK):
                if j + 2 < NBLK:
                    turn_rows(j + 2, (j + 2) // 4, (j + 2) % 4)
                turn_hidden(j, j % 2)
                if j + 1 < NBLK:
                    gate_up(j + 1, (j + 1) % 2)
                down(j, j % 2)

            pe.wait_ge(kv_rotated, 1)
            pe.wait_ge(x2_ready, NT)
            for t in range(NT):
                mm = pe.transpose(bank[4 + t // 4][:, (t % 4) * P:(t % 4 + 1) * P], kvr[:, t].rearrange("p a d -> p (a d)"), identf[:])
            mm.then_inc(kv_turned, 1)
            pe.wait_ge(XN_ready, 2)
            for h in range(NT // 2):
                for k in range(2):
                    for t in range(2):
                        mm = pe.transpose(bank[h][:, (2 * k + t) * P:(2 * k + t + 1) * P],
                                          XN[:, 2 * h + t, k * P:(k + 1) * P], identf[:])
                mm.then_inc(XN_turned, 1)
            pe.wait_ge(kvrT_ready, 2)
            pe.wait_ge(XNT_ready, NT)
            pe.sem_inc(V_ready, 2)
            pe.sem_inc(keyed, 2)
            pe.sem_inc(s_ready, 1)
            pe.sem_inc(c_ready, 1)

            def fold(u, q, par):
                pe.wait_ge(f_loaded[par], 96 * q + 96)
                for c in range(2):
                    pe.wait_ge(s_less, 2 * u + 1 + c)
                    for h in range(2):
                        mm = pe.matmul(bank[4 + c][:, h * QD:(h + 1) * QD], f_wq[par][:, h, c * P:(c + 1) * P],
                                       f_kcq[par][:, h, :], start=True, stop=True)
                    mm.then_inc(A_ready, 1)
                pe.wait_ge(roped_ready, NUNIT * u + 2)
                for h in range(2):
                    for c in range(2):
                        mm = pe.transpose(bank[0][:, h * H + c * P:h * H + (c + 1) * P], f_wo[par][:, c, h * KD:(h + 1) * KD], identf[:])
                mm.then_inc(wo_turned, 1)
                for c in range(3):
                    pe.transpose(bank[1][0:S, c * P:(c + 1) * P], f_qr[par][:, c, :], identf[:])
                pe.transpose(bank[1][0:S, 3 * P:4 * P], f_kr[par][:], identf[:]).then_inc(qr_turned, 1)
                pe.wait_ge(qrT_ready, 2 * u + 2)
                pe.wait_ge(woT_done, u + 1)
                for h in range(2):
                    mm = pe.matmul(bank[2][h * S:(h + 1) * S, 0:H], f_kv[par][:, h, :], woT[:, h, :], start=True, stop=True)
                mm.then_inc(V_ready, 1)
                pe.wait_ge(qrwT_done, u + 1)
                for r in range(2):
                    for c, (at, n) in enumerate(((0, 64), (64, 128), (192, 64))):
                        k0 = 64 if c == 2 else 0
                        mm = pe.matmul(bank[3][:, r * 2 * P + at:r * 2 * P + at + n],
                                       qrwT[:, r, :, :].rearrange("p h q -> p (h q)")[:, c * P:(c + 1) * P],
                                       krT[:, k0:k0 + n], start=True, stop=True)
                mm.then_inc(M_ready, 1)

            def rotated(u, par):
                pe.wait_ge(A_done, 2 * u + 2)
                pe.wait_ge(woT_done, u + 1)
                pe.wait_ge(qrwT_done, u + 1)

                def project(n):
                    c, g = UNITS[n]
                    pe.wait_ge(roped_ready, NUNIT * u + n + 1)
                    for k in range(2):
                        mm = pe.matmul(bank[g][:], AW[par][:, k, c * P:(c + 1) * P], XNT[:, k, g * 512:(g + 1) * 512],
                                       start=k == 0, stop=k == 1)
                    mm.then_inc(q_ready, 1)

                def to_keys_outer(g):
                    pe.wait_ge(roped_ready, NUNIT * u + 2 + g + 3)
                    for r in range(2):
                        for h, n, at in ((0, g, 0), (1, 2 + g, 192)):
                            pe.matmul(bank[2 + g][h * S:(h + 1) * S, :], MW[par][:, r, at:at + S], roped[n][:, r, :],
                                      start=r == 0, stop=False, skip_group_check=True)

                def to_keys_middle(g):
                    pe.wait_ge(roped_ready, NUNIT * u + 4 + g + 3)
                    for r in range(2):
                        mm = pe.matmul(bank[2 + g][:], MW[par][:, r, 64:192], roped[4 + g][:, r, :],
                                       start=False, stop=r == 1, skip_group_check=True)
                    mm.then_inc(keyed, 1)

                for n in range(4):
                    project(n)
                pe.wait_ge(V_done, u + 1)
                pe.wait_ge(M_done, u + 1)
                to_keys_outer(0)
                project(4)
                to_keys_outer(1)
                project(5)
                to_keys_middle(0)
                to_keys_middle(1)

            def scores(u, last=False):
                pe.wait_ge(qrT_ready, 2 * u + 4)
                pe.wait_ge(A_done, 2 * u + (2 if last else 4))
                pe.sem_inc(pe_waited, 1)
                for b in range(2 * NT):
                    for h in range(2):
                        mm = pe.matmul(bank[4 + h][64 * (b % 2):64 * (b % 2) + 64, (b // 2) * S:(b // 2 + 1) * S],
                                       qrT[h * S:(h + 1) * S, b * S:(b + 1) * S], kvrT[h * S:(h + 1) * S, b * S:(b + 1) * S],
                                       start=True, stop=True)
                mm.then_inc(s_ready, 1)

            def turn_probs(u):
                pe.wait_ge(prob_ready, 2 * u + 2)
                for t in range(NT):
                    if t % 4 == 0:
                        pe.wait_ge(ctxT_ready, 2 * u + t // 4 + 1)
                    mm = pe.transpose(bank[6 + t // 4][:, (t % 4) * P:(t % 4 + 1) * P], prob[:, t].rearrange("p h l -> p (h l)"), identf[:])
                    if t % 4 == 3:
                        mm.then_inc(prob_turned, 1)

            def contexts(u):
                pe.wait_ge(probT_ready, 2 * u + 2)
                pe.sem_inc(pe_waited, 1)
                for n in range(2 * NT):
                    for h in range(2):
                        b = (n + NT * h) % (2 * NT)
                        mm = pe.matmul(bank[6 + b // NT][h * S:(h + 1) * S, (b % NT) * S:(b % NT + 1) * S], kvr2[h * S:(h + 1) * S, b, :],
                                       probT[h * S:(h + 1) * S, b * S:(b + 1) * S], start=True, stop=True)
                mm.then_inc(c_ready, 1)

            fold(0, 0, 0)
            rotated(0, 0)
            fold(1, 0, 1)
            scores(0)
            with pe.Fori(0, NU // 2 - 1) as i:
                for u, q, par in ((2 * i + 1, i + 1, 1), (2 * i + 2, i + 1, 0)):
                    rotated(u, par)
                    turn_probs(u - 1)
                    fold(u + 1, q, 1 - par)
                    scores(u)
                    contexts(u - 1)
            rotated(NU - 1, 1)
            turn_probs(NU - 2)
            pe.wait_ge(s_less, 2 * (NU - 1) + 4)
            scores(NU - 1, last=True)
            contexts(NU - 2)
            turn_probs(NU - 1)
            contexts(NU - 1)
            pe.wait_ge(ctxT_ready, 2 * NU + 2)
            for t in range(NT):
                for u in range(NU):
                    mm = pe.matmul(bank[t // 2][:, (t % 2) * H:(t % 2 + 1) * H], ctxT[:, u, t * P:(t + 1) * P], VW[:, u, :],
                                   start=u == 0, stop=u == NU - 1)
                if t % 2:
                    mm.then_inc(o_ready, 1)

            pe.wait_ge(w_scaled_d, 1)
            for c in range(2):
                for k in range(2):
                    mm = pe.transpose(bank[6][:, k * H + c * P:k * H + (c + 1) * P], w_raw[:, c, k * P:(k + 1) * P], identf[:])
            for k in range(2):
                mm = pe.transpose(bank[7][:, k * NE_D:(k + 1) * NE_D], rd_raw[:, k * P:(k + 1) * P], identf[0:NE_D, 0:NE_D])
            mm.then_inc(w_turned_d, 1)
            pe.wait_ge(XN_ready, 3)
            for h in range(NT // 2):
                for k in range(2):
                    for t in range(2):
                        mm = pe.transpose(bank[h][:, (2 * k + t) * P:(2 * k + t + 1) * P],
                                          XN[:, 2 * h + t, k * P:(k + 1) * P], identf[:])
                mm.then_inc(XN_turned, 1)
            pe.wait_ge(rdT_ready, 1)
            for t in range(NT):
                pe.wait_ge(XNT_ready, NT + t // 2 + 1)
                for k in range(2):
                    mm = pe.matmul(bank[4][:, t * NE_D:(t + 1) * NE_D], XNT[:, k, t * P:(t + 1) * P], rdT[:, k, :],
                                   start=k == 0, stop=k == 1)
            mm.then_inc(logits_ready, 1)
            pe.wait_ge(hot_ready, 2)
            pe.matmul(bank[5][:, 0:NT * NE_D], before[:], RD.hot_b[:].rearrange("p t e -> p (t e)"), start=True, stop=True)
            pe.matmul(bank[5][:, NT * NE_D:], ones_b[:], RD.hot_b[:].rearrange("p t e -> p (t e)"),
                      start=True, stop=True).then_inc(counted, 1)
            pe.sem_inc(m_turned, 4)
            pe.sem_inc(z_ready, 2)
            with pe.Fori(0, 2) as i:
                for e in range(16):
                    pe.wait_ge(m_loaded[e // 4], 16 * i + 16)
                    pe.wait_ge(WE_ready, 16 * i + e + 1)
                    for c in range(2):
                        for k in range(2):
                            mm = pe.transpose(bank[e % 4][:, k * H + c * P:k * H + (c + 1) * P],
                                              m_raw[e // 4][:, e % 4, c, k * P:(k + 1) * P], identf[:])
                    mm.then_inc(m_turned, 1)
            pe.wait_ge(WE_ready, NE_D + 4)
            pe.wait_ge(block_e_ready, 2)
            pe.wait_ge(rank_read, 2)

            def turn_d(j, q, r):
                pe.wait_ge(d_gathered[r], 16 * q + 16)
                pe.wait_ge(dgT_ready, j + 1)
                for k in range(2):
                    mm = pe.transpose(bank[4 + r % 2][:, k * P:(k + 1) * P], dg[r][:, k * P:(k + 1) * P], identf[:])
                mm.then_inc(dg_turned, 1)

            def expert_d(j, par):
                e = pe.value_load(RD.block_ei[0:1, bass.ds(j, 1)], min_val=0, max_val=NE_D - 1)
                pe.wait_ge(dgT_ready, j + 3)
                pe.wait_ge(z_copied, j + 1)
                for k in range(2):
                    mm = pe.matmul(bank[6 + par][:, 0:H], dgT[par][:, k * P:(k + 1) * P],
                                   WE[:, bass.ds(e, 1), k, :].rearrange("p a o -> p (a o)"), start=k == 0, stop=k == 1)
                mm.then_inc(z_ready, 1)

            turn_d(0, 0, 0)
            with pe.Fori(0, NBLK_D // 4 - 1) as i:
                for r in range(4):
                    turn_d(4 * i + r + 1, i + (r + 1) // 4, (r + 1) % 4)
                    expert_d(4 * i + r, r % 2)
            for j in range(NBLK_D - 4, NBLK_D):
                if j + 1 < NBLK_D:
                    turn_d(j + 1, (j + 1) // 4, (j + 1) % 4)
                expert_d(j, j % 2)

        @block.scalar
        def _(act):
            act.sem_inc(probs_ready, 2)
            act.sem_inc(q_unturned, 2)

            def unturn(t, par):
                act.wait_ge(scores_ready, 4 * t + 4)
                for u in (1, 2):
                    act.wait_ge(turned, 3 * t + u + 7)
                    c = (u - 1) * 8 * P
                    act.activation(qT[par][:, c:c + 8 * P], bank[(3 * par + u) % 2].bitcast(BF16)[0:KROWS, 0:8 * P],
                                   ACT.Copy).then_inc(q_unturned, 1)

            def exps(t):
                for q in range(4):
                    act.wait_ge(scores_ready, 4 * t + q + 9)
                    act.wait_ge(probs_used, 4 * t + q + 5)
                    act.activation(pT[q][:], bank[4 + q % 2][:], ACT.Exp).then_inc(probs_ready, 1)

            unturn(0, 0)
            with act.Fori(0, NT // 2 - 1) as i:
                for t, par in ((2 * i, 0), (2 * i + 1, 1)):
                    unturn(t + 1, 1 - par)
                    exps(t)
            unturn(NT - 1, 1)
            exps(NT - 2)
            exps(NT - 1)

            def weights(e, h, par):
                act.wait_ge(raw_loaded[par], 48 * h + 48)
                act.wait_ge(w_total, e + 1)
                for m in range(3):
                    ins = act.activation(w_junk[:, m, :], raw[par][:, m, :], ACT.Abs, accum_out=w_sum[par][:, m:m + 1])
                ins.then_inc(w_summed, 1)
                act.wait_ge(w_rec_ready, e + 2)
                for m in range(3):
                    act.activation(raw[par][:, m, :], raw[par][:, m, :], ACT.Identity, scale=w_rec[par][:, m:m + 1],
                                   bias=magic[:]).then_inc(w_scaled, 1)

            act.wait_ge(magic_set, 1)
            with act.Fori(0, NE // 2) as i:
                weights(2 * i, i, 0)
                weights(2 * i + 1, i, 1)
            act.wait_ge(r_turned, 1)
            act.activation(rT[:].rearrange("p k e -> p (k e)"), bank[3][:, 0:2 * NE], ACT.Copy).then_inc(r_ready, 1)
            for h in range(NT // 2):
                act.wait_ge(XN_turned, h + 1)
                act.activation(XNT[:, :, 2 * h * P:2 * (h + 1) * P], bank[4 + h % 4][:].rearrange("p (k n) -> p k n", k=2),
                               ACT.Copy).then_inc(XNT_ready, 1)
            act.wait_ge(xs_ready, 1)
            for t in range(NT):
                act.activation(xq32[:, t, :], XN[:, t, :], ACT.Identity, scale=row_max[:, 1, t:t + 1], bias=magic[:]).then_inc(xq_ready, 1)
            act.wait_ge(gap_ready, 1)
            act.activation(gate[:, 1, :], gate[:, 0, :], ACT.Exp).then_inc(gate_exp, 1)
            act.sem_inc(xgT_ready, 1)
            act.sem_inc(hT_ready, 1)
            act.sem_inc(y_copied, 1)

            def rows(j, par):
                act.wait_ge(xg_turned, j + 1)
                act.activation(xgT[par][:], bank[0].bitcast(BF16)[:, 0:H], ACT.Copy).then_inc(xgT_ready, 1)

            def relus(j, par):
                act.wait_ge(gu_ready, j + 1)
                act.wait_ge(hid_done, j + 1)
                act.activation(relu[par][:], bank[1 + par][:], ACT.Relu).then_inc(relu_ready, 1)

            def hidden_rows(j, par):
                act.wait_ge(h_turned, j + 1)
                act.activation(hidT[par][:], bank[5].bitcast(BF16)[:, 0:FF], ACT.Copy).then_inc(hT_ready, 1)

            def outputs(j, h, par):
                act.wait_ge(y_ready, j + 1)
                act.wait_ge(y_stored[par], 16 * h + 16)
                act.activation(y[par][:], bank[6][:, 0:H], ACT.Copy, scale=hs[par][:, 5:6]).then_inc(y_copied, 1)

            rows(0, 0)
            rows(1, 1)
            relus(0, 0)
            with act.Fori(0, NBLK // 2 - 1) as i:
                for par in range(2):
                    j = 2 * i + par
                    rows(j + 2, par)
                    hidden_rows(j, par)
                    relus(j + 1, 1 - par)
                    outputs(j, i, par)
            hidden_rows(NBLK - 2, 0)
            relus(NBLK - 1, 1)
            outputs(NBLK - 2, NBLK // 2 - 1, 0)
            hidden_rows(NBLK - 1, 1)
            outputs(NBLK - 1, NBLK // 2 - 1, 1)

            act.wait_ge(kv_turned, 1)
            for h in range(2):
                act.activation(kvrT[:, h * 512:(h + 1) * 512], bank[4 + h][:], ACT.Copy).then_inc(kvrT_ready, 1)
            for h in range(NT // 2):
                act.wait_ge(XN_turned, NT // 2 + h + 1)
                act.activation(XNT[:, :, 2 * h * P:2 * (h + 1) * P], bank[h][:].rearrange("p (k n) -> p k n", k=2),
                               ACT.Copy).then_inc(XNT_ready, 1)
            act.sem_inc(qrT_ready, 2)
            act.sem_inc(ctxT_ready, 2)

            def fold(u, par):
                for c in range(2):
                    act.wait_ge(A_ready, 2 * u + c + 1)
                    act.activation(AW[par][:, c, :], bank[4 + c][:, 0:2 * QD], ACT.Copy).then_inc(A_done, 1)
                act.wait_ge(wo_turned, u + 1)
                act.activation(woT[:].rearrange("p h o -> p (h o)"), bank[0][:], ACT.Copy).then_inc(woT_done, 1)
                act.wait_ge(V_ready, u + 3)
                act.activation(VW[:, bass.ds(u, 1), :].rearrange("p a o -> p (a o)"), bank[2][:, 0:H], ACT.Copy).then_inc(V_done, 1)

            def exps(u):
                for h in range(2):
                    act.wait_ge(s_less, 2 * u + h + 5)
                    act.activation(prob[:, :, h, :], prob[:, :, h, :], ACT.Exp).then_inc(s_exp, 1)

            def queries(u):
                for g in range(2):
                    act.wait_ge(keyed, 2 * u + g + 3)
                    act.wait_ge(s_ready, u + 1)
                    act.activation(qrT[:, g * 512:(g + 1) * 512], bank[2 + g][:], ACT.Copy).then_inc(qrT_ready, 1)

            def probs(u):
                for g in range(2):
                    act.wait_ge(prob_turned, 2 * u + g + 1)
                    act.wait_ge(c_ready, u + 1)
                    act.activation(probT[:, g * 512:(g + 1) * 512], bank[6 + g][:], ACT.Copy).then_inc(probT_ready, 1)

            def contexts(u):
                act.wait_ge(c_ready, u + 2)
                for g in range(2):
                    act.activation(ctxT[:, bass.ds(u, 1), g * 512:(g + 1) * 512].rearrange("p a n -> p (a n)"), bank[6 + g][:],
                                   ACT.Copy).then_inc(ctxT_ready, 1)

            fold(0, 0)
            queries(0)
            fold(1, 1)
            with act.Fori(0, NU // 2 - 1) as i:
                for u, par in ((2 * i + 1, 1), (2 * i + 2, 0)):
                    exps(u - 1)
                    queries(u)
                    probs(u - 1)
                    fold(u + 1, 1 - par)
                    contexts(u - 1)
            exps(NU - 2)
            queries(NU - 1)
            probs(NU - 2)
            contexts(NU - 2)
            exps(NU - 1)
            probs(NU - 1)
            contexts(NU - 1)

            act.wait_ge(w_turned_d, 1)
            act.activation(rdT[:].rearrange("p k e -> p (k e)"), bank[7][:, 0:2 * NE_D], ACT.Copy).then_inc(rdT_ready, 1)
            for h in range(NT // 2):
                act.wait_ge(XN_turned, NT + h + 1)
                act.activation(XNT[:, :, 2 * h * P:2 * (h + 1) * P], bank[h][:].rearrange("p (k n) -> p k n", k=2),
                               ACT.Copy).then_inc(XNT_ready, 1)
            act.wait_ge(less_ready, 1)
            act.activation(l_exp[:], l_exp[:], ACT.Exp).then_inc(l_exp_ready, 1)
            act.sem_inc(dgT_ready, 2)
            with act.Fori(0, NBLK_D // 2) as i:
                for par in range(2):
                    j = 2 * i + par
                    act.wait_ge(dg_turned, j + 1)
                    act.wait_ge(z_ready, j + 1)
                    act.activation(dgT[par][:], bank[4 + par][:, 0:H], ACT.Copy).then_inc(dgT_ready, 1)

        @block.vector
        def _(dve):
            link = Chain(dve, dve_chain)
            dve.sem_inc(nat_read, 2)
            dve.sem_inc(att_read, 1)
            dve.wait_ge(x_loaded, 16)
            for t in range(NT):
                link(dve.bn_stats(stats[:, t, :], X[:, t, :]))
                link(dve.bn_aggr(mv[:, t, :], stats[:, t, :]))
            link(dve.tensor_scalar(var[:], mv[:, :, 1], EPS, None, ALU.add))
            dve.tensor_scalar(half_bits[:], var[:].bitcast(I32), 1, None, ALU.arith_shift_right).then_inc(stats_ready, 1)
            dve.wait_ge(ctx_loaded, 64)
            link(dve.tensor_copy(k_split[:, :, 0, :], ctxn[:]))
            link(dve.tensor_tensor(k_rest[:], ctxn[:], k_split[:, :, 0, :], ALU.subtract))
            link(dve.tensor_copy(k_split[:, :, 1, :], k_rest[:]))
            link(dve.tensor_tensor(k_split[:, :, 2, :], k_rest[:], k_split[:, :, 1, :], ALU.subtract))
            for term, part in enumerate((0, 1, 2, 0, 1, 0)):
                for g in range(2):
                    link(dve.tensor_copy(k_all[:, :, :, term, g, :],
                                         k_split[:, :, part, :].rearrange("p t (k d) -> p t k d", d=HD)))
            dve.wait_ge(rstd_ready, 1)

            def parts(t, par):
                Q = q_parts[par]
                qv = qn[:].rearrange("p (r e) -> p r e", e=2 * HD)
                qr = q_rest[:].rearrange("p (r e) -> p r e", e=2 * HD)
                link(dve.tensor_scalar(qn[:], row(X, t), row(mv, t)[:, 0:1], rstd[:, bass.ds(t, 1)], ALU.subtract, ALU.mult))
                dve.wait_ge(turned, 3 * t + 3)
                link(dve.tensor_copy(Q[:, :, 0, :], qv))
                link(dve.tensor_tensor(qr, qv, Q[:, :, 0, :], ALU.subtract))
                link(dve.tensor_copy(Q[:, :, 3, :], qr))
                dve.tensor_copy(Q[:, :, 1, :], Q[:, :, 0, :])
                dve.tensor_copy(Q[:, :, 2, :], Q[:, :, 0, :])
                dve.tensor_copy(Q[:, :, 4, :], Q[:, :, 3, :])
                dve.tensor_copy(k_parts[par][:].rearrange("p k a g d -> p (k a g d)"),
                                k_all[:, bass.ds(t, 1)].rearrange("p t k a g d -> p (t k a g d)"))
                dve.tensor_tensor(Q[:, :, 5, :], qr, Q[:, :, 3, :], ALU.subtract).then_inc(parts_ready, 1)

            def values(t, par):
                dve.tensor_copy(v_blk[par][:].rearrange("p b k g e -> p (b k g e)"),
                                v_all[:, bass.ds(2 * t, 2)].rearrange("p b k g e -> p (b k g e)")).then_inc(v_ready, 1)

            def unturn(t, par):
                dve.wait_ge(scores_ready, 4 * t + 4)
                dve.wait_ge(turned, 3 * t + 7)
                T = bank[(3 * par) % 2].bitcast(BF16)[0:KROWS, 0:8 * P].rearrange("p (k b s) -> p k b s", b=2, s=S)
                for g in range(2):
                    ins = dve.tensor_scalar(kT[par][:, :, :, g, :], T, cst[0:KROWS, g:g + 1], None, ALU.mult)
                ins.then_inc(k_unturned, 1)

            def maxima(t):
                for q in range(4):
                    dve.wait_ge(nat_ready, 4 * t + q + 1)
                    dve.tensor_reduce(mx[:, 8 * q:8 * q + 8], bank[2 + q % 2][:].rearrange("p (h s) -> p h s", s=S),
                                      AX.X, ALU.max).then_inc(nat_read, 1)
                dve.wait_ge(nat_read, 4 * t + 6)
                link(dve.tensor_copy(mx_parts[:, 0, :], mx[:]))
                link(dve.tensor_tensor(mx_rest[:, 0, :], mx[:], mx_parts[:, 0, :], ALU.subtract))
                link(dve.tensor_copy(mx_parts[:, 1, :], mx_rest[:, 0, :]))
                dve.tensor_tensor(mx_parts[:, 2, :], mx_rest[:, 0, :], mx_parts[:, 1, :], ALU.subtract).then_inc(mx_ready, 1)

            def unturn_max(t, par):
                dve.wait_ge(mx_turned, t + 1)
                dve.tensor_copy(mxT[par][:], bank[6].bitcast(BF16)[0:96, 0:P]).then_inc(mxT_ready, 1)

            def add_att(t):
                dve.wait_ge(probs_used, 4 * t + 12)
                o = bank[7][:, 0:NPAIR * 18].rearrange("p (h e) -> p h e", e=HD + 1)
                link(dve.reciprocal(den_rec[:], o[:, :, HD]))
                dve.tensor_tensor(att[:].rearrange("p (h d) -> p h d", d=HD), o[:, :, 0:HD],
                                  den_rec[:, :, None].to_broadcast([P, 32, HD]), ALU.mult).then_inc(att_read, 1)
                dve.wait_ge(att_read, t + 2)
                dve.tensor_tensor(row(X, t), row(X, t), att[:], ALU.add).then_inc(x1_ready, 1)

            parts(0, 0)
            parts(1, 1)
            dve.wait_ge(v_all_ready, 4)
            values(0, 0)
            values(1, 1)
            unturn(0, 0)
            maxima(0)
            unturn_max(0, 0)
            with dve.Fori(0, NT // 2 - 1) as i:
                link.enter(i, 16)
                for t, par in ((2 * i, 0), (2 * i + 1, 1)):
                    unturn(t + 1, 1 - par)
                    parts(t + 2, par)
                    maxima(t + 1)
                    unturn_max(t + 1, 1 - par)
                    add_att(t)
                    values(t + 2, par)
                link.leave(NT // 2 - 1, 16)
            unturn(NT - 1, 1)
            maxima(NT - 1)
            unturn_max(NT - 1, 1)
            add_att(NT - 2)
            add_att(NT - 1)


            dve.memset(magic[:], MAGIC).then_inc(magic_set, 1)
            dve.sem_inc(raw_used, 2)
            dve.sem_inc(w_rec_ready, 1)
            dve.sem_inc(tern_done, 3)

            def weights(e, par):
                dve.wait_ge(w_total, e + 3)
                link(dve.tensor_scalar(w_sum2[:], bank[7][:, 0:3], 1.0 / (FF * H), EPS, ALU.mult, ALU.max))
                dve.tensor_copy(w_mean[:, bass.ds(e, 1), :].rearrange("p a m -> p (a m)"), w_sum2[:])
                dve.reciprocal(w_rec[par][:], w_sum2[:]).then_inc(w_rec_ready, 1)
                for m in range(3):
                    dve.wait_ge(w_scaled, 3 * e + m + 1)
                    dve.wait_ge(tern_turned, 3 * e + m + 1)
                    ins = dve.tensor_scalar(tern[par][:, m, :], raw[par][:, m, :], MAGIC, 1.0, ALU.subtract, ALU.min)
                    ins.then_inc(tern_ready, 1)
                dve.wait_ge(tern_ready, 3 * e + 3)
                dve.sem_inc(raw_used, 1)
                for m in range(3):
                    dve.wait_ge(tern_turned, 3 * e + m + 7)
                    if m < 2:
                        dst = WGU[:, bass.ds(e, 1), :, m, :].rearrange("p a k i -> p (a k) i")
                        src = bank[m].bitcast(BF16)[:].rearrange("p (k i) -> p k i", k=2)
                    else:
                        dst = WD[:, bass.ds(e, 1)].rearrange("p a k o -> p (a k o)")
                        src = bank[m].bitcast(BF16)[:]
                    dve.tensor_scalar(dst, src, -1.0, None, ALU.max).then_inc(tern_done, 1)

            with dve.Fori(0, NE // 2) as i:
                link.enter(i, 2)
                weights(2 * i, 0)
                weights(2 * i + 1, 1)
                link.leave(NE // 2, 2)

            def normalise(n):
                for t in range(NT):
                    link(dve.bn_stats(stats[:, t, :], X[:, t, :]))
                    link(dve.bn_aggr(mv[:, t, :], stats[:, t, :]))
                link(dve.tensor_scalar(var[:], mv[:, :, 1], EPS, None, ALU.add))
                dve.tensor_scalar(half_bits[:], var[:].bitcast(I32), 1, None, ALU.arith_shift_right).then_inc(stats_ready, 1)
                dve.wait_ge(rstd_ready, n)
                for t in range(NT):
                    ins = dve.tensor_scalar(XN[:, t, :], X[:, t, :], mv[:, t, 0:1], rstd[:, t:t + 1], ALU.subtract, ALU.mult)
                ins.then_inc(XN_ready, 1)

            normalise(2)
            dve.wait_ge(XN_ready, 1)
            link(dve.tensor_reduce(row_max[:, 0, :], XN[:], AX.X, ALU.max, apply_absolute_value=True))
            link(dve.tensor_scalar(row_max[:, 0, :], row_max[:, 0, :], EPS, 1.0 / QMAX, ALU.max, ALU.mult))
            dve.reciprocal(row_max[:, 1, :], row_max[:, 0, :]).then_inc(xs_ready, 1)
            link(dve.tensor_tensor(row_max[:, 2, :], row_max[:, 0, :], row_max[:, 0, :], ALU.mult))
            link(dve.tensor_tensor(xrow[:, :, H:H + 2].bitcast(F32).rearrange("p t a -> p (t a)"),
                                   row_max[:, 2, :], row_max[:, 0, :], ALU.mult))
            dve.wait_ge(xq_ready, NT)
            dve.tensor_scalar(xrow[:, :, 0:H], xq32[:], MAGIC, None, ALU.subtract).then_inc(xrow_ready, 1)

            dve.wait_ge(logits_ready, 1)
            link(dve.tensor_copy(RB.logits[:].rearrange("p t e -> p (t e)"), bank[3][:, 64:64 + NT * NE]))
            best(dve, link, RB)
            dve.tensor_tensor(gate[:, 0, :], RB.top[:, :, 1], RB.top[:, :, 0], ALU.subtract).then_inc(gap_ready, 1)
            mark(dve, link, RB)
            dve.tensor_tensor(RB.hot_b[:], RB.hot[:, 0], RB.hot[:, 1], ALU.add).then_inc(hot_ready, 1)
            dve.wait_ge(gate_exp, 1)
            link(dve.tensor_scalar(gate[:, 0, :], gate[:, 1, :], 1.0, None, ALU.add))
            link(dve.reciprocal(gate[:, 0, :], gate[:, 0, :]))
            link(dve.tensor_tensor(gate[:, 1, :], gate[:, 1, :], gate[:, 0, :], ALU.mult))
            dve.wait_ge(counted, 1)
            link(dve.tensor_copy(RB.rank[:].rearrange("p t e -> p (t e)"), bank[4][:, 0:NT * NE]))
            dve.tensor_copy(RB.tots[:].rearrange("p t e -> p (t e)"), bank[4][:, 64:64 + NT * NE]).then_inc(rank_read, 1)
            dve.wait_ge(rank_read, 1)
            positions(dve, link, RB, 1)
            link(dve.tensor_tensor(w_prod[:, 0, :], w_mean[:, :, 0], w_mean[:, :, 0], ALU.mult))
            link(dve.tensor_tensor(w_prod[:, 0, :], w_prod[:, 0, :], w_mean[:, :, 1], ALU.mult))
            link(dve.tensor_scalar(w_prod[:, 1, :], w_mean[:, :, 2], 1.0 / QMAX, None, ALU.mult))
            link(dve.tensor_tensor(RB.below[:], RB.block_e[:, :, None].to_broadcast([P, NBLK, NE]),
                                   cst[:, None, C_IOTA:C_IOTA + NE].to_broadcast([P, NBLK, NE]), ALU.is_equal))
            for k in range(2):
                link(dve.tensor_tensor(below2[:], RB.below[:], w_prod[:, k:k + 1, :].to_broadcast([P, NBLK, NE]), ALU.mult))
                link(dve.tensor_reduce(block_w[:, k, :], below2[:], AX.X, ALU.add))

            dve.sem_inc(hid_done, 2)

            def hidden(j, q, r):
                par = r % 2
                h = hs[par]
                dve.wait_ge(gathered[r], 16 * q + 16)
                link(dve.tensor_tensor(h[:, 0:1], xg[r][:, H:H + 2].bitcast(F32), block_w[:, 0, bass.ds(j, 1)], ALU.mult))
                dve.sem_inc(xg_read, 1)
                dve.wait_ge(relu_ready, j + 1)
                link(dve.scalar_tensor_tensor(hid[par][:], bank[1 + par][:], 0.0, relu[par][:], ALU.max, ALU.mult))
                dve.tensor_tensor(hid[par][:], hid[par][:], bank[3 + par][:], ALU.mult).then_inc(hid_done, 1)
                dve.wait_ge(hid_done, j + 3)
                link(dve.tensor_reduce(h[:, 1:2], hid[par][:], AX.X, ALU.max, apply_absolute_value=True))
                link(dve.tensor_scalar(h[:, 2:3], h[:, 1:2], h[:, 0:1], EPS, ALU.mult, ALU.max))
                link(dve.reciprocal(h[:, 3:4], h[:, 2:3]))
                link(dve.tensor_scalar(h[:, 4:5], h[:, 3:4], h[:, 0:1], QMAX, ALU.mult, ALU.mult))
                link(dve.tensor_scalar(hid[par][:], hid[par][:], h[:, 4:5], MAGIC, ALU.mult, ALU.add))
                if not (isinstance(j, int) and j < 2):
                    dve.wait_ge(y_copied, j)
                dve.tensor_scalar(h[:, 5:6], h[:, 2:3], block_w[:, 1, bass.ds(j, 1)], None, ALU.mult)
                dve.tensor_scalar(hid_q[par][:], hid[par][:], MAGIC, None, ALU.subtract).then_inc(hq_ready, 1)

            for j in range(4):
                hidden(j, 0, j)
            with dve.Fori(1, NBLK // 4) as i:
                link.enter(i - 1, 28)
                for r in range(4):
                    hidden(4 * i + r, i, r)
                link.leave(NBLK // 4 - 1, 28)

            dve.wait_ge(y_back, 16 * 2 * NT)
            for t in range(NT):
                ins = dve.scalar_tensor_tensor(X[:, t, :], yg[:, t, 0, :], gate[:, 0, t:t + 1], X[:, t, :], ALU.mult, ALU.add)
            link(ins)
            for t in range(NT):
                dve.scalar_tensor_tensor(X[:, t, :], yg[:, t, 1, :], gate[:, 1, t:t + 1], X[:, t, :],
                                         ALU.mult, ALU.add).then_inc(x2_ready, 1)

            dve.wait_ge(x2_ready, NT)
            normalise(3)
            dve.sem_inc(roped_ready, 2)
            dve.sem_inc(s_less, 4)

            def fold(u, par):
                dve.wait_ge(qr_turned, u + 1)
                T = bank[1][0:S, 0:3 * P].rearrange("p (h a q) -> p h a q", h=2, a=2)
                dve.tensor_copy(qrwT[:, 0, :, :].rearrange("p h q -> p (h q)"), bank[1][0:S, 0:3 * P])
                for a in range(2):
                    dve.tensor_copy(qrwT[:, 1, :, :].rearrange("p h (a q) -> p h a q", a=2)[:, :, a, :], T[:, :, 1 - a, :])
                dve.tensor_copy(krT[:], bank[1][0:S, 3 * P:4 * P]).then_inc(qrwT_done, 1)
                dve.wait_ge(M_ready, u + 1)
                dve.tensor_tensor(MW[par][:], bank[3][:].rearrange("p (r n) -> p r n", r=2),
                                  mask_m[:, None, :].to_broadcast([P, 2, 2 * P]), ALU.mult).then_inc(M_done, 1)

            def rope(u, n):
                c, g = UNITS[n]
                dve.wait_ge(q_ready, NUNIT * u + n + 1)
                dve.wait_ge(keyed, 2 * u + 2)
                src = bank[g][:].rearrange("p (b s) -> p b s", s=S)
                for r in range(2):
                    at = C_QCOS + (2 * c + r) * S
                    ins = dve.tensor_tensor(roped[n][:, r, :].rearrange("p (b s) -> p b s", s=S), src,
                                            cst[:, None, at:at + S].to_broadcast([P, 8, S]), ALU.mult)
                ins.then_inc(roped_ready, 1)

            def less_max(u, h):
                dve.wait_ge(s_ready, u + 2)
                dve.wait_ge(prob_turned, 2 * u + 0) if not isinstance(u, int) or u else None
                src = bank[4 + h][:].rearrange("p (t l) -> p t l", l=S)
                link(dve.tensor_reduce(s_stat[:, h, 0, :], src, AX.X, ALU.max))
                dve.tensor_tensor(prob[:, :, h, :], src, s_stat[:, h, 0, :, None].to_broadcast([P, NT, S]), ALU.subtract).then_inc(s_less, 1)

            def by_sum(u, h):
                dve.wait_ge(s_exp, 2 * u + h + 1)
                link(dve.tensor_reduce(s_stat[:, h, 1, :], prob[:, :, h, :], AX.X, ALU.add))
                link(dve.reciprocal(s_stat[:, h, 2, :], s_stat[:, h, 1, :]))
                dve.tensor_tensor(prob[:, :, h, :], prob[:, :, h, :], s_stat[:, h, 2, :, None].to_broadcast([P, NT, S]), ALU.mult).then_inc(prob_ready, 1)

            fold(0, 0)
            for n in range(NUNIT):
                rope(0, n)
            fold(1, 1)

            def pair(u):
                less_max(u - 1, 0)
                rope(u, 0)
                less_max(u - 1, 1)
                rope(u, 1)
                by_sum(u - 1, 0)
                rope(u, 2)
                by_sum(u - 1, 1)
                for n in range(3, NUNIT):
                    rope(u, n)

            with dve.Fori(0, NU // 2 - 1) as i:
                link.enter(i, 12)
                for u, par in ((2 * i + 1, 1), (2 * i + 2, 0)):
                    pair(u)
                    fold(u + 1, 1 - par)
                link.leave(NU // 2 - 1, 12)
            pair(NU - 1)
            for h in range(2):
                less_max(NU - 1, h)
            for h in range(2):
                by_sum(NU - 1, h)
            dve.wait_ge(d_loaded, 48)
            link(dve.tensor_scalar(w_raw[:], w_raw[:], 2.0, MAGIC, ALU.mult, ALU.add))
            link(dve.tensor_scalar(w_raw[:], w_raw[:], MAGIC, 1.0, ALU.subtract, ALU.min))
            link(dve.tensor_scalar(w_raw[:], w_raw[:], -1.0, None, ALU.max))
            dve.tensor_tensor(w_raw[:], w_raw[:], o_scale[:, :, None].to_broadcast([P, 2, H]), ALU.mult).then_inc(w_scaled_d, 1)
            for h in range(NT // 2):
                dve.wait_ge(o_ready, h + 1)
                for t in range(2):
                    dve.tensor_tensor(X[:, 2 * h + t, :], X[:, 2 * h + t, :], bank[h][:, t * H:(t + 1) * H], ALU.add).then_inc(x3_ready, 1)
            dve.wait_ge(x3_ready, NT)
            normalise(4)
            dve.wait_ge(w_turned_d, 1)
            link(dve.tensor_copy(wT[:].rearrange("p k o -> p (k o)"), bank[6][:]))
            dve.wait_ge(logits_ready, 2)
            link(dve.tensor_copy(RD.logits[:].rearrange("p t e -> p (t e)"), bank[4][:, 0:NT * NE_D]))
            best(dve, link, RD)
            dve.tensor_tensor(l_exp[:], RD.logits[:], RD.top[:, :, 0:1].to_broadcast([P, NT, NE_D]), ALU.subtract).then_inc(less_ready, 1)
            mark(dve, link, RD)
            dve.tensor_copy(RD.hot_b[:], RD.hot[:, 0]).then_inc(hot_ready, 1)
            dve.wait_ge(l_exp_ready, 1)
            link(dve.tensor_reduce(top_w[:, 0, :], l_exp[:], AX.X, ALU.add))
            link(dve.reciprocal(top_w[:, 1, :], top_w[:, 0, :]))
            dve.wait_ge(counted, 2)
            link(dve.tensor_copy(RD.rank[:].rearrange("p t e -> p (t e)"), bank[5][:, 0:NT * NE_D]))
            dve.tensor_copy(RD.tots[:].rearrange("p t e -> p (t e)"), bank[5][:, NT * NE_D:]).then_inc(rank_read, 1)
            dve.wait_ge(rank_read, 2)
            positions(dve, link, RD, 2)
            dve.sem_inc(WE_ready, 4)
            with dve.Fori(0, NE_D // 4) as i:
                for r in range(4):
                    dve.wait_ge(m_turned, 4 * i + r + 5)
                    dve.tensor_tensor(WE[:, bass.ds(4 * i + r, 1)].rearrange("p a k o -> p (a k o)"), bank[r][:],
                                      wT[:].rearrange("p k o -> p (k o)"), ALU.mult).then_inc(WE_ready, 1)
            dve.sem_inc(z_copied, 2)
            with dve.Fori(0, NBLK_D // 2) as i:
                for par in range(2):
                    j = 2 * i + par
                    dve.wait_ge(z_ready, j + 3)
                    dve.wait_ge(z_stored[par], 16 * i + 16)
                    dve.tensor_copy(z[par][:], bank[6 + par][:, 0:H]).then_inc(z_copied, 1)
            dve.wait_ge(z_back, 16 * NT)
            for t in range(NT):
                dve.scalar_tensor_tensor(X[:, t, :], zg[:, t, :], top_w[:, 1, t:t + 1], X[:, t, :],
                                         ALU.mult, ALU.add).then_inc(x4_ready, 1)


def constants():
    c = np.zeros((P, C_W), np.float32)
    p = np.arange(P)
    for g in range(2):
        c[:, g] = (p // HD) % 2 == g
        c[:, 2 + g] = p // S == g
    c[:, C_IOTA:C_IOTA + 48] = np.arange(48)
    c[:, C_TOKEN:C_TOKEN + NT] = p[:, None] + P * np.arange(NT)
    pos = np.arange(S, dtype=np.float32)

    def angles(dim):
        inv = np.float32(1.0) / np.float32(10000.0) ** (np.arange(0, dim, 2, dtype=np.float32) / np.float32(dim))
        a = np.repeat(pos[:, None] * inv[None, :], 2, axis=-1).astype(np.float32)
        return np.cos(a), np.sin(a)

    cos, sin = angles(S)
    sin = np.concatenate([-sin[:, :S // 2], sin[:, S // 2:]], axis=1)
    c[:, C_KCOS:C_KCOS + S] = cos[p % S]
    c[:, C_KSIN:C_KSIN + S] = sin[p % S]
    cos, sin = angles(QD)
    sin = np.concatenate([sin[:, QD // 2:], -sin[:, :QD // 2]], axis=1)
    for ch in range(3):
        f = (ch * P + p) % QD
        for r, table in enumerate((cos, sin)):
            at = C_QCOS + (2 * ch + r) * S
            c[:, at:at + S] = table[:, f].T
    return c


LAYOUTS = {
    "x": (NT * P, H), "ctx_512": (NT * P, S), "constants": (P, C_W),
    "L0_ffn_router_w": (NE, H), "L0_ffn_gate_w": (NE, FF, H), "L0_ffn_up_w": (NE, FF, H), "L0_ffn_down_w": (NE, H, FF),
    "L1_xattn_Wq": (NH * KD, H), "L1_xattn_w_kc_q": (NH, KD, QD), "L1_xattn_w_kc_kv": (NH, KD, S),
    "L1_xattn_W_qr": (NH * QD, S), "L1_xattn_W_kr": (NH * S, S), "L1_xattn_Wo": (H, NH * KD),
    "L1_ffn_weight": (H, H), "L1_ffn_scale": (P, 2), "L1_ffn_expert_masks": (NE_D, H, H), "L1_ffn_router_w": (NE_D, H),
}


def kernel(**inputs):
    import concourse.bacc as bacc
    from concourse.bass_utils import run_bass_kernel_spmd

    inputs = dict(inputs, constants=constants())
    inputs["L1_ffn_scale"] = np.asarray(inputs["L1_ffn_scale"]).reshape(2, P).T
    nc = bacc.Bacc("TRN2", target_bir_lowering=False, num_devices=1)
    arrays, args = {}, []
    for name, shape in LAYOUTS.items():
        a = np.ascontiguousarray(np.asarray(inputs[name]).reshape(shape))
        arrays[f"in_{name}_dram"] = a
        args.append(nc.dram_tensor(f"in_{name}_dram", a.shape, mybir.dt.from_np(a.dtype), kind="ExternalInput").ap())
    args.append(nc.dram_tensor("out_0_dram", (NT * P, H), F32, kind="ExternalOutput").ap())
    build(nc, *args)
    result = run_bass_kernel_spmd(nc, [arrays], core_ids=[0])
    return result.results[0]["out_0_dram"].reshape(2 * NT, S, H)
```

```python
from contextlib import ExitStack

import numpy as np

import concourse.bass as bass
from concourse import mybir

F32, BF16, I32, U32 = mybir.dt.float32, mybir.dt.bfloat16, mybir.dt.int32, mybir.dt.uint32
ALU, ACT, AX = mybir.AluOpType, mybir.ActivationFunctionType, mybir.AxisListType
P = 128
NT = 8
H = 256
S = 64
NPAIR = 16
NKV = 8
HD = 8
NTERM = 6
KROWS = NTERM * 2 * HD
EPS = 1e-5
MAGIC = 1.5 * 2.0 ** 23
NE = 8
FF = 512
NBLK = 24
XROW = 258
QMAX = 127.0
NE_D = 32
NBLK_D = 40

NH = 16
NU = NH // 2
KD = 128
QD = 192
NUNIT = 6
UNITS = [(0, 0), (0, 1), (2, 0), (2, 1), (1, 0), (1, 1)]
SBUF_BASE, SBUF_END = 16512, 229344

C_HEAD, C_HALF, C_IOTA, C_TOKEN, C_KCOS, C_KSIN, C_QCOS = 0, 2, 4, 52, 64, 128, 192
C_W = C_QCOS + 3 * 2 * S
Q_SCALE = float(np.float32(1.0) / np.sqrt(np.float32(HD)))


class Chain:

    def __init__(self, eng, sem):
        self.eng, self.sem, self.base, self.n = eng, sem, 0, 0

    def __call__(self, ins):
        self.n += 1
        ins.then_inc(self.sem, 1)
        self.eng.wait_ge(self.sem, self.base + self.n)

    def enter(self, i, per):
        self.start = self.base + self.n
        self.base, self.n = self.start + i * per, 0

    def leave(self, trips, per):
        assert self.n == per, (self.n, per)
        self.base, self.n = self.start + trips * per, 0


class Routing:

    def __init__(self, sb, s, n_e, n_blk, choices):
        n = choices * NT
        self.n_e, self.n_blk, self.choices = n_e, n_blk, choices
        self.logits = sb(f"logits{s}", [P, NT, n_e])
        self.top = sb(f"top{s}", [P, NT, 8])
        self.top_i = sb(f"top_i{s}", [P, NT, 8], U32)
        self.top_f = sb(f"top_f{s}", [P, NT, choices])
        self.hot = sb(f"hot{s}", [P, choices, NT, n_e])
        self.hot_b = sb(f"hot_b{s}", [P, NT, n_e], BF16)
        self.rank = sb(f"rank{s}", [P, NT, n_e])
        self.tots = sb(f"tots{s}", [P, NT, n_e])
        self.counts = sb(f"counts{s}", [P, 4, n_e])
        self.counts_i = sb(f"counts_i{s}", [P, n_e], I32)
        self.picked = sb(f"picked{s}", [P, 2, NT, n_e])
        self.spot = sb(f"spot{s}", [P, 6, n])
        self.spot_i = sb(f"spot_i{s}", [P, n], I32)
        self.y_index = sb(f"y_index{s}", [P, n], U32)
        self.inv_index = sb(f"inv_index{s}", [P, n], U32)
        self.owner = sb(f"owner{s}", [P, n_blk], U32)
        self.below = sb(f"below{s}", [P, n_blk, n_e])
        self.block_e = sb(f"block_e{s}", [P, n_blk])
        self.block_ei = sb(f"block_ei{s}", [P, n_blk], U32)


def build(nc, x, ctx_in, cst_in, router_w, gate_w, up_w, down_w, wq, w_kc_q, w_kc_kv, w_qr, w_kr, wo,
          weight, scale, masks, router_d, out):
    with ExitStack() as ctx:
        place = [SBUF_BASE]

        def sb(name, shape, dt=F32):
            n = int(np.prod(shape[1:])) * (2 if dt == BF16 else 4)
            at = place[0]
            place[0] = (at + n + 31) // 32 * 32
            return nc.alloc_sbuf_tensor_at(name, shape, dt, offset=at)

        def sem(name):
            return ctx.enter_context(nc.semaphore(name))

        bank = [ctx.enter_context(nc.psum_tensor(f"bank{i}", [P, 512], F32)) for i in range(8)]
        X = sb("X", [P, NT, H])
        ctxn = sb("ctxn", [P, NT, S])
        ctx2 = sb("ctx2", [P, 2 * NT, S])
        cst = sb("cst", [P, C_W])
        ident = sb("ident", [P, P], BF16)
        token = sb("token", [P, NT], U32)
        zeros = sb("zeros", [P, NBLK + NBLK_D])

        stats = sb("stats", [P, NT, 6])
        mv = sb("mv", [P, NT, 2])
        var = sb("var", [P, NT])
        half_bits = sb("half_bits", [P, NT], I32)
        rstd = sb("rstd", [P, NT])
        root_tmp = sb("root_tmp", [P, 2, NT])
        identf = sb("identf", [P, P])
        ones = sb("ones", [P, P])
        ones_b = sb("ones_b", [P, P], BF16)
        before = sb("before", [P, P], BF16)
        row_max = sb("row_max", [P, 4, NT])
        mask_m = sb("mask_m", [P, 2 * P])
        kvr = sb("kvr", [P, NT, 2, S])
        kvr2 = sb("kvr2", [P, 2 * NT, S])
        rot = sb("rot", [P, 2 * NT, S])
        kvrT = sb("kvrT", [P, NT * P])
        b_place = place[0]
        raw = [sb(f"raw{i}", [P, 3, 4 * H]) for i in range(2)]
        w_junk = sb("w_junk", [P, 3, 4 * H], BF16)
        w_sum = [sb(f"w_sum{i}", [P, 3]) for i in range(2)]
        w_sum2 = sb("w_sum2", [P, 3])
        magic = sb("magic", [P, 1])
        w_rec = [sb(f"w_rec{i}", [P, 3]) for i in range(2)]
        w_mean = sb("w_mean", [P, NE, 3])
        tern = [sb(f"tern{i}", [P, 3, 4 * H], BF16) for i in range(2)]
        WGU = sb("WGU", [P, NE, 2, 2, FF], BF16)
        WD = sb("WD", [P, NE, 4, H], BF16)
        r_raw = sb("r_raw", [NE, H])
        rT = sb("rT", [P, 2, NE])
        RB = Routing(sb, "_b", NE, NBLK, 2)
        gate = sb("gate", [P, 2, NT])
        below2 = sb("below2", [P, NBLK, NE])
        block_w = sb("block_w", [P, 2, NBLK])
        w_prod = sb("w_prod", [P, 2, NE])
        hs = [sb(f"hs{i}", [P, 6]) for i in range(4)]
        a_place = place[0]
        qn = sb("qn", [P, H])
        q_parts = [sb(f"q_parts{i}", [P, NPAIR, NTERM, 2 * HD], BF16) for i in range(2)]
        k_parts = [sb(f"k_parts{i}", [P, NKV, NTERM, 2, HD], BF16) for i in range(2)]
        q_rest = sb("q_rest", [P, H])
        k_rest = sb("k_rest", [P, NT, S])
        k_split = sb("k_split", [P, NT, 3, S], BF16)
        k_all = sb("k_all", [P, NT, NKV, NTERM, 2, HD], BF16)
        v_all = sb("v_all", [P, 2 * NT, NKV, 2, HD + 1])
        qT = [sb(f"qT{i}", [KROWS, NPAIR * P], BF16) for i in range(2)]
        kT = [sb(f"kT{i}", [KROWS, NKV, 2, 2, S], BF16) for i in range(2)]
        negsel = sb("negsel", [96, NPAIR, 2, S], BF16)
        v_blk = [sb(f"v_blk{i}", [P, 2, NKV, 2, HD + 1]) for i in range(2)]
        mx = sb("mx", [P, 32])
        mx_rest = sb("mx_rest", [P, 2, 32])
        mx_parts = sb("mx_parts", [P, 3, 32], BF16)
        mxT = [sb(f"mxT{i}", [96, P], BF16) for i in range(2)]
        pT = [sb(f"pT{i}", [P, 512]) for i in range(4)]
        den_rec = sb("den_rec", [P, 32])
        att = sb("att", [P, H])
        place[0] = a_place
        xq32 = sb("xq32", [P, NT, H])
        xrow = sb("xrow", [P, NT, XROW], BF16)
        xg = [sb(f"xg{i}", [P, XROW], BF16) for i in range(4)]
        xgT = [sb(f"xgT{i}", [P, H], BF16) for i in range(2)]
        relu = [sb(f"relu{i}", [P, FF]) for i in range(2)]
        hid = [sb(f"hid{i}", [P, FF]) for i in range(4)]
        hid_q = [sb(f"hid_q{i}", [P, FF], BF16) for i in range(2)]
        hidT = [sb(f"hidT{i}", [P, FF], BF16) for i in range(2)]
        y = [sb(f"y{i}", [P, H]) for i in range(2)]
        yg = sb("yg", [P, NT, 2, H])
        assert place[0] <= SBUF_END - 2 * 4 * NT * H
        place[0] = SBUF_END - 2 * 4 * NT * H
        XN = sb("XN", [P, NT, H])
        XNT = sb("XNT", [P, 2, NT * P])
        place[0] = b_place
        f_wq = [sb(f"f_wq{i}", [P, 2, H]) for i in range(2)]
        f_kcq = [sb(f"f_kcq{i}", [P, 2, QD]) for i in range(2)]
        f_wo = [sb(f"f_wo{i}", [P, 2, 2 * KD]) for i in range(2)]
        f_kv = [sb(f"f_kv{i}", [P, 2, S]) for i in range(2)]
        f_qr = [sb(f"f_qr{i}", [P, 3, S]) for i in range(2)]
        f_kr = [sb(f"f_kr{i}", [P, S]) for i in range(2)]
        woT = sb("woT", [P, 2, H])
        qrwT = sb("qrwT", [S, 2, 2, QD])
        krT = sb("krT", [S, P])
        AW = [sb(f"AW{i}", [P, 2, 2 * QD]) for i in range(2)]
        MW = [sb(f"MW{i}", [P, 2, 2 * P]) for i in range(2)]
        VW = sb("VW", [P, NU, H])
        roped = [sb(f"roped{i}", [P, 2, 512]) for i in range(NUNIT)]
        qrT = sb("qrT", [P, NT * P])
        prob = sb("prob", [P, NT, 2, S])
        probT = sb("probT", [P, NT * P])
        s_stat = sb("s_stat", [P, 2, 3, NT])
        ctxT = sb("ctxT", [P, NU, NT * P])
        c_end = place[0]
        m_raw = [sb(f"m_raw{i}", [P, 4, 2, H]) for i in range(4)]
        w_raw = sb("w_raw", [P, 2, H])
        o_scale = sb("o_scale", [P, 2])
        rd_raw = sb("rd_raw", [NE_D, H])
        assert place[0] <= SBUF_END - 2 * 4 * NT * H
        place[0] = b_place
        WE = sb("WE", [P, NE_D, 2, H])
        wT = sb("wT", [P, 2, H])
        rdT = sb("rdT", [P, 2, NE_D])
        RD = Routing(sb, "_d", NE_D, NBLK_D, 1)
        l_exp = sb("l_exp", [P, NT, NE_D])
        top_w = sb("top_w", [P, 2, NT])
        dg = [sb(f"dg{i}", [P, H]) for i in range(4)]
        dgT = [sb(f"dgT{i}", [P, H]) for i in range(2)]
        z = [sb(f"z{i}", [P, H]) for i in range(2)]
        zg = sb("zg", [P, NT, H])
        assert place[0] <= c_end
        n_rows = nc.dram_tensor("n_rows", (NT * P, H), F32).ap()
        owners_d = nc.dram_tensor("owners_d", (P * NBLK_D, 1), U32).ap()
        z_rows = nc.dram_tensor("z_rows", (NBLK_D * P, H), F32).ap()
        x_rows = nc.dram_tensor("x_rows", (NT * P, XROW // 2), U32).ap()
        owners = nc.dram_tensor("owners", (P * NBLK, 1), U32).ap()
        y_rows = nc.dram_tensor("y_rows", (NBLK * P, H), F32).ap()

        x_loaded, ctx_loaded, out_stored = sem("x_loaded"), sem("ctx_loaded"), sem("out_stored")
        consts_built = sem("consts_built")
        stats_ready, rstd_ready = sem("stats_ready"), sem("rstd_ready")
        bconsts_built, negsel_built, v_all_ready = sem("bconsts_built"), sem("negsel_built"), sem("v_all_ready")
        parts_ready, v_ready = sem("parts_ready"), sem("v_ready")
        turned, k_unturned, q_unturned = sem("turned"), sem("k_unturned"), sem("q_unturned")
        nat_ready, nat_read = sem("nat_ready"), sem("nat_read")
        mx_ready, mx_turned, mxT_ready = sem("mx_ready"), sem("mx_turned"), sem("mxT_ready")
        scores_ready, probs_ready, probs_used = sem("scores_ready"), sem("probs_ready"), sem("probs_used")
        att_read, x1_ready = sem("att_read"), sem("x1_ready")
        dve_chain, pool_chain = sem("dve_chain"), sem("pool_chain")

        raw_loaded = [sem(f"raw_loaded{i}") for i in range(2)]
        raw_used, w_summed, w_total, w_rec_ready, w_scaled = (sem(n) for n in ("raw_used", "w_summed", "w_total", "w_rec_ready", "w_scaled"))
        tern_ready, tern_turned, tern_done = sem("tern_ready"), sem("tern_turned"), sem("tern_done")
        magic_set = sem("magic_set")
        r_loaded, r_turned, r_ready = sem("r_loaded"), sem("r_turned"), sem("r_ready")
        XN_ready, XN_turned, XNT_ready, logits_ready = sem("XN_ready"), sem("XN_turned"), sem("XNT_ready"), sem("logits_ready")
        xs_ready, xq_ready, xrow_ready, xrow_stored = sem("xs_ready"), sem("xq_ready"), sem("xrow_ready"), sem("xrow_stored")
        gap_ready, gate_exp, hot_ready, counted = sem("gap_ready"), sem("gate_exp"), sem("hot_ready"), sem("counted")
        spots_ready, owner_zeroed, owner_stored, owner_loaded = sem("spots_ready"), sem("owner_zeroed"), sem("owner_stored"), sem("owner_loaded")
        block_e_ready, rank_read = sem("block_e_ready"), sem("rank_read")
        gathered = [sem(f"gathered{i}") for i in range(4)]
        xg_turned, xgT_ready, block_w_ready, gu_ready, hid_scaled = (sem(n) for n in ("xg_turned", "xgT_ready", "block_w_ready", "gu_ready", "hid_scaled"))
        h_scale_ready, relu_ready = sem("h_scale_ready"), sem("relu_ready")
        hid_done, hq_ready, h_turned, hT_ready, y_ready, y_copied = (sem(n) for n in ("hid_done", "hq_ready", "h_turned", "hT_ready", "y_ready", "y_copied"))
        y_stored = [sem(f"y_stored{i}") for i in range(2)]
        y_back, x2_ready = sem("y_back"), sem("x2_ready")
        kv_rotated, kv_turned, kvrT_ready, mask_built = sem("kv_rotated"), sem("kv_turned"), sem("kvrT_ready"), sem("mask_built")
        f_loaded = [sem(f"f_loaded{i}") for i in range(2)]
        A_ready, A_done, wo_turned, woT_done = (sem(n) for n in ("A_ready", "A_done", "wo_turned", "woT_done"))
        qr_turned, qrwT_done, V_ready, V_done, M_ready, M_done = (sem(n) for n in ("qr_turned", "qrwT_done", "V_ready", "V_done", "M_ready", "M_done"))
        q_ready, roped_ready, keyed, qrT_ready = (sem(n) for n in ("q_ready", "roped_ready", "keyed", "qrT_ready"))
        s_ready, s_less, s_exp, prob_ready = (sem(n) for n in ("s_ready", "s_less", "s_exp", "prob_ready"))
        prob_turned, probT_ready, c_ready, ctxT_ready = (sem(n) for n in ("prob_turned", "probT_ready", "c_ready", "ctxT_ready"))
        o_ready, x3_ready, pe_waited = sem("o_ready"), sem("x3_ready"), sem("pe_waited")
        m_loaded = [sem(f"m_loaded{i}") for i in range(4)]
        d_loaded, w_scaled_d, w_turned_d, wT_ready, rdT_ready = (sem(n) for n in ("d_loaded", "w_scaled_d", "w_turned_d", "wT_ready", "rdT_ready"))
        m_turned, WE_ready, n_stored, less_ready, l_exp_ready = (sem(n) for n in ("m_turned", "WE_ready", "n_stored", "less_ready", "l_exp_ready"))
        d_gathered = [sem(f"d_gathered{i}") for i in range(4)]
        dg_turned, dgT_ready, z_ready, z_copied, z_back, x4_ready = (sem(n) for n in ("dg_turned", "dgT_ready", "z_ready", "z_copied", "z_back", "x4_ready"))
        z_stored = [sem(f"z_stored{i}") for i in range(2)]

        block = ctx.enter_context(nc.Block())

        def row(a, t):
            return a[:, bass.ds(t, 1), :].rearrange("p a d -> p (a d)")

        def inverse_root(pool, link, c):
            y, v = rstd[:, c], var[:, c]
            a, b = root_tmp[:, 0, c], root_tmp[:, 1, c]
            link(pool.tensor_scalar(y.bitcast(I32), half_bits[:, c], -1.0, float(0x5F3759DF), ALU.mult, ALU.add))
            for _ in range(3):
                link(pool.tensor_tensor(a, y, y, ALU.mult))
                link(pool.tensor_tensor(b, a, v, ALU.mult))
                link(pool.tensor_scalar(a, b, -0.5, 1.5, ALU.mult, ALU.add))
                link(pool.tensor_tensor(y, y, a, ALU.mult))

        def positions(dve, link, R, nth):
            n_e, n_blk = R.n_e, R.n_blk
            for t in range(1, NT):
                link(dve.tensor_tensor(R.rank[:, t, :], R.rank[:, t, :], R.tots[:, t - 1, :], ALU.add))
                link(dve.tensor_tensor(R.tots[:, t, :], R.tots[:, t, :], R.tots[:, t - 1, :], ALU.add))
            nb, upto, start = (R.counts[:, i, :] for i in range(3))
            link(dve.tensor_scalar(R.counts_i[:], R.tots[:, NT - 1, :], float(P - 1), None, ALU.add))
            link(dve.tensor_scalar(R.counts_i[:], R.counts_i[:], 7, None, ALU.arith_shift_right))
            link(dve.tensor_copy(nb, R.counts_i[:]))
            link(dve.tensor_tensor_scan(upto, ones[:, 0:n_e], nb, 0.0, ALU.mult, ALU.add))
            link(dve.tensor_tensor(start, upto, nb, ALU.subtract))
            for k in range(R.choices):
                c = slice(k * NT, (k + 1) * NT)
                link(dve.tensor_tensor(R.picked[:, 0], R.hot[:, k], R.rank[:], ALU.mult))
                link(dve.tensor_reduce(R.spot[:, 0, c], R.picked[:, 0], AX.X, ALU.add))
                link(dve.tensor_tensor(R.picked[:, 1], R.hot[:, k], start[:, None, :].to_broadcast([P, NT, n_e]), ALU.mult))
                link(dve.tensor_reduce(R.spot[:, 1, c], R.picked[:, 1], AX.X, ALU.add))
            rank, first, hi, lo, blk = (R.spot[:, i, :] for i in range(5))
            link(dve.tensor_copy(R.spot_i[:], rank))
            link(dve.tensor_scalar(R.spot_i[:], R.spot_i[:], 7, None, ALU.arith_shift_right))
            link(dve.tensor_copy(hi, R.spot_i[:]))
            link(dve.scalar_tensor_tensor(lo, hi, -float(P), rank, ALU.mult, ALU.add))
            link(dve.tensor_tensor(blk, first, hi, ALU.add))
            link(dve.scalar_tensor_tensor(R.inv_index[:], lo, float(n_blk), blk, ALU.mult, ALU.add))
            dve.scalar_tensor_tensor(R.y_index[:], blk, float(P), lo, ALU.mult, ALU.add).then_inc(spots_ready, 1)
            link(dve.tensor_tensor(R.below[:], upto[:, None, :].to_broadcast([P, n_blk, n_e]),
                                   cst[:, C_IOTA:C_IOTA + n_blk, None].to_broadcast([P, n_blk, n_e]), ALU.is_le))
            link(dve.tensor_reduce(R.block_e[:], R.below[:], AX.X, ALU.add))
            link(dve.tensor_scalar(R.block_e[:], R.block_e[:], float(n_e - 1), None, ALU.min))
            dve.tensor_copy(R.block_ei[:], R.block_e[:]).then_inc(block_e_ready, 1)
            dve.wait_ge(block_e_ready, nth)

        def best(dve, link, R):
            for t in range(NT):
                link(dve.max(R.top[:, t, :], R.logits[:, t, :]))
                ins = dve.max_index(R.top_i[:, t, :], R.top[:, t, :], R.logits[:, t, :])
            link(ins)

        def mark(dve, link, R):
            link(dve.tensor_copy(R.top_f[:], R.top_i[:, :, 0:R.choices]))
            for k in range(R.choices):
                link(dve.tensor_tensor(R.hot[:, k], R.top_f[:, :, k:k + 1].to_broadcast([P, NT, R.n_e]),
                                       cst[:, None, C_IOTA:C_IOTA + R.n_e].to_broadcast([P, NT, R.n_e]), ALU.is_equal))

        @block.sync
        def _(sp):
            sp.dma_start(X[:], x.rearrange("(t p) d -> p t d", p=P)).then_inc(x_loaded, 16)
            sp.dma_start(ctxn[:], ctx_in.rearrange("(t p) d -> p t d", p=P)).then_inc(ctx_loaded, 16)
            for g in range(2):
                sp.dma_start(ctx2[64 * g:64 * g + 64], ctx_in.rearrange("(b s) d -> s b d", s=S)).then_inc(ctx_loaded, 16)
            sp.dma_start(cst[:], cst_in).then_inc(ctx_loaded, 16)
            sp.dma_start(r_raw[:], router_w).then_inc(r_loaded, 16)
            with sp.Fori(0, NE // 2) as i:
                for par in range(2):
                    sp.wait_ge(raw_used, 2 * i + par + 1)
                    for m, w in enumerate((gate_w, up_w, down_w)):
                        sp.dma_start(raw[par][:, m, :].rearrange("p (c h) -> p c h", h=w.shape[2]),
                                     w[bass.ds(2 * i + par, 1)].rearrange("a (c p) h -> p (a c) h", p=P)).then_inc(raw_loaded[par], 16)
            sp.wait_ge(xrow_ready, 1)
            sp.dma_start(x_rows.rearrange("(t p) d -> p t d", p=P), xrow[:].bitcast(U32)).then_inc(xrow_stored, 16)
            sp.wait_ge(owner_stored, 16 * 2 * NT)
            sp.dma_start(RB.owner[:], owners.rearrange("(p j) a -> p (j a)", p=P)).then_inc(owner_loaded, 16)
            for par in range(2):
                sp.sem_inc(y_stored[par], 16)
            with sp.Fori(0, NBLK // 2) as i:
                for par in range(2):
                    sp.wait_ge(y_copied, 2 * i + par + 2)
                    sp.dma_start(y_rows[bass.ds((2 * i + par) * P, P), :], y[par][:]).then_inc(y_stored[par], 16)
            sp.wait_ge(x2_ready, NT)
            for c, (dst, src) in enumerate(((w_raw, weight.rearrange("(c p) i -> p c i", p=P)), (o_scale, scale), (rd_raw, router_d))):
                sp.dma_start(dst[:], src).then_inc(d_loaded, 16)
            with sp.Fori(0, NU // 2) as i:
                for par in range(2):
                    u = 2 * i + par
                    sp.wait_ge(V_ready, u + 1)
                    for dst, src in ((f_wq, wq.rearrange("(h k) i -> k h i", k=KD)[:, bass.ds(2 * u, 2), :]),
                                     (f_kcq, w_kc_q.rearrange("h k q -> k h q")[:, bass.ds(2 * u, 2), :]),
                                     (f_wo, wo.rearrange("(c o) n -> o c n", o=P)[:, :, bass.ds(2 * KD * u, 2 * KD)]),
                                     (f_kv, w_kc_kv.rearrange("h k d -> k h d")[:, bass.ds(2 * u, 2), :]),
                                     (f_qr, w_qr.rearrange("(u c p) r -> u p c r", c=3, p=P)[bass.ds(u, 1)].rearrange("a p c r -> p (a c) r")),
                                     (f_kr, w_kr[bass.ds(P * u, P), :])):
                        sp.dma_start(dst[par][:], src).then_inc(f_loaded[par], 16)
            def load_masks(g):
                sp.dma_start(m_raw[g % 4][:], masks[4 * g:4 * g + 4].rearrange("e (c p) i -> p e c i", p=P)).then_inc(m_loaded[g % 4], 16)

            for g in range(4):
                load_masks(g)
            sp.wait_ge(XN_ready, 3)
            sp.dma_start(n_rows.rearrange("(t p) d -> p t d", p=P), XN[:]).then_inc(n_stored, 16)
            sp.wait_ge(owner_stored, 16 * 3 * NT)
            sp.dma_start(RD.owner[:], owners_d.rearrange("(p j) a -> p (j a)", p=P)).then_inc(owner_loaded, 16)
            for g in range(4, 8):
                sp.wait_ge(m_turned, 4 * (g - 3) + 4)
                load_masks(g)
            for par in range(2):
                sp.sem_inc(z_stored[par], 16)
            with sp.Fori(0, NBLK_D // 2) as i:
                for par in range(2):
                    sp.wait_ge(z_copied, 2 * i + par + 3)
                    sp.dma_start(z_rows[bass.ds((2 * i + par) * P, P), :], z[par][:]).then_inc(z_stored[par], 16)
            for t in range(NT):
                sp.wait_ge(x4_ready, t + 1)
                sp.dma_start(out[t * P:(t + 1) * P, :], X[:, t, :]).then_inc(out_stored, 16)
            sp.wait_ge(out_stored, 16 * NT)

        @block.gpsimd
        def _(pool):
            link = Chain(pool, pool_chain)
            link(pool.memset(ident[:], 0.0))
            pool.affine_select(out=ident[:], in_=ident[:], compare_op=ALU.not_equal, fill=1.0, base=0,
                               pattern=[[-1, P]], channel_multiplier=1).then_inc(consts_built, 1)
            pool.memset(ones[:], 1.0).then_inc(consts_built, 1)
            pool.wait_ge(stats_ready, 1)
            inverse_root(pool, link, slice(0, NT))
            pool.tensor_scalar(rstd[:], rstd[:], Q_SCALE, None, ALU.mult).then_inc(rstd_ready, 1)
            pool.wait_ge(ctx_loaded, 64)
            for g in range(2):
                pool.tensor_tensor(v_all[:, :, :, g, 0:HD], ctx2[:].rearrange("p b (k d) -> p b k d", d=HD),
                                   cst[:, 2 + g:3 + g, None, None].to_broadcast([P, 2 * NT, NKV, HD]), ALU.mult).then_inc(v_all_ready, 1)
                pool.tensor_copy(v_all[:, :, :, g, HD], cst[:, 2 + g:3 + g, None].to_broadcast([P, 2 * NT, NKV])).then_inc(v_all_ready, 1)
            link(pool.memset(negsel[:], 0.0))
            for s in range(3):
                link(pool.affine_select(out=negsel[32 * s:32 * s + 32], in_=negsel[32 * s:32 * s + 32],
                                        compare_op=ALU.not_equal, fill=-1.0, base=0,
                                        pattern=[[-2, NPAIR], [-1, 2], [0, S]], channel_multiplier=1))
            pool.nop().then_inc(negsel_built, 1)
            pool.memset(ones_b[:], 1.0).then_inc(bconsts_built, 1)
            link(pool.memset(identf[:], 0.0))
            pool.affine_select(out=identf[:], in_=identf[:], compare_op=ALU.not_equal, fill=1.0, base=0,
                               pattern=[[-1, P]], channel_multiplier=1).then_inc(bconsts_built, 1)
            link(pool.memset(before[:], 0.0))
            pool.affine_select(out=before[:], in_=before[:], compare_op=ALU.is_ge, fill=1.0, base=0,
                               pattern=[[-1, P]], channel_multiplier=1).then_inc(bconsts_built, 1)
            link(pool.memset(zeros[:], 0.0))
            pool.dma_start(owners.rearrange("(p j) a -> p (j a)", p=P), zeros[:, 0:NBLK].bitcast(U32)).then_inc(owner_zeroed, 16)
            pool.dma_start(owners_d.rearrange("(p j) a -> p (j a)", p=P), zeros[:, NBLK:NBLK + NBLK_D].bitcast(U32)).then_inc(owner_zeroed, 16)
            pool.tensor_copy(token[:], cst[:, C_TOKEN:C_TOKEN + NT]).then_inc(bconsts_built, 1)
            link(pool.memset(mask_m[:], 1.0))
            link(pool.memset(mask_m[0:64, P:P + 64], 0.0))
            link(pool.memset(mask_m[64:P, 64:P], 0.0))
            for dst, src in ((kvr2[:], ctx2[:]), (kvr[:, :, 0, :], ctxn[:])):
                n = src.shape[1]
                r = rot[:, 0:n, :]
                cos = cst[:, None, C_KCOS:C_KCOS + S].to_broadcast([P, n, S])
                sin = cst[:, None, C_KSIN:C_KSIN + S].to_broadcast([P, n, S])
                link(pool.tensor_tensor(dst, src, cos, ALU.mult))
                link(pool.tensor_tensor(r[:, :, 0:32], src[:, :, 32:64], sin[:, :, 0:32], ALU.mult))
                link(pool.tensor_tensor(r[:, :, 32:64], src[:, :, 0:32], sin[:, :, 32:64], ALU.mult))
                link(pool.tensor_tensor(dst, dst, r, ALU.add))
            pool.tensor_copy(kvr[:, :, 1, :], kvr[:, :, 0, :]).then_inc(kv_rotated, 1)
            pool.wait_ge(stats_ready, 2)
            inverse_root(pool, link, slice(0, NT))
            pool.nop().then_inc(rstd_ready, 1)
            pool.wait_ge(owner_zeroed, 32)
            pool.wait_ge(spots_ready, 1)
            for t in range(NT):
                for k in range(2):
                    c = k * NT + t
                    pool.indirect_dma_start(out=owners, out_offset=bass.IndirectOffsetOnAxis(ap=RB.inv_index[:, c:c + 1], axis=0),
                                            in_=token[:, t:t + 1], in_offset=None).then_inc(owner_stored, 16)
            pool.wait_ge(xrow_stored, 16)
            pool.wait_ge(owner_loaded, 16)
            for j in range(NBLK):
                if j >= 4:
                    pool.wait_ge(xgT_ready, j - 2)
                    pool.wait_ge(gathered[j % 4], 16 * (j // 4))
                pool.indirect_dma_start(out=xg[j % 4][:].bitcast(U32), out_offset=None, in_=x_rows,
                                        in_offset=bass.IndirectOffsetOnAxis(ap=RB.owner[:, j:j + 1], axis=0)).then_inc(gathered[j % 4], 16)
            for par in range(2):
                pool.wait_ge(y_stored[par], 16 * (NBLK // 2) + 16)
            for t in range(NT):
                for k in range(2):
                    c = k * NT + t
                    pool.indirect_dma_start(out=yg[:, t, k, :], out_offset=None, in_=y_rows,
                                            in_offset=bass.IndirectOffsetOnAxis(ap=RB.y_index[:, c:c + 1], axis=0)).then_inc(y_back, 16)
            for n in (3, 4):
                pool.wait_ge(stats_ready, n)
                inverse_root(pool, link, slice(0, NT))
                pool.nop().then_inc(rstd_ready, 1)
            pool.wait_ge(spots_ready, 2)
            for t in range(NT):
                pool.indirect_dma_start(out=owners_d, out_offset=bass.IndirectOffsetOnAxis(ap=RD.inv_index[:, t:t + 1], axis=0),
                                        in_=token[:, t:t + 1], in_offset=None).then_inc(owner_stored, 16)
            pool.wait_ge(n_stored, 16)
            pool.wait_ge(owner_loaded, 32)
            for j in range(NBLK_D):
                if j >= 4:
                    pool.wait_ge(dg_turned, j - 3)
                pool.indirect_dma_start(out=dg[j % 4][:], out_offset=None, in_=n_rows,
                                        in_offset=bass.IndirectOffsetOnAxis(ap=RD.owner[:, j:j + 1], axis=0)).then_inc(d_gathered[j % 4], 16)
            for par in range(2):
                pool.wait_ge(z_stored[par], 16 * (NBLK_D // 2) + 16)
            for t in range(NT):
                pool.indirect_dma_start(out=zg[:, t, :], out_offset=None, in_=z_rows,
                                        in_offset=bass.IndirectOffsetOnAxis(ap=RD.y_index[:, t:t + 1], axis=0)).then_inc(z_back, 16)

        @block.tensor
        def _(pe):
            pe.sem_inc(turned, 6)
            pe.sem_inc(scores_ready, 8)
            pe.sem_inc(probs_used, 8)
            pe.sem_inc(tern_turned, 6)
            pe.sem_inc(w_total, 2)
            pe.wait_ge(consts_built, 1)

            def turn(t, par, units=(0, 1, 2)):
                pe.wait_ge(parts_ready, t + 1)
                k = k_parts[par][:].rearrange("p k a g d -> p k (a g d)")
                q = q_parts[par][:].rearrange("p r a e -> p r (a e)")
                for u in units:
                    src = (k, q[:, 0:8, :], q[:, 8:16, :])[u]
                    T = bank[u % 2].bitcast(BF16)
                    if u == 2:
                        pe.wait_ge(k_unturned, t + 1)
                    elif not isinstance(t, int) or t:
                        pe.wait_ge(tern_done, 3 * t + u - 1)
                    for j in range(8):
                        mm = pe.transpose(T[0:KROWS, j * P:(j + 1) * P], src[:, j, :], ident[:])
                    mm.then_inc(turned, 1)

            def natural(t, par):
                pe.wait_ge(k_unturned, t + 1)
                pe.wait_ge(q_unturned, 2 * t + 4)
                for q in range(4):
                    pe.wait_ge(nat_read, 4 * t + q + 1)
                    for j in range(4):
                        for b in range(2):
                            r = 4 * q + j
                            mm = pe.matmul(bank[2 + q % 2][64 * b:64 * b + 64, j * P:(j + 1) * P],
                                           qT[par][:, r * P + 64 * b:r * P + 64 * b + 64],
                                           kT[par][:, r // 2, b, :, :].rearrange("p g s -> p (g s)"), start=True, stop=True)
                    mm.then_inc(nat_ready, 1)

            def turn_max(t):
                pe.wait_ge(mx_ready, t + 1)
                if not isinstance(t, int) or t:
                    pe.wait_ge(w_rec_ready, t + 1)
                pe.transpose(bank[6].bitcast(BF16)[0:96, 0:P], mx_parts[:].rearrange("p a h -> p (a h)"),
                             ident[:]).then_inc(mx_turned, 1)

            def total(e, par):
                pe.wait_ge(w_summed, e + 1)
                pe.matmul(bank[6][:, 64:67], ones[:], w_sum[par][:], start=True, stop=True).then_inc(w_total, 1)

            def turn_weights(e, par, m, after_queries=True):
                pe.wait_ge(tern_ready, 3 * e + m + 1)
                if m < 2 and after_queries:
                    pe.wait_ge(q_unturned, 2 * e + m + 7)
                else:
                    pe.wait_ge(tern_done, 3 * e + (6, 5, 7)[m])
                B = bank[1 - m % 2].bitcast(BF16)
                for c in range(4 if m < 2 else 2):
                    for k in range(2 if m < 2 else 4):
                        src = tern[par][:, m, (c * 2 + k if m < 2 else c * 4 + k) * P:][:, 0:P]
                        o = k * FF + c * P if m < 2 else k * H + c * P
                        mm = pe.transpose(B[:, o:o + P], src, ident[:])
                mm.then_inc(tern_turned, 1)

            def attend(t, par, units):
                pe.wait_ge(mxT_ready, t + 1)
                for q in units:
                    if q == 0:
                        total(t, par)
                    if q < 4:
                        B = bank[4 + q % 2]
                        pe.wait_ge(probs_ready, 4 * t + q + 1)
                        for j in range(4):
                            for b in range(2):
                                r = 4 * q + j
                                o = B[:, (2 * j + b) * 64:(2 * j + b) * 64 + 64]
                                pe.matmul(o, kT[par][:, r // 2, b, :, :].rearrange("p g s -> p (g s)"),
                                          qT[par][:, r * P + 64 * b:r * P + 64 * b + 64], start=True, stop=False)
                                mm = pe.matmul(o, negsel[:, r, :, :].rearrange("p g s -> p (g s)"),
                                               mxT[par][:, 64 * b:64 * b + 64], start=False, stop=True)
                        mm.then_inc(scores_ready, 1)
                    if q == 1:
                        pe.wait_ge(att_read, t + 1)
                        pe.wait_ge(v_ready, t + 1)
                    if q >= 1:
                        pe.wait_ge(probs_ready, 4 * t + q + 2)
                        for j in range(4):
                            for b in range(2):
                                r = 4 * (q - 1) + j
                                mm = pe.matmul(bank[7][64 * b:64 * b + 64, r * 18:r * 18 + 18],
                                               pT[q - 1][:, (2 * j + b) * 64:(2 * j + b) * 64 + 64],
                                               v_blk[par][:, b, r // 2, :, :].rearrange("p g e -> p (g e)"), start=True, stop=True)
                        mm.then_inc(probs_used, 1)

            def tile(t, par, first=False):
                turn(t + 1, 1 - par, (0, 1))
                attend(t, par, (0,))
                turn(t + 1, 1 - par, (2,))
                attend(t, par, (1,))
                if not first:
                    turn_weights(t - 1, 1 - par, 0)
                natural(t + 1, 1 - par)
                if not first:
                    turn_weights(t - 1, 1 - par, 1)
                attend(t, par, (2, 3, 4))
                if not first:
                    turn_weights(t - 1, 1 - par, 2)
                turn_max(t + 1)

            turn(0, 0)
            natural(0, 0)
            turn_max(0)
            pe.wait_ge(negsel_built, 1)
            pe.wait_ge(consts_built, 2)
            tile(0, 0, first=True)
            with pe.Fori(0, NT // 2 - 1) as i:
                tile(2 * i + 1, 1)
                tile(2 * i + 2, 0)
            attend(NT - 1, 1, (0, 1))
            turn_weights(NT - 2, 0, 0, after_queries=False)
            attend(NT - 1, 1, (2, 3, 4))
            for m in (1, 2):
                turn_weights(NT - 2, 0, m, after_queries=False)
            for m in range(3):
                turn_weights(NT - 1, 1, m, after_queries=False)

            pe.wait_ge(bconsts_built, 4)
            pe.wait_ge(x1_ready, NT)

            pe.wait_ge(r_loaded, 16)
            for k in range(2):
                mm = pe.transpose(bank[3][:, k * NE:(k + 1) * NE], r_raw[:, k * P:(k + 1) * P], identf[0:NE, 0:NE])
            mm.then_inc(r_turned, 1)
            pe.wait_ge(XN_ready, 1)
            for h in range(NT // 2):
                for k in range(2):
                    for t in range(2):
                        mm = pe.transpose(bank[4 + h % 4][:, (2 * k + t) * P:(2 * k + t + 1) * P],
                                          XN[:, 2 * h + t, k * P:(k + 1) * P], identf[:])
                mm.then_inc(XN_turned, 1)
            pe.wait_ge(r_ready, 1)
            for t in range(NT):
                pe.wait_ge(XNT_ready, t // 2 + 1)
                for k in range(2):
                    mm = pe.matmul(bank[3][:, 64 + t * NE:64 + (t + 1) * NE], XNT[:, k, t * P:(t + 1) * P], rT[:, k, :],
                                   start=k == 0, stop=k == 1)
            mm.then_inc(logits_ready, 1)
            pe.wait_ge(hot_ready, 1)
            pe.matmul(bank[4][:, 0:NT * NE], before[:], RB.hot_b[:].rearrange("p t e -> p (t e)"), start=True, stop=True)
            pe.matmul(bank[4][:, 64:64 + NT * NE], ones_b[:], RB.hot_b[:].rearrange("p t e -> p (t e)"),
                      start=True, stop=True).then_inc(counted, 1)

            pe.wait_ge(block_e_ready, 1)
            pe.wait_ge(rank_read, 1)
            pe.sem_inc(h_turned, 2)

            def turn_rows(j, q, r):
                pe.wait_ge(gathered[r], 16 * q + 16)
                pe.wait_ge(xgT_ready, j + 1)
                for k in range(2):
                    mm = pe.transpose(bank[0].bitcast(BF16)[:, k * P:(k + 1) * P], xg[r][:, k * P:(k + 1) * P], ident[:])
                mm.then_inc(xg_turned, 1)

            def expert_of(j):
                return pe.value_load(RB.block_ei[0:1, bass.ds(j, 1)], min_val=0, max_val=NE - 1)

            def gate_up(j, par, e):
                pe.wait_ge(xgT_ready, j + 2)
                pe.wait_ge(hid_done, j + 1)
                for k in range(2):
                    for m in range(2):
                        mm = pe.matmul(bank[1 + 2 * m + par][:], xgT[par][:, k * P:(k + 1) * P],
                                       WGU[:, bass.ds(e, 1), k, m, :].rearrange("p a i -> p (a i)"), start=k == 0, stop=k == 1)
                mm.then_inc(gu_ready, 1)

            def turn_hidden(j, par):
                pe.wait_ge(hq_ready, j + 1)
                pe.wait_ge(hT_ready, j + 1)
                for k in range(4):
                    mm = pe.transpose(bank[5].bitcast(BF16)[:, k * P:(k + 1) * P], hid_q[par][:, k * P:(k + 1) * P], ident[:])
                mm.then_inc(h_turned, 1)

            def down(j, par, e):
                pe.wait_ge(hT_ready, j + 2)
                pe.wait_ge(y_copied, j + 1)
                for k in range(4):
                    mm = pe.matmul(bank[6][:, 0:H], hidT[par][:, k * P:(k + 1) * P],
                                   WD[:, bass.ds(e, 1), k, :].rearrange("p a o -> p (a o)"), start=k == 0, stop=k == 3)
                mm.then_inc(y_ready, 1)

            for j in range(4):
                turn_rows(j, 0, j)
                if j:
                    gate_up(j - 1, (j - 1) % 2, expert_of(j - 1))
            with pe.Fori(0, NBLK // 4 - 1) as i:
                for r in range(4):
                    j = 4 * i + r
                    e_up, e_down = expert_of(j + 3), expert_of(j)
                    turn_hidden(j, r % 2)
                    turn_rows(j + 4, i + 1, r)
                    gate_up(j + 3, (r + 1) % 2, e_up)
                    down(j, r % 2, e_down)
            for j in range(NBLK - 4, NBLK):
                e_down = expert_of(j)
                turn_hidden(j, j % 2)
                if j + 3 < NBLK:
                    gate_up(j + 3, (j + 1) % 2, expert_of(j + 3))
                down(j, j % 2, e_down)

            pe.wait_ge(kv_rotated, 1)
            pe.wait_ge(x2_ready, NT)
            for t in range(NT):
                mm = pe.transpose(bank[4 + t // 4][:, (t % 4) * P:(t % 4 + 1) * P], kvr[:, t].rearrange("p a d -> p (a d)"), identf[:])
            mm.then_inc(kv_turned, 1)
            pe.wait_ge(XN_ready, 2)
            for h in range(NT // 2):
                for k in range(2):
                    for t in range(2):
                        mm = pe.transpose(bank[h][:, (2 * k + t) * P:(2 * k + t + 1) * P],
                                          XN[:, 2 * h + t, k * P:(k + 1) * P], identf[:])
                mm.then_inc(XN_turned, 1)
            pe.wait_ge(kvrT_ready, 2)
            pe.wait_ge(XNT_ready, NT)
            pe.sem_inc(V_ready, 2)
            pe.sem_inc(keyed, 2)
            pe.sem_inc(s_ready, 1)
            pe.sem_inc(c_ready, 1)

            def fold(u, q, par):
                pe.wait_ge(f_loaded[par], 96 * q + 96)
                for c in range(2):
                    pe.wait_ge(s_less, 2 * u + 1 + c)
                    for h in range(2):
                        mm = pe.matmul(bank[4 + c][:, h * QD:(h + 1) * QD], f_wq[par][:, h, c * P:(c + 1) * P],
                                       f_kcq[par][:, h, :], start=True, stop=True)
                    mm.then_inc(A_ready, 1)
                pe.wait_ge(roped_ready, NUNIT * u + 2)
                for h in range(2):
                    for c in range(2):
                        mm = pe.transpose(bank[0][:, h * H + c * P:h * H + (c + 1) * P], f_wo[par][:, c, h * KD:(h + 1) * KD], identf[:])
                mm.then_inc(wo_turned, 1)
                for c in range(3):
                    pe.transpose(bank[1][0:S, c * P:(c + 1) * P], f_qr[par][:, c, :], identf[:])
                pe.transpose(bank[1][0:S, 3 * P:4 * P], f_kr[par][:], identf[:]).then_inc(qr_turned, 1)
                pe.wait_ge(qrT_ready, 2 * u + 2)
                pe.wait_ge(woT_done, u + 1)
                for h in range(2):
                    mm = pe.matmul(bank[2][h * S:(h + 1) * S, 0:H], f_kv[par][:, h, :], woT[:, h, :], start=True, stop=True)
                mm.then_inc(V_ready, 1)
                pe.wait_ge(qrwT_done, u + 1)
                for r in range(2):
                    for c, (at, n) in enumerate(((0, 64), (64, 128), (192, 64))):
                        k0 = 64 if c == 2 else 0
                        mm = pe.matmul(bank[3][:, r * 2 * P + at:r * 2 * P + at + n],
                                       qrwT[:, r, :, :].rearrange("p h q -> p (h q)")[:, c * P:(c + 1) * P],
                                       krT[:, k0:k0 + n], start=True, stop=True)
                mm.then_inc(M_ready, 1)

            def rotated(u, par):
                pe.wait_ge(A_done, 2 * u + 2)
                pe.wait_ge(woT_done, u + 1)
                pe.wait_ge(qrwT_done, u + 1)

                def project(n):
                    c, g = UNITS[n]
                    pe.wait_ge(roped_ready, NUNIT * u + n + 1)
                    for k in range(2):
                        mm = pe.matmul(bank[g][:], AW[par][:, k, c * P:(c + 1) * P], XNT[:, k, g * 512:(g + 1) * 512],
                                       start=k == 0, stop=k == 1)
                    mm.then_inc(q_ready, 1)

                def to_keys_outer(g):
                    pe.wait_ge(roped_ready, NUNIT * u + 2 + g + 3)
                    for r in range(2):
                        for h, n, at in ((0, g, 0), (1, 2 + g, 192)):
                            pe.matmul(bank[2 + g][h * S:(h + 1) * S, :], MW[par][:, r, at:at + S], roped[n][:, r, :],
                                      start=r == 0, stop=False, skip_group_check=True)

                def to_keys_middle(g):
                    pe.wait_ge(roped_ready, NUNIT * u + 4 + g + 3)
                    for r in range(2):
                        mm = pe.matmul(bank[2 + g][:], MW[par][:, r, 64:192], roped[4 + g][:, r, :],
                                       start=False, stop=r == 1, skip_group_check=True)
                    mm.then_inc(keyed, 1)

                for n in range(4):
                    project(n)
                pe.wait_ge(V_done, u + 1)
                pe.wait_ge(M_done, u + 1)
                to_keys_outer(0)
                project(4)
                to_keys_outer(1)
                project(5)
                to_keys_middle(0)
                to_keys_middle(1)

            def scores(u, last=False):
                pe.wait_ge(qrT_ready, 2 * u + 4)
                pe.wait_ge(A_done, 2 * u + (2 if last else 4))
                pe.sem_inc(pe_waited, 1)
                for b in range(2 * NT):
                    for h in range(2):
                        mm = pe.matmul(bank[4 + h][64 * (b % 2):64 * (b % 2) + 64, (b // 2) * S:(b // 2 + 1) * S],
                                       qrT[h * S:(h + 1) * S, b * S:(b + 1) * S], kvrT[h * S:(h + 1) * S, b * S:(b + 1) * S],
                                       start=True, stop=True)
                mm.then_inc(s_ready, 1)

            def turn_probs(u):
                pe.wait_ge(prob_ready, 2 * u + 2)
                for t in range(NT):
                    if t % 4 == 0:
                        pe.wait_ge(ctxT_ready, 2 * u + t // 4 + 1)
                    mm = pe.transpose(bank[6 + t // 4][:, (t % 4) * P:(t % 4 + 1) * P], prob[:, t].rearrange("p h l -> p (h l)"), identf[:])
                    if t % 4 == 3:
                        mm.then_inc(prob_turned, 1)

            def contexts(u):
                pe.wait_ge(probT_ready, 2 * u + 2)
                pe.sem_inc(pe_waited, 1)
                for n in range(2 * NT):
                    for h in range(2):
                        b = (n + NT * h) % (2 * NT)
                        mm = pe.matmul(bank[6 + b // NT][h * S:(h + 1) * S, (b % NT) * S:(b % NT + 1) * S], kvr2[h * S:(h + 1) * S, b, :],
                                       probT[h * S:(h + 1) * S, b * S:(b + 1) * S], start=True, stop=True)
                mm.then_inc(c_ready, 1)

            fold(0, 0, 0)
            rotated(0, 0)
            fold(1, 0, 1)
            scores(0)
            with pe.Fori(0, NU // 2 - 1) as i:
                for u, q, par in ((2 * i + 1, i + 1, 1), (2 * i + 2, i + 1, 0)):
                    rotated(u, par)
                    turn_probs(u - 1)
                    fold(u + 1, q, 1 - par)
                    scores(u)
                    contexts(u - 1)
            rotated(NU - 1, 1)
            turn_probs(NU - 2)
            pe.wait_ge(s_less, 2 * (NU - 1) + 4)
            scores(NU - 1, last=True)
            contexts(NU - 2)
            turn_probs(NU - 1)
            contexts(NU - 1)
            pe.wait_ge(ctxT_ready, 2 * NU + 2)
            for t in range(NT):
                for u in range(NU):
                    mm = pe.matmul(bank[t // 2][:, (t % 2) * H:(t % 2 + 1) * H], ctxT[:, u, t * P:(t + 1) * P], VW[:, u, :],
                                   start=u == 0, stop=u == NU - 1)
                if t % 2:
                    mm.then_inc(o_ready, 1)

            pe.wait_ge(w_scaled_d, 1)
            for c in range(2):
                for k in range(2):
                    mm = pe.transpose(bank[6][:, k * H + c * P:k * H + (c + 1) * P], w_raw[:, c, k * P:(k + 1) * P], identf[:])
            for k in range(2):
                mm = pe.transpose(bank[7][:, k * NE_D:(k + 1) * NE_D], rd_raw[:, k * P:(k + 1) * P], identf[0:NE_D, 0:NE_D])
            mm.then_inc(w_turned_d, 1)
            pe.wait_ge(XN_ready, 3)
            for h in range(NT // 2):
                for k in range(2):
                    for t in range(2):
                        mm = pe.transpose(bank[h][:, (2 * k + t) * P:(2 * k + t + 1) * P],
                                          XN[:, 2 * h + t, k * P:(k + 1) * P], identf[:])
                mm.then_inc(XN_turned, 1)
            pe.wait_ge(rdT_ready, 1)
            for t in range(NT):
                pe.wait_ge(XNT_ready, NT + t // 2 + 1)
                for k in range(2):
                    mm = pe.matmul(bank[4][:, t * NE_D:(t + 1) * NE_D], XNT[:, k, t * P:(t + 1) * P], rdT[:, k, :],
                                   start=k == 0, stop=k == 1)
            mm.then_inc(logits_ready, 1)
            pe.wait_ge(hot_ready, 2)
            pe.matmul(bank[5][:, 0:NT * NE_D], before[:], RD.hot_b[:].rearrange("p t e -> p (t e)"), start=True, stop=True)
            pe.matmul(bank[5][:, NT * NE_D:], ones_b[:], RD.hot_b[:].rearrange("p t e -> p (t e)"),
                      start=True, stop=True).then_inc(counted, 1)
            pe.sem_inc(m_turned, 4)
            pe.sem_inc(z_ready, 2)
            with pe.Fori(0, 2) as i:
                for e in range(16):
                    pe.wait_ge(m_loaded[e // 4], 16 * i + 16)
                    pe.wait_ge(WE_ready, 16 * i + e + 1)
                    for c in range(2):
                        for k in range(2):
                            mm = pe.transpose(bank[e % 4][:, k * H + c * P:k * H + (c + 1) * P],
                                              m_raw[e // 4][:, e % 4, c, k * P:(k + 1) * P], identf[:])
                    mm.then_inc(m_turned, 1)
            pe.wait_ge(WE_ready, NE_D + 4)
            pe.wait_ge(block_e_ready, 2)
            pe.wait_ge(rank_read, 2)

            def turn_d(j, q, r):
                pe.wait_ge(d_gathered[r], 16 * q + 16)
                pe.wait_ge(dgT_ready, j + 1)
                for k in range(2):
                    mm = pe.transpose(bank[4 + r % 2][:, k * P:(k + 1) * P], dg[r][:, k * P:(k + 1) * P], identf[:])
                mm.then_inc(dg_turned, 1)

            def expert_d(j, par):
                e = pe.value_load(RD.block_ei[0:1, bass.ds(j, 1)], min_val=0, max_val=NE_D - 1)
                pe.wait_ge(dgT_ready, j + 3)
                pe.wait_ge(z_copied, j + 1)
                for k in range(2):
                    mm = pe.matmul(bank[6 + par][:, 0:H], dgT[par][:, k * P:(k + 1) * P],
                                   WE[:, bass.ds(e, 1), k, :].rearrange("p a o -> p (a o)"), start=k == 0, stop=k == 1)
                mm.then_inc(z_ready, 1)

            turn_d(0, 0, 0)
            with pe.Fori(0, NBLK_D // 4 - 1) as i:
                for r in range(4):
                    turn_d(4 * i + r + 1, i + (r + 1) // 4, (r + 1) % 4)
                    expert_d(4 * i + r, r % 2)
            for j in range(NBLK_D - 4, NBLK_D):
                if j + 1 < NBLK_D:
                    turn_d(j + 1, (j + 1) // 4, (j + 1) % 4)
                expert_d(j, j % 2)

        @block.scalar
        def _(act):
            act.sem_inc(probs_ready, 2)
            act.sem_inc(q_unturned, 2)

            def unturn(t, par, u):
                act.wait_ge(scores_ready, 4 * t + 4)
                act.wait_ge(turned, 3 * t + u + 7)
                c = (u - 1) * 8 * P
                act.activation(qT[par][:, c:c + 8 * P], bank[u % 2].bitcast(BF16)[0:KROWS, 0:8 * P],
                               ACT.Copy).then_inc(q_unturned, 1)

            def exp(t, q):
                act.wait_ge(scores_ready, 4 * t + q + 9)
                act.wait_ge(probs_used, 4 * t + q + 5)
                act.activation(pT[q][:], bank[4 + q % 2][:], ACT.Exp).then_inc(probs_ready, 1)

            def over_mean(e, par, m):
                act.wait_ge(w_rec_ready, e + 2)
                act.activation(raw[par][:, m, :], raw[par][:, m, :], ACT.Identity, scale=w_rec[par][:, m:m + 1],
                               bias=magic[:]).then_inc(w_scaled, 1)

            def magnitudes(e, h, par):
                act.wait_ge(raw_loaded[par], 48 * h + 48)
                act.wait_ge(w_total, e + 1)
                for m in range(3):
                    ins = act.activation(w_junk[:, m, :], raw[par][:, m, :], ACT.Abs, accum_out=w_sum[par][:, m:m + 1])
                ins.then_inc(w_summed, 1)

            act.wait_ge(magic_set, 1)
            magnitudes(0, 0, 0)
            def tile(t, par, h=None):
                if h is not None:
                    unturn(t + 1, 1 - par, 1)
                exp(t, 0)
                if h is not None:
                    unturn(t + 1, 1 - par, 2)
                over_mean(t, par, 0)
                exp(t, 1)
                over_mean(t, par, 1)
                over_mean(t, par, 2)
                exp(t, 2)
                exp(t, 3)
                if h is not None:
                    magnitudes(t + 1, h, 1 - par)

            unturn(0, 0, 1)
            unturn(0, 0, 2)
            tile(0, 0, 0)
            with act.Fori(0, NT // 2 - 1) as i:
                tile(2 * i + 1, 1, i + 1)
                tile(2 * i + 2, 0, i + 1)
            tile(NT - 1, 1)
            act.wait_ge(r_turned, 1)
            act.activation(rT[:].rearrange("p k e -> p (k e)"), bank[3][:, 0:2 * NE], ACT.Copy).then_inc(r_ready, 1)
            for h in range(NT // 2):
                act.wait_ge(XN_turned, h + 1)
                act.activation(XNT[:, :, 2 * h * P:2 * (h + 1) * P], bank[4 + h % 4][:].rearrange("p (k n) -> p k n", k=2),
                               ACT.Copy).then_inc(XNT_ready, 1)
            act.wait_ge(xs_ready, 1)
            for t in range(NT):
                act.activation(xq32[:, t, :], XN[:, t, :], ACT.Identity, scale=row_max[:, 1, t:t + 1], bias=magic[:]).then_inc(xq_ready, 1)
            act.wait_ge(gap_ready, 1)
            act.activation(gate[:, 1, :], gate[:, 0, :], ACT.Exp).then_inc(gate_exp, 1)
            act.sem_inc(xgT_ready, 1)
            act.sem_inc(hT_ready, 1)
            act.sem_inc(y_copied, 1)

            def rows(j, par, r):
                act.wait_ge(xg_turned, j + 1)
                act.activation(hs[r][:, 0:1], xg[r][:, H:H + 2].bitcast(F32), ACT.Copy, scale=block_w[:, 0, bass.ds(j, 1)])
                act.activation(xgT[par][:], bank[0].bitcast(BF16)[:, 0:H], ACT.Copy).then_inc(xgT_ready, 1)

            def relus(j, par):
                act.wait_ge(gu_ready, j + 1)
                act.wait_ge(hid_done, j + 1)
                act.activation(relu[par][:], bank[1 + par][:], ACT.Relu).then_inc(relu_ready, 1)

            def hidden_scaled(j, r):
                act.wait_ge(h_scale_ready, j + 1)
                act.activation(hid[r][:], hid[r][:], ACT.Identity, scale=hs[r][:, 4:5], bias=magic[:]).then_inc(hid_scaled, 1)

            def hidden_rows(j, par):
                act.wait_ge(h_turned, j + 3)
                act.activation(hidT[par][:], bank[5].bitcast(BF16)[:, 0:FF], ACT.Copy).then_inc(hT_ready, 1)

            def outputs(j, h, par, r):
                act.wait_ge(y_ready, j + 1)
                act.wait_ge(y_stored[par], 16 * h + 16)
                act.activation(y[par][:], bank[6][:, 0:H], ACT.Copy, scale=hs[r][:, 5:6]).then_inc(y_copied, 1)

            act.wait_ge(block_w_ready, 1)
            for j in range(4):
                rows(j, j % 2, j)
                if j:
                    relus(j - 1, (j - 1) % 2)
                if j == 2:
                    hidden_scaled(0, 0)
            with act.Fori(0, NBLK // 4 - 1) as i:
                for r in range(4):
                    j = 4 * i + r
                    hidden_scaled(j + 1, (r + 1) % 4)
                    hidden_rows(j, r % 2)
                    rows(j + 4, r % 2, r)
                    relus(j + 3, (r + 1) % 2)
                    outputs(j, 2 * i + r // 2, r % 2, r)
            for j in range(NBLK - 4, NBLK):
                if j + 1 < NBLK:
                    hidden_scaled(j + 1, (j + 1) % 4)
                hidden_rows(j, j % 2)
                if j + 3 < NBLK:
                    relus(j + 3, (j + 1) % 2)
                outputs(j, j // 2, j % 2, j % 4)

            act.wait_ge(kv_turned, 1)
            for h in range(2):
                act.activation(kvrT[:, h * 512:(h + 1) * 512], bank[4 + h][:], ACT.Copy).then_inc(kvrT_ready, 1)
            for h in range(NT // 2):
                act.wait_ge(XN_turned, NT // 2 + h + 1)
                act.activation(XNT[:, :, 2 * h * P:2 * (h + 1) * P], bank[h][:].rearrange("p (k n) -> p k n", k=2),
                               ACT.Copy).then_inc(XNT_ready, 1)
            act.sem_inc(qrT_ready, 2)
            act.sem_inc(ctxT_ready, 2)

            def fold(u, par):
                for c in range(2):
                    act.wait_ge(A_ready, 2 * u + c + 1)
                    act.activation(AW[par][:, c, :], bank[4 + c][:, 0:2 * QD], ACT.Copy).then_inc(A_done, 1)
                act.wait_ge(wo_turned, u + 1)
                act.activation(woT[:].rearrange("p h o -> p (h o)"), bank[0][:], ACT.Copy).then_inc(woT_done, 1)
                act.wait_ge(V_ready, u + 3)
                act.activation(VW[:, bass.ds(u, 1), :].rearrange("p a o -> p (a o)"), bank[2][:, 0:H], ACT.Copy).then_inc(V_done, 1)

            def exps(u):
                for h in range(2):
                    act.wait_ge(s_less, 2 * u + h + 5)
                    act.activation(prob[:, :, h, :], prob[:, :, h, :], ACT.Exp).then_inc(s_exp, 1)

            def queries(u):
                for g in range(2):
                    act.wait_ge(keyed, 2 * u + g + 3)
                    act.wait_ge(s_ready, u + 1)
                    act.activation(qrT[:, g * 512:(g + 1) * 512], bank[2 + g][:], ACT.Copy).then_inc(qrT_ready, 1)

            def probs(u):
                for g in range(2):
                    act.wait_ge(prob_turned, 2 * u + g + 1)
                    act.wait_ge(c_ready, u + 1)
                    act.activation(probT[:, g * 512:(g + 1) * 512], bank[6 + g][:], ACT.Copy).then_inc(probT_ready, 1)

            def contexts(u):
                act.wait_ge(c_ready, u + 2)
                for g in range(2):
                    act.activation(ctxT[:, bass.ds(u, 1), g * 512:(g + 1) * 512].rearrange("p a n -> p (a n)"), bank[6 + g][:],
                                   ACT.Copy).then_inc(ctxT_ready, 1)

            fold(0, 0)
            queries(0)
            fold(1, 1)
            with act.Fori(0, NU // 2 - 1) as i:
                for u, par in ((2 * i + 1, 1), (2 * i + 2, 0)):
                    exps(u - 1)
                    queries(u)
                    probs(u - 1)
                    fold(u + 1, 1 - par)
                    contexts(u - 1)
            exps(NU - 2)
            queries(NU - 1)
            probs(NU - 2)
            contexts(NU - 2)
            exps(NU - 1)
            probs(NU - 1)
            contexts(NU - 1)

            act.wait_ge(w_turned_d, 1)
            act.activation(rdT[:].rearrange("p k e -> p (k e)"), bank[7][:, 0:2 * NE_D], ACT.Copy).then_inc(rdT_ready, 1)
            for h in range(NT // 2):
                act.wait_ge(XN_turned, NT + h + 1)
                act.activation(XNT[:, :, 2 * h * P:2 * (h + 1) * P], bank[h][:].rearrange("p (k n) -> p k n", k=2),
                               ACT.Copy).then_inc(XNT_ready, 1)
            act.wait_ge(less_ready, 1)
            act.activation(l_exp[:], l_exp[:], ACT.Exp).then_inc(l_exp_ready, 1)
            act.sem_inc(dgT_ready, 2)
            with act.Fori(0, NBLK_D // 2) as i:
                for par in range(2):
                    j = 2 * i + par
                    act.wait_ge(dg_turned, j + 1)
                    act.wait_ge(z_ready, j + 1)
                    act.activation(dgT[par][:], bank[4 + par][:, 0:H], ACT.Copy).then_inc(dgT_ready, 1)

        @block.vector
        def _(dve):
            link = Chain(dve, dve_chain)
            dve.sem_inc(nat_read, 2)
            dve.sem_inc(att_read, 1)
            dve.memset(magic[:], MAGIC).then_inc(magic_set, 1)
            dve.sem_inc(raw_used, 2)
            dve.sem_inc(w_rec_ready, 1)
            dve.sem_inc(tern_done, 6)
            dve.wait_ge(x_loaded, 16)
            for t in range(NT):
                link(dve.bn_stats(stats[:, t, :], X[:, t, :]))
                link(dve.bn_aggr(mv[:, t, :], stats[:, t, :]))
            link(dve.tensor_scalar(var[:], mv[:, :, 1], EPS, None, ALU.add))
            dve.tensor_scalar(half_bits[:], var[:].bitcast(I32), 1, None, ALU.arith_shift_right).then_inc(stats_ready, 1)
            dve.wait_ge(ctx_loaded, 64)
            link(dve.tensor_copy(k_split[:, :, 0, :], ctxn[:]))
            link(dve.tensor_tensor(k_rest[:], ctxn[:], k_split[:, :, 0, :], ALU.subtract))
            link(dve.tensor_copy(k_split[:, :, 1, :], k_rest[:]))
            link(dve.tensor_tensor(k_split[:, :, 2, :], k_rest[:], k_split[:, :, 1, :], ALU.subtract))
            for term, part in enumerate((0, 1, 2, 0, 1, 0)):
                for g in range(2):
                    link(dve.tensor_copy(k_all[:, :, :, term, g, :],
                                         k_split[:, :, part, :].rearrange("p t (k d) -> p t k d", d=HD)))
            dve.wait_ge(rstd_ready, 1)

            def parts(t, par):
                Q = q_parts[par]
                qv = qn[:].rearrange("p (r e) -> p r e", e=2 * HD)
                qr = q_rest[:].rearrange("p (r e) -> p r e", e=2 * HD)
                link(dve.tensor_scalar(qn[:], row(X, t), row(mv, t)[:, 0:1], rstd[:, bass.ds(t, 1)], ALU.subtract, ALU.mult))
                dve.wait_ge(turned, 3 * t + 3)
                link(dve.tensor_copy(Q[:, :, 0, :], qv))
                link(dve.tensor_tensor(qr, qv, Q[:, :, 0, :], ALU.subtract))
                link(dve.tensor_copy(Q[:, :, 3, :], qr))
                dve.tensor_copy(Q[:, :, 1, :], Q[:, :, 0, :])
                dve.tensor_copy(Q[:, :, 2, :], Q[:, :, 0, :])
                dve.tensor_copy(Q[:, :, 4, :], Q[:, :, 3, :])
                dve.tensor_copy(k_parts[par][:].rearrange("p k a g d -> p (k a g d)"),
                                k_all[:, bass.ds(t, 1)].rearrange("p t k a g d -> p (t k a g d)"))
                dve.tensor_tensor(Q[:, :, 5, :], qr, Q[:, :, 3, :], ALU.subtract).then_inc(parts_ready, 1)

            def values(t, par):
                dve.tensor_copy(v_blk[par][:].rearrange("p b k g e -> p (b k g e)"),
                                v_all[:, bass.ds(2 * t, 2)].rearrange("p b k g e -> p (b k g e)")).then_inc(v_ready, 1)

            def unturn(t, par):
                dve.wait_ge(scores_ready, 4 * t + 4)
                dve.wait_ge(turned, 3 * t + 7)
                T = bank[0].bitcast(BF16)[0:KROWS, 0:8 * P].rearrange("p (k b s) -> p k b s", b=2, s=S)
                for g in range(2):
                    ins = dve.tensor_scalar(kT[par][:, :, :, g, :], T, cst[0:KROWS, g:g + 1], None, ALU.mult)
                ins.then_inc(k_unturned, 1)

            def maxima(t):
                for q in range(4):
                    dve.wait_ge(nat_ready, 4 * t + q + 1)
                    dve.tensor_reduce(mx[:, 8 * q:8 * q + 8], bank[2 + q % 2][:].rearrange("p (h s) -> p h s", s=S),
                                      AX.X, ALU.max).then_inc(nat_read, 1)
                dve.wait_ge(nat_read, 4 * t + 6)
                link(dve.tensor_copy(mx_parts[:, 0, :], mx[:]))
                link(dve.tensor_tensor(mx_rest[:, 0, :], mx[:], mx_parts[:, 0, :], ALU.subtract))
                link(dve.tensor_copy(mx_parts[:, 1, :], mx_rest[:, 0, :]))
                dve.tensor_tensor(mx_parts[:, 2, :], mx_rest[:, 0, :], mx_parts[:, 1, :], ALU.subtract).then_inc(mx_ready, 1)

            def unturn_max(t, par):
                dve.wait_ge(mx_turned, t + 1)
                dve.tensor_copy(mxT[par][:], bank[6].bitcast(BF16)[0:96, 0:P]).then_inc(mxT_ready, 1)

            def add_att(t):
                dve.wait_ge(probs_used, 4 * t + 12)
                o = bank[7][:, 0:NPAIR * 18].rearrange("p (h e) -> p h e", e=HD + 1)
                link(dve.reciprocal(den_rec[:], o[:, :, HD]))
                dve.tensor_tensor(att[:].rearrange("p (h d) -> p h d", d=HD), o[:, :, 0:HD],
                                  den_rec[:, :, None].to_broadcast([P, 32, HD]), ALU.mult).then_inc(att_read, 1)
                dve.wait_ge(att_read, t + 2)
                dve.tensor_tensor(row(X, t), row(X, t), att[:], ALU.add).then_inc(x1_ready, 1)

            def mean(e, par):
                dve.wait_ge(w_total, e + 3)
                link(dve.tensor_scalar(w_sum2[:], bank[6][:, 64:67], 1.0 / (FF * H), EPS, ALU.mult, ALU.max))
                dve.tensor_copy(w_mean[:, bass.ds(e, 1), :].rearrange("p a m -> p (a m)"), w_sum2[:])
                dve.reciprocal(w_rec[par][:], w_sum2[:]).then_inc(w_rec_ready, 1)

            def ternary(e, par):
                for m in range(3):
                    dve.wait_ge(w_scaled, 3 * e + m + 1)
                    dve.wait_ge(tern_turned, 3 * e + m + 1)
                    dve.tensor_scalar(tern[par][:, m, :], raw[par][:, m, :], MAGIC, 1.0, ALU.subtract, ALU.min).then_inc(tern_ready, 1)
                dve.wait_ge(tern_ready, 3 * e + 3)
                dve.sem_inc(raw_used, 1)

            def unturn_weights(e, m):
                dve.wait_ge(tern_turned, 3 * e + m + 7)
                src = bank[1 - m % 2].bitcast(BF16)[:]
                if m < 2:
                    dst = WGU[:, bass.ds(e, 1), :, m, :].rearrange("p a k i -> p (a k) i")
                    src = src.rearrange("p (k i) -> p k i", k=2)
                else:
                    dst = WD[:, bass.ds(e, 1)].rearrange("p a k o -> p (a k o)")
                dve.tensor_scalar(dst, src, -1.0, None, ALU.max).then_inc(tern_done, 1)

            def tile(t, par, first=False, ahead=True):
                unturn(t + 1, 1 - par)
                mean(t, par)
                if not first:
                    ternary(t - 1, 1 - par)
                maxima(t + 1)
                if not first:
                    unturn_weights(t - 1, 0)
                    unturn_weights(t - 1, 1)
                if ahead:
                    parts(t + 2, par)
                unturn_max(t + 1, 1 - par)
                if not first:
                    unturn_weights(t - 1, 2)
                add_att(t)
                if ahead:
                    values(t + 2, par)

            parts(0, 0)
            parts(1, 1)
            dve.wait_ge(v_all_ready, 4)
            values(0, 0)
            values(1, 1)
            unturn(0, 0)
            maxima(0)
            unturn_max(0, 0)
            tile(0, 0, first=True)
            with dve.Fori(0, NT // 2 - 2) as i:
                link.enter(i, 18)
                tile(2 * i + 1, 1)
                tile(2 * i + 2, 0)
                link.leave(NT // 2 - 2, 18)
            tile(NT - 3, 1)
            tile(NT - 2, 0, ahead=False)
            mean(NT - 1, 1)
            ternary(NT - 2, 0)
            unturn_weights(NT - 2, 0)
            add_att(NT - 1)
            for m in (1, 2):
                unturn_weights(NT - 2, m)
            ternary(NT - 1, 1)
            for m in range(3):
                unturn_weights(NT - 1, m)

            def normalise(n):
                for t in range(NT):
                    link(dve.bn_stats(stats[:, t, :], X[:, t, :]))
                    link(dve.bn_aggr(mv[:, t, :], stats[:, t, :]))
                link(dve.tensor_scalar(var[:], mv[:, :, 1], EPS, None, ALU.add))
                dve.tensor_scalar(half_bits[:], var[:].bitcast(I32), 1, None, ALU.arith_shift_right).then_inc(stats_ready, 1)
                dve.wait_ge(rstd_ready, n)
                for t in range(NT):
                    ins = dve.tensor_scalar(XN[:, t, :], X[:, t, :], mv[:, t, 0:1], rstd[:, t:t + 1], ALU.subtract, ALU.mult)
                ins.then_inc(XN_ready, 1)

            normalise(2)
            dve.wait_ge(XN_ready, 1)
            link(dve.tensor_reduce(row_max[:, 0, :], XN[:], AX.X, ALU.max, apply_absolute_value=True))
            link(dve.tensor_scalar(row_max[:, 0, :], row_max[:, 0, :], EPS, 1.0 / QMAX, ALU.max, ALU.mult))
            dve.reciprocal(row_max[:, 1, :], row_max[:, 0, :]).then_inc(xs_ready, 1)
            link(dve.tensor_tensor(row_max[:, 2, :], row_max[:, 0, :], row_max[:, 0, :], ALU.mult))
            link(dve.tensor_tensor(xrow[:, :, H:H + 2].bitcast(F32).rearrange("p t a -> p (t a)"),
                                   row_max[:, 2, :], row_max[:, 0, :], ALU.mult))
            dve.wait_ge(xq_ready, NT)
            dve.tensor_scalar(xrow[:, :, 0:H], xq32[:], MAGIC, None, ALU.subtract).then_inc(xrow_ready, 1)

            dve.wait_ge(logits_ready, 1)
            link(dve.tensor_copy(RB.logits[:].rearrange("p t e -> p (t e)"), bank[3][:, 64:64 + NT * NE]))
            best(dve, link, RB)
            dve.tensor_tensor(gate[:, 0, :], RB.top[:, :, 1], RB.top[:, :, 0], ALU.subtract).then_inc(gap_ready, 1)
            mark(dve, link, RB)
            dve.tensor_tensor(RB.hot_b[:], RB.hot[:, 0], RB.hot[:, 1], ALU.add).then_inc(hot_ready, 1)
            dve.wait_ge(gate_exp, 1)
            link(dve.tensor_scalar(gate[:, 0, :], gate[:, 1, :], 1.0, None, ALU.add))
            link(dve.reciprocal(gate[:, 0, :], gate[:, 0, :]))
            link(dve.tensor_tensor(gate[:, 1, :], gate[:, 1, :], gate[:, 0, :], ALU.mult))
            dve.wait_ge(counted, 1)
            link(dve.tensor_copy(RB.rank[:].rearrange("p t e -> p (t e)"), bank[4][:, 0:NT * NE]))
            dve.tensor_copy(RB.tots[:].rearrange("p t e -> p (t e)"), bank[4][:, 64:64 + NT * NE]).then_inc(rank_read, 1)
            dve.wait_ge(rank_read, 1)
            positions(dve, link, RB, 1)
            link(dve.tensor_tensor(w_prod[:, 0, :], w_mean[:, :, 0], w_mean[:, :, 0], ALU.mult))
            link(dve.tensor_tensor(w_prod[:, 0, :], w_prod[:, 0, :], w_mean[:, :, 1], ALU.mult))
            link(dve.tensor_scalar(w_prod[:, 1, :], w_mean[:, :, 2], 1.0 / QMAX, None, ALU.mult))
            link(dve.tensor_tensor(RB.below[:], RB.block_e[:, :, None].to_broadcast([P, NBLK, NE]),
                                   cst[:, None, C_IOTA:C_IOTA + NE].to_broadcast([P, NBLK, NE]), ALU.is_equal))
            for k in range(2):
                link(dve.tensor_tensor(below2[:], RB.below[:], w_prod[:, k:k + 1, :].to_broadcast([P, NBLK, NE]), ALU.mult))
                link(dve.tensor_reduce(block_w[:, k, :], below2[:], AX.X, ALU.add))
            dve.sem_inc(block_w_ready, 1)

            dve.sem_inc(hid_done, 2)

            def hidden(j, r):
                par, h = r % 2, hs[r]
                if not isinstance(j, int) or j >= 4:
                    dve.wait_ge(hq_ready, j - 3)
                dve.wait_ge(relu_ready, j + 1)
                link(dve.scalar_tensor_tensor(hid[r][:], bank[1 + par][:], 0.0, relu[par][:], ALU.max, ALU.mult))
                dve.tensor_tensor(hid[r][:], hid[r][:], bank[3 + par][:], ALU.mult).then_inc(hid_done, 1)
                dve.wait_ge(hid_done, j + 3)
                link(dve.tensor_reduce(h[:, 1:2], hid[r][:], AX.X, ALU.max, apply_absolute_value=True))
                link(dve.tensor_scalar(h[:, 2:3], h[:, 1:2], h[:, 0:1], EPS, ALU.mult, ALU.max))
                link(dve.reciprocal(h[:, 3:4], h[:, 2:3]))
                dve.tensor_scalar(h[:, 5:6], h[:, 2:3], block_w[:, 1, bass.ds(j, 1)], None, ALU.mult)
                dve.tensor_scalar(h[:, 4:5], h[:, 3:4], h[:, 0:1], QMAX, ALU.mult, ALU.mult).then_inc(h_scale_ready, 1)

            def integers(j, par, r):
                dve.wait_ge(hid_scaled, j + 1)
                dve.wait_ge(h_turned, j + 1)
                dve.tensor_scalar(hid_q[par][:], hid[r][:], MAGIC, None, ALU.subtract).then_inc(hq_ready, 1)

            for j in range(4):
                hidden(j, j)
                if j:
                    integers(j - 1, (j - 1) % 2, j - 1)
            with dve.Fori(1, NBLK // 4) as i:
                link.enter(i - 1, 16)
                for r in range(4):
                    hidden(4 * i + r, r)
                    integers(4 * i + r - 1, (r - 1) % 2, (r - 1) % 4)
                link.leave(NBLK // 4 - 1, 16)
            integers(NBLK - 1, (NBLK - 1) % 2, (NBLK - 1) % 4)

            dve.wait_ge(y_back, 16 * 2 * NT)
            for t in range(NT):
                ins = dve.scalar_tensor_tensor(X[:, t, :], yg[:, t, 0, :], gate[:, 0, t:t + 1], X[:, t, :], ALU.mult, ALU.add)
            link(ins)
            for t in range(NT):
                dve.scalar_tensor_tensor(X[:, t, :], yg[:, t, 1, :], gate[:, 1, t:t + 1], X[:, t, :],
                                         ALU.mult, ALU.add).then_inc(x2_ready, 1)

            dve.wait_ge(x2_ready, NT)
            normalise(3)
            dve.sem_inc(roped_ready, 2)
            dve.sem_inc(s_less, 4)

            def fold(u, par):
                dve.wait_ge(qr_turned, u + 1)
                T = bank[1][0:S, 0:3 * P].rearrange("p (h a q) -> p h a q", h=2, a=2)
                dve.tensor_copy(qrwT[:, 0, :, :].rearrange("p h q -> p (h q)"), bank[1][0:S, 0:3 * P])
                for a in range(2):
                    dve.tensor_copy(qrwT[:, 1, :, :].rearrange("p h (a q) -> p h a q", a=2)[:, :, a, :], T[:, :, 1 - a, :])
                dve.tensor_copy(krT[:], bank[1][0:S, 3 * P:4 * P]).then_inc(qrwT_done, 1)
                dve.wait_ge(M_ready, u + 1)
                dve.tensor_tensor(MW[par][:], bank[3][:].rearrange("p (r n) -> p r n", r=2),
                                  mask_m[:, None, :].to_broadcast([P, 2, 2 * P]), ALU.mult).then_inc(M_done, 1)

            def rope(u, n):
                c, g = UNITS[n]
                dve.wait_ge(q_ready, NUNIT * u + n + 1)
                dve.wait_ge(keyed, 2 * u + 2)
                src = bank[g][:].rearrange("p (b s) -> p b s", s=S)
                for r in range(2):
                    at = C_QCOS + (2 * c + r) * S
                    ins = dve.tensor_tensor(roped[n][:, r, :].rearrange("p (b s) -> p b s", s=S), src,
                                            cst[:, None, at:at + S].to_broadcast([P, 8, S]), ALU.mult)
                ins.then_inc(roped_ready, 1)

            def less_max(u, h):
                dve.wait_ge(s_ready, u + 2)
                dve.wait_ge(prob_turned, 2 * u + 0) if not isinstance(u, int) or u else None
                src = bank[4 + h][:].rearrange("p (t l) -> p t l", l=S)
                link(dve.tensor_reduce(s_stat[:, h, 0, :], src, AX.X, ALU.max))
                dve.tensor_tensor(prob[:, :, h, :], src, s_stat[:, h, 0, :, None].to_broadcast([P, NT, S]), ALU.subtract).then_inc(s_less, 1)

            def by_sum(u, h):
                dve.wait_ge(s_exp, 2 * u + h + 1)
                link(dve.tensor_reduce(s_stat[:, h, 1, :], prob[:, :, h, :], AX.X, ALU.add))
                link(dve.reciprocal(s_stat[:, h, 2, :], s_stat[:, h, 1, :]))
                dve.tensor_tensor(prob[:, :, h, :], prob[:, :, h, :], s_stat[:, h, 2, :, None].to_broadcast([P, NT, S]), ALU.mult).then_inc(prob_ready, 1)

            fold(0, 0)
            for n in range(NUNIT):
                rope(0, n)
            fold(1, 1)

            def pair(u):
                less_max(u - 1, 0)
                rope(u, 0)
                less_max(u - 1, 1)
                rope(u, 1)
                by_sum(u - 1, 0)
                rope(u, 2)
                by_sum(u - 1, 1)
                for n in range(3, NUNIT):
                    rope(u, n)

            with dve.Fori(0, NU // 2 - 1) as i:
                link.enter(i, 12)
                for u, par in ((2 * i + 1, 1), (2 * i + 2, 0)):
                    pair(u)
                    fold(u + 1, 1 - par)
                link.leave(NU // 2 - 1, 12)
            pair(NU - 1)
            for h in range(2):
                less_max(NU - 1, h)
            for h in range(2):
                by_sum(NU - 1, h)
            dve.wait_ge(d_loaded, 48)
            link(dve.tensor_scalar(w_raw[:], w_raw[:], 2.0, MAGIC, ALU.mult, ALU.add))
            link(dve.tensor_scalar(w_raw[:], w_raw[:], MAGIC, 1.0, ALU.subtract, ALU.min))
            link(dve.tensor_scalar(w_raw[:], w_raw[:], -1.0, None, ALU.max))
            dve.tensor_tensor(w_raw[:], w_raw[:], o_scale[:, :, None].to_broadcast([P, 2, H]), ALU.mult).then_inc(w_scaled_d, 1)
            for h in range(NT // 2):
                dve.wait_ge(o_ready, h + 1)
                for t in range(2):
                    dve.tensor_tensor(X[:, 2 * h + t, :], X[:, 2 * h + t, :], bank[h][:, t * H:(t + 1) * H], ALU.add).then_inc(x3_ready, 1)
            dve.wait_ge(x3_ready, NT)
            normalise(4)
            dve.wait_ge(w_turned_d, 1)
            link(dve.tensor_copy(wT[:].rearrange("p k o -> p (k o)"), bank[6][:]))
            dve.wait_ge(logits_ready, 2)
            link(dve.tensor_copy(RD.logits[:].rearrange("p t e -> p (t e)"), bank[4][:, 0:NT * NE_D]))
            best(dve, link, RD)
            dve.tensor_tensor(l_exp[:], RD.logits[:], RD.top[:, :, 0:1].to_broadcast([P, NT, NE_D]), ALU.subtract).then_inc(less_ready, 1)
            mark(dve, link, RD)
            dve.tensor_copy(RD.hot_b[:], RD.hot[:, 0]).then_inc(hot_ready, 1)
            dve.wait_ge(l_exp_ready, 1)
            link(dve.tensor_reduce(top_w[:, 0, :], l_exp[:], AX.X, ALU.add))
            link(dve.reciprocal(top_w[:, 1, :], top_w[:, 0, :]))
            dve.wait_ge(counted, 2)
            link(dve.tensor_copy(RD.rank[:].rearrange("p t e -> p (t e)"), bank[5][:, 0:NT * NE_D]))
            dve.tensor_copy(RD.tots[:].rearrange("p t e -> p (t e)"), bank[5][:, NT * NE_D:]).then_inc(rank_read, 1)
            dve.wait_ge(rank_read, 2)
            positions(dve, link, RD, 2)
            dve.sem_inc(WE_ready, 4)
            with dve.Fori(0, NE_D // 4) as i:
                for r in range(4):
                    dve.wait_ge(m_turned, 4 * i + r + 5)
                    dve.tensor_tensor(WE[:, bass.ds(4 * i + r, 1)].rearrange("p a k o -> p (a k o)"), bank[r][:],
                                      wT[:].rearrange("p k o -> p (k o)"), ALU.mult).then_inc(WE_ready, 1)
            dve.sem_inc(z_copied, 2)
            with dve.Fori(0, NBLK_D // 2) as i:
                for par in range(2):
                    j = 2 * i + par
                    dve.wait_ge(z_ready, j + 3)
                    dve.wait_ge(z_stored[par], 16 * i + 16)
                    dve.tensor_copy(z[par][:], bank[6 + par][:, 0:H]).then_inc(z_copied, 1)
            dve.wait_ge(z_back, 16 * NT)
            for t in range(NT):
                dve.scalar_tensor_tensor(X[:, t, :], zg[:, t, :], top_w[:, 1, t:t + 1], X[:, t, :],
                                         ALU.mult, ALU.add).then_inc(x4_ready, 1)


def constants():
    c = np.zeros((P, C_W), np.float32)
    p = np.arange(P)
    for g in range(2):
        c[:, g] = (p // HD) % 2 == g
        c[:, 2 + g] = p // S == g
    c[:, C_IOTA:C_IOTA + 48] = np.arange(48)
    c[:, C_TOKEN:C_TOKEN + NT] = p[:, None] + P * np.arange(NT)
    pos = np.arange(S, dtype=np.float32)

    def angles(dim):
        inv = np.float32(1.0) / np.float32(10000.0) ** (np.arange(0, dim, 2, dtype=np.float32) / np.float32(dim))
        a = np.repeat(pos[:, None] * inv[None, :], 2, axis=-1).astype(np.float32)
        return np.cos(a), np.sin(a)

    cos, sin = angles(S)
    sin = np.concatenate([-sin[:, :S // 2], sin[:, S // 2:]], axis=1)
    c[:, C_KCOS:C_KCOS + S] = cos[p % S]
    c[:, C_KSIN:C_KSIN + S] = sin[p % S]
    cos, sin = angles(QD)
    sin = np.concatenate([sin[:, QD // 2:], -sin[:, :QD // 2]], axis=1)
    for ch in range(3):
        f = (ch * P + p) % QD
        for r, table in enumerate((cos, sin)):
            at = C_QCOS + (2 * ch + r) * S
            c[:, at:at + S] = table[:, f].T
    return c


LAYOUTS = {
    "x": (NT * P, H), "ctx_512": (NT * P, S), "constants": (P, C_W),
    "L0_ffn_router_w": (NE, H), "L0_ffn_gate_w": (NE, FF, H), "L0_ffn_up_w": (NE, FF, H), "L0_ffn_down_w": (NE, H, FF),
    "L1_xattn_Wq": (NH * KD, H), "L1_xattn_w_kc_q": (NH, KD, QD), "L1_xattn_w_kc_kv": (NH, KD, S),
    "L1_xattn_W_qr": (NH * QD, S), "L1_xattn_W_kr": (NH * S, S), "L1_xattn_Wo": (H, NH * KD),
    "L1_ffn_weight": (H, H), "L1_ffn_scale": (P, 2), "L1_ffn_expert_masks": (NE_D, H, H), "L1_ffn_router_w": (NE_D, H),
}


def kernel(**inputs):
    import concourse.bacc as bacc
    from concourse.bass_utils import run_bass_kernel_spmd

    inputs = dict(inputs, constants=constants())
    inputs["L1_ffn_scale"] = np.asarray(inputs["L1_ffn_scale"]).reshape(2, P).T
    nc = bacc.Bacc("TRN2", target_bir_lowering=False, num_devices=1)
    arrays, args = {}, []
    for name, shape in LAYOUTS.items():
        a = np.ascontiguousarray(np.asarray(inputs[name]).reshape(shape))
        arrays[f"in_{name}_dram"] = a
        args.append(nc.dram_tensor(f"in_{name}_dram", a.shape, mybir.dt.from_np(a.dtype), kind="ExternalInput").ap())
    args.append(nc.dram_tensor("out_0_dram", (NT * P, H), F32, kind="ExternalOutput").ap())
    build(nc, *args)
    result = run_bass_kernel_spmd(nc, [arrays], core_ids=[0])
    return result.results[0]["out_0_dram"].reshape(2 * NT, S, H)
```

```python
from contextlib import ExitStack

import numpy as np

import concourse.bass as bass
from concourse import mybir

F32, F32R, BF16, I32, U32 = mybir.dt.float32, mybir.dt.float32r, mybir.dt.bfloat16, mybir.dt.int32, mybir.dt.uint32
ALU, ACT, AX = mybir.AluOpType, mybir.ActivationFunctionType, mybir.AxisListType
P = 128
NT = 8
H = 256
S = 64
NPAIR = 16
NKV = 8
HD = 8
NTERM = 6
KROWS = NTERM * 2 * HD
EPS = 1e-5
MAGIC = 1.5 * 2.0 ** 23
NE = 8
FF = 512
NBLK = 24
XROW = 258
QMAX = 127.0
NE_D = 32
PACK = 4
E_BITS, B_BITS = 5, 3
NPAIR_D = 40

NH = 16
NU = NH // 2
KD = 128
QD = 192
NUNIT = 6
UNITS = [(0, 0), (0, 1), (2, 0), (2, 1), (1, 0), (1, 1)]
SBUF_BASE, SBUF_END = 16512, 229344

C_HEAD, C_HALF, C_IOTA, C_ROW, C_TILE, C_KCOS, C_KSIN, C_QCOS = 0, 2, 4, 132, 133, 144, 208, 272
C_W = C_QCOS + 3 * 2 * S
Q_SCALE = float(np.float32(1.0) / np.sqrt(np.float32(HD)))


class Chain:

    def __init__(self, eng, sem):
        self.eng, self.sem, self.base, self.n = eng, sem, 0, 0

    def __call__(self, ins):
        self.n += 1
        ins.then_inc(self.sem, 1)
        self.eng.wait_ge(self.sem, self.base + self.n)

    def enter(self, i, per):
        self.start = self.base + self.n
        self.base, self.n = self.start + i * per, 0

    def leave(self, trips, per):
        assert self.n == per, (self.n, per)
        self.base, self.n = self.start + trips * per, 0


class Routing:

    def __init__(self, sb, s, n_e, n_blk, choices):
        n = choices * NT
        self.n_e, self.n_blk, self.choices = n_e, n_blk, choices
        self.logits = sb(f"logits{s}", [P, NT, n_e])
        self.top = sb(f"top{s}", [P, NT, 8])
        self.top_i = sb(f"top_i{s}", [P, NT, 8], U32)
        self.top_f = sb(f"top_f{s}", [P, NT, choices])
        self.hot = sb(f"hot{s}", [P, choices, NT, n_e])
        self.hot_b = sb(f"hot_b{s}", [P, NT, n_e], BF16)
        self.base = sb(f"base{s}", [P, NT, n_e])
        self.counts = sb(f"counts{s}", [P, 3, n_e])
        self.counts_i = sb(f"counts_i{s}", [P, 2, n_e], I32)
        self.picked = sb(f"picked{s}", [P, NT, n_e])
        self.pos = sb(f"pos{s}", [P, 3, n])
        self.pos_i = sb(f"pos_i{s}", [P, n], I32)
        self.y_index = sb(f"y_index{s}", [P, n], U32)
        self.at_row = sb(f"at_row{s}", [P, n, P], BF16)
        self.of_block = sb(f"of_block{s}", [P, 3, n, n_blk], BF16)
        self.owner = sb(f"owner{s}", [P, n_blk], U32)


def build(nc, x, ctx_in, cst_in, router_w, gate_w, up_w, down_w, wq, w_kc_q, w_kc_kv, w_qr, w_kr, wo,
          weight, scale, masks, router_d, out):
    with ExitStack() as ctx:
        places = {}
        place = [SBUF_BASE]

        def sb(name, shape, dt=F32):
            n = int(np.prod(shape[1:])) * (2 if dt == BF16 else 4)
            at = place[0]
            place[0] = (at + n + 31) // 32 * 32
            places[name] = at
            return nc.alloc_sbuf_tensor_at(name, shape, dt, offset=at)

        def over(name, base, shape, dt):
            return nc.alloc_sbuf_tensor_at(name, shape, dt, offset=places[base])

        def sem(name):
            return ctx.enter_context(nc.semaphore(name))

        bank = [ctx.enter_context(nc.psum_tensor(f"bank{i}", [P, 512], F32)) for i in range(8)]
        X = sb("X", [P, NT, H])
        ctxn = sb("ctxn", [P, NT, S])
        ctx2 = sb("ctx2", [P, 2 * NT, S])
        cst = sb("cst", [P, C_W])
        ident = sb("ident", [P, P], BF16)

        stats = sb("stats", [P, NT, 6])
        mv = sb("mv", [P, NT, 2])
        var = sb("var", [P, NT])
        half_bits = sb("half_bits", [P, NT], I32)
        rstd = sb("rstd", [P, NT])
        root_tmp = sb("root_tmp", [P, 2, NT])
        identf = sb("identf", [P, P])
        ones = sb("ones", [P, P])
        ones_b = sb("ones_b", [P, P], BF16)
        before = sb("before", [P, P], BF16)
        before_e = sb("before_e", [NE_D, NE_D])
        row_max = sb("row_max", [P, 4, NT])
        mask_m = sb("mask_m", [P, 2 * P])
        kvr_place = place[0]
        kvr = sb("kvr", [P, NT, 2, S])
        rot = sb("rot", [P, 2 * NT, S])
        kvr2 = sb("kvr2", [P, 2 * NT, S])
        kvrT = sb("kvrT", [P, NT * P])
        b_place = place[0]
        raw = [sb(f"raw{i}", [P, 3, 4 * H]) for i in range(2)]
        w_junk = sb("w_junk", [P, 3, 4 * H], BF16)
        w_sum = [sb(f"w_sum{i}", [P, 3]) for i in range(2)]
        w_sum2 = sb("w_sum2", [P, 3])
        magic = sb("magic", [P, 1])
        w_rec = [sb(f"w_rec{i}", [P, 3]) for i in range(2)]
        w_mean = sb("w_mean", [P, NE, 3])
        tern = [sb(f"tern{i}", [P, 3, 4 * H], BF16) for i in range(2)]
        WGU = sb("WGU", [P, NE, 2, 2, FF], BF16)
        WD = sb("WD", [P, NE, 4, H], BF16)
        r_raw = sb("r_raw", [NE, H])
        rT = sb("rT", [P, 2, NE])
        RB = Routing(sb, "_b", NE, NBLK, 2)
        gate = sb("gate", [P, 2, NT])
        below = sb("below", [P, NBLK, NE])
        block_e = sb("block_e", [P, NBLK])
        block_ei = sb("block_ei", [P, NBLK], U32)
        below2 = sb("below2", [P, NBLK, NE])
        block_w = sb("block_w", [P, 2, NBLK])
        w_prod = sb("w_prod", [P, 2, NE])
        hs = [sb(f"hs{i}", [P, 6]) for i in range(4)]
        a_place = place[0]
        qn = sb("qn", [P, H])
        q_parts = [sb(f"q_parts{i}", [P, NPAIR, NTERM, 2 * HD], BF16) for i in range(2)]
        k_parts = [sb(f"k_parts{i}", [P, NKV, NTERM, 2, HD], BF16) for i in range(2)]
        q_rest = sb("q_rest", [P, H])
        k_rest = sb("k_rest", [P, NT, S])
        k_split = sb("k_split", [P, NT, 3, S], BF16)
        k_all = sb("k_all", [P, NT, NKV, NTERM, 2, HD], BF16)
        v_all = sb("v_all", [P, 2 * NT, NKV, 2, HD + 1])
        qT = [sb(f"qT{i}", [KROWS, NPAIR * P], BF16) for i in range(2)]
        kT = [sb(f"kT{i}", [KROWS, NKV, 2, 2, S], BF16) for i in range(2)]
        negsel = sb("negsel", [96, NPAIR, 2, S], BF16)
        v_blk = [sb(f"v_blk{i}", [P, 2, NKV, 2, HD + 1]) for i in range(2)]
        mx = sb("mx", [P, 32])
        mx_rest = sb("mx_rest", [P, 2, 32])
        mx_parts = sb("mx_parts", [P, 3, 32], BF16)
        mxT = [sb(f"mxT{i}", [96, P], BF16) for i in range(2)]
        pT = [sb(f"pT{i}", [P, 512]) for i in range(4)]
        den_rec = sb("den_rec", [P, 32])
        att = sb("att", [P, H])
        place[0] = a_place
        xq32 = sb("xq32", [P, NT, H])
        xrow = sb("xrow", [P, NT, XROW], BF16)
        xg = [sb(f"xg{i}", [P, XROW], BF16) for i in range(4)]
        xgT = [sb(f"xgT{i}", [P, H], BF16) for i in range(2)]
        relu = [sb(f"relu{i}", [P, FF]) for i in range(2)]
        hid = [sb(f"hid{i}", [P, FF]) for i in range(4)]
        hid_q = [sb(f"hid_q{i}", [P, FF], BF16) for i in range(2)]
        hidT = [sb(f"hidT{i}", [P, FF], BF16) for i in range(2)]
        y = [sb(f"y{i}", [P, H]) for i in range(2)]
        yg = sb("yg", [P, NT, 2, H])
        assert place[0] <= SBUF_END - 2 * 4 * NT * H
        place[0] = SBUF_END - 2 * 4 * NT * H
        XN = sb("XN", [P, NT, H])
        XNT = sb("XNT", [P, 2, NT * P])
        place[0] = b_place
        f_wq = [sb(f"f_wq{i}", [P, 2, H]) for i in range(2)]
        f_kcq = [sb(f"f_kcq{i}", [P, 2, QD]) for i in range(2)]
        f_wo = [sb(f"f_wo{i}", [P, 2, 2 * KD]) for i in range(2)]
        f_kv = [sb(f"f_kv{i}", [P, 2, S]) for i in range(2)]
        f_qr = [sb(f"f_qr{i}", [P, 3, S]) for i in range(2)]
        f_kr = [sb(f"f_kr{i}", [P, S]) for i in range(2)]
        woT = sb("woT", [P, 2, H])
        qrwT = sb("qrwT", [S, 2, 2, QD])
        krT = sb("krT", [S, P])
        AW = [sb(f"AW{i}", [P, 2, 2 * QD]) for i in range(2)]
        MW = [sb(f"MW{i}", [P, 2, 2 * P]) for i in range(2)]
        roped = [sb(f"roped{i}", [P, 2, 512]) for i in range(NUNIT)]
        AW_lo = [over(f"AW_lo{i}", f"AW{i}", [P, 2, 2 * QD], F32R) for i in range(2)]
        XNT_hi = sb("XNT_hi", [P, 2, NT * P], F32R)
        XNT_lo = over("XNT_lo", "XNT", [P, 2, NT * P], F32R)
        qrT = sb("qrT", [P, NT * P])
        prob = sb("prob", [P, NT, 2, S])
        probT = sb("probT", [P, NT * P])
        s_stat = sb("s_stat", [P, 2, 3, NT])
        c_last, place[0] = place[0], kvr_place
        AW_hi = [sb(f"AW_hi{i}", [P, 2, 2 * QD], F32R) for i in range(2)]
        place[0] = c_last
        VW = sb("VW", [P, NU, H])
        ctxT = sb("ctxT", [P, NU, NT * P])
        c_end = place[0]
        place[0] = b_place
        WE = sb("WE", [P, NE_D, 2, H])
        assert place[0] <= c_last
        RD = Routing(sb, "_d", NE_D, NT, 1)
        l_exp = sb("l_exp", [P, NT, NE_D])
        top_w = sb("top_w", [P, 2, NT])
        ecol = sb("ecol", [NE_D, 10])
        ecol_i = sb("ecol_i", [NE_D, 2], I32)
        pair_hot = sb("pair_hot", [NE_D, 2, NPAIR_D])
        pair_v = sb("pair_v", [NE_D, 4, P])
        pairs = sb("pairs", [P, 8, NPAIR_D])
        packed = sb("packed", [P, 2, NPAIR_D // PACK])
        pair_ei = sb("pair_ei", [P, NPAIR_D // PACK], U32)
        pair_bi = sb("pair_bi", [P, NPAIR_D // PACK], U32)
        dg = sb("dg", [P, NT, 2 * H])
        dgT = sb("dgT", [P, NT, 2 * P])
        pT_d = [sb(f"pT_d{i}", [P, 2 * P]) for i in range(4)]
        place[0] = max(place[0], c_end)
        m_raw = [sb(f"m_raw{i}", [P, 4, 2, H]) for i in range(4)]
        w_raw = sb("w_raw", [P, 2, H])
        wT = sb("wT", [P, 2, H])
        rdT = sb("rdT", [P, 2, NE_D])
        o_scale = sb("o_scale", [P, 2])
        rd_raw = sb("rd_raw", [NE_D, H])
        assert place[0] <= SBUF_END - 2 * 4 * NT * H
        n_rows = nc.dram_tensor("n_rows", (NT * P, 2 * H), F32).ap()
        x_rows = nc.dram_tensor("x_rows", (NT * P, XROW // 2), U32).ap()
        y_rows = nc.dram_tensor("y_rows", (NBLK * P, H), F32).ap()

        x_loaded, ctx_loaded, out_stored = sem("x_loaded"), sem("ctx_loaded"), sem("out_stored")
        consts_built = sem("consts_built")
        bconsts_built, negsel_built, v_all_ready = sem("bconsts_built"), sem("negsel_built"), sem("v_all_ready")
        parts_ready, v_ready = sem("parts_ready"), sem("v_ready")
        turned, k_unturned, q_unturned = sem("turned"), sem("k_unturned"), sem("q_unturned")
        nat_ready, nat_read = sem("nat_ready"), sem("nat_read")
        mx_ready, mx_turned, mxT_ready = sem("mx_ready"), sem("mx_turned"), sem("mxT_ready")
        scores_ready, probs_ready, probs_used = sem("scores_ready"), sem("probs_ready"), sem("probs_used")
        att_read, x1_ready = sem("att_read"), sem("x1_ready")
        dve_chain, pool_chain = sem("dve_chain"), sem("pool_chain")

        raw_loaded = [sem(f"raw_loaded{i}") for i in range(2)]
        raw_used, w_summed, w_total, w_rec_ready, w_scaled = (sem(n) for n in ("raw_used", "w_summed", "w_total", "w_rec_ready", "w_scaled"))
        tern_ready, tern_turned, tern_done = sem("tern_ready"), sem("tern_turned"), sem("tern_done")
        magic_set = sem("magic_set")
        r_loaded, r_turned, r_ready = sem("r_loaded"), sem("r_turned"), sem("r_ready")
        XN_ready, XN_turned, XNT_ready, logits_ready = sem("XN_ready"), sem("XN_turned"), sem("XNT_ready"), sem("logits_ready")
        xs_ready, xq_ready, xrow_ready, xrow_stored = sem("xs_ready"), sem("xq_ready"), sem("xrow_ready"), sem("xrow_stored")
        gap_ready, gate_exp, hot_ready, counted = sem("gap_ready"), sem("gate_exp"), sem("hot_ready"), sem("counted")
        spots_ready, owner_summed, owner_ready = sem("spots_ready"), sem("owner_summed"), sem("owner_ready")
        block_e_ready = sem("block_e_ready")
        gathered = [sem(f"gathered{i}") for i in range(4)]
        xg_turned, xgT_ready, block_w_ready, gu_ready, hid_scaled = (sem(n) for n in ("xg_turned", "xgT_ready", "block_w_ready", "gu_ready", "hid_scaled"))
        h_scale_ready, relu_ready = sem("h_scale_ready"), sem("relu_ready")
        hid_done, hq_ready, h_turned, hT_ready, y_ready, y_copied = (sem(n) for n in ("hid_done", "hq_ready", "h_turned", "hT_ready", "y_ready", "y_copied"))
        y_stored = [sem(f"y_stored{i}") for i in range(2)]
        y_back, x2_ready, XNT_split = [sem(f"y_back{t}") for t in range(NT)], sem("x2_ready"), sem("XNT_split")
        kv_rotated, kv_turned, kvrT_ready = sem("kv_rotated"), sem("kv_turned"), sem("kvrT_ready")
        f_loaded = [sem(f"f_loaded{i}") for i in range(2)]
        A_split = sem("A_split")
        A_ready, A_done, wo_turned, woT_done = (sem(n) for n in ("A_ready", "A_done", "wo_turned", "woT_done"))
        qr_turned, qrwT_done, V_ready, V_done, M_ready, M_done = (sem(n) for n in ("qr_turned", "qrwT_done", "V_ready", "V_done", "M_ready", "M_done"))
        q_ready, roped_ready, keyed, qrT_ready = (sem(n) for n in ("q_ready", "roped_ready", "keyed", "qrT_ready"))
        s_ready, s_less, s_exp, prob_ready = (sem(n) for n in ("s_ready", "s_less", "s_exp", "prob_ready"))
        prob_turned, probT_ready, c_ready, ctxT_ready = (sem(n) for n in ("prob_turned", "probT_ready", "c_ready", "ctxT_ready"))
        o_ready, x3_ready, pe_waited = sem("o_ready"), sem("x3_ready"), sem("pe_waited")
        m_loaded = [sem(f"m_loaded{i}") for i in range(4)]
        d_loaded, w_scaled_d, w_turned_d, rdT_ready = (sem(n) for n in ("d_loaded", "w_scaled_d", "w_turned_d", "rdT_ready"))
        m_turned, WE_ready, n_stored, less_ready, l_exp_ready = (sem(n) for n in ("m_turned", "WE_ready", "n_stored", "less_ready", "l_exp_ready"))
        top_w_ready, XW_ready, pairs_ready, ecol_ready, ecol_summed = (
            sem(n) for n in ("top_w_ready", "XW_ready", "pairs_ready", "ecol_ready", "ecol_summed"))
        d_gathered = [sem(f"d_gathered{i}") for i in range(NT)]
        dg_turned, dgT_ready, pT_ready, z_ready, z_added = (sem(n) for n in ("dg_turned", "dgT_ready", "pT_ready", "z_ready", "z_added"))

        block = ctx.enter_context(nc.Block())

        def row(a, t):
            return a[:, bass.ds(t, 1), :].rearrange("p a d -> p (a d)")

        def inverse_root(dve, link):
            y, (a, b) = rstd[:], (root_tmp[:, i, :] for i in range(2))
            link(dve.tensor_scalar(half_bits[:], var[:].bitcast(I32), 1, None, ALU.arith_shift_right))
            link(dve.tensor_scalar(y.bitcast(I32), half_bits[:], -1.0, float(0x5F3759DF), ALU.mult, ALU.add))
            for _ in range(3):
                link(dve.tensor_tensor(a, y, y, ALU.mult))
                link(dve.scalar_tensor_tensor(b, a, -0.5, var[:], ALU.mult, ALU.mult))
                link(dve.scalar_tensor_tensor(y, b, 1.5, y, ALU.add, ALU.mult))

        def positions(dve, link, R, start, nth, B):
            n = R.choices * NT
            link(dve.tensor_tensor(R.base[:], R.base[:], start[:, None, :].to_broadcast([P, NT, R.n_e]), ALU.add))
            for k in range(R.choices):
                link(dve.tensor_tensor(R.picked[:], R.hot[:, k], R.base[:], ALU.mult))
                link(dve.tensor_reduce(R.pos[:, 0, k * NT:(k + 1) * NT], R.picked[:], AX.X, ALU.add))
            pos, lo, blk = (R.pos[:, i, :] for i in range(3))
            link(dve.tensor_copy(R.pos_i[:], pos))
            link(dve.tensor_scalar(R.pos_i[:], R.pos_i[:], 7, None, ALU.arith_shift_right))
            link(dve.tensor_copy(blk, R.pos_i[:]))
            link(dve.scalar_tensor_tensor(lo, blk, -float(P), pos, ALU.mult, ALU.add))
            link(dve.tensor_copy(R.y_index[:], pos))
            link(dve.tensor_tensor(R.of_block[:, 0], blk[:, :, None].to_broadcast([P, n, R.n_blk]),
                                   cst[:, None, C_IOTA:C_IOTA + R.n_blk].to_broadcast([P, n, R.n_blk]), ALU.is_equal))
            for k in range(R.choices):
                c = slice(k * NT, (k + 1) * NT)
                dve.tensor_tensor(R.of_block[:, 1, c], R.of_block[:, 0, c],
                                  cst[:, C_TILE:C_TILE + NT, None].to_broadcast([P, NT, R.n_blk]), ALU.mult)
            dve.tensor_scalar(R.of_block[:, 2], R.of_block[:, 0], cst[:, C_ROW:C_ROW + 1], None, ALU.mult)
            dve.tensor_tensor(R.at_row[:], lo[:, :, None].to_broadcast([P, n, P]),
                              cst[:, None, C_IOTA:C_IOTA + P].to_broadcast([P, n, P]), ALU.is_equal).then_inc(spots_ready, 1)
            dve.wait_ge(owner_summed, nth)
            dve.tensor_copy(R.owner[:], B[:, 0:R.n_blk]).then_inc(owner_ready, 1)

        def count(pe, R, B):
            hot = R.hot_b[:].rearrange("p t e -> p (t e)")
            n = NT * R.n_e
            for back in range(NT):
                pe.matmul(B[:, back * R.n_e:n], (ones_b if back else before)[:], hot[:, 0:n - back * R.n_e],
                          start=back == 0, stop=back == NT - 1, skip_group_check=True)
            for t in range(NT):
                mm = pe.matmul(B[:, n:n + R.n_e], ones_b[:], hot[:, t * R.n_e:(t + 1) * R.n_e],
                               start=t == 0, stop=t == NT - 1, skip_group_check=True)
            mm.then_inc(counted, 1)

        def sort(pe, R, B, nth):
            pe.wait_ge(spots_ready, nth)
            n = R.choices * NT
            for c in range(n):
                for part in (1, 2):
                    mm = pe.matmul(B[:, 0:R.n_blk], R.at_row[:, c, :], R.of_block[:, part, c, :],
                                   start=c == 0 and part == 1, stop=c == n - 1 and part == 2)
            mm.then_inc(owner_summed, 1)

        def best(dve, link, R):
            for t in range(NT):
                ins = dve.max(R.top[:, t, :], R.logits[:, t, :])
            link(ins)
            for t in range(NT):
                ins = dve.max_index(R.top_i[:, t, :], R.top[:, t, :], R.logits[:, t, :])
            link(ins)

        def mark(dve, link, R):
            link(dve.tensor_copy(R.top_f[:], R.top_i[:, :, 0:R.choices]))
            for k in range(R.choices):
                link(dve.tensor_tensor(R.hot[:, k], R.top_f[:, :, k:k + 1].to_broadcast([P, NT, R.n_e]),
                                       cst[:, None, C_IOTA:C_IOTA + R.n_e].to_broadcast([P, NT, R.n_e]), ALU.is_equal))

        @block.sync
        def _(sp):
            sp.dma_start(X[:], x.rearrange("(t p) d -> p t d", p=P)).then_inc(x_loaded, 16)
            sp.dma_start(ctxn[:], ctx_in.rearrange("(t p) d -> p t d", p=P)).then_inc(ctx_loaded, 16)
            for g in range(2):
                sp.dma_start(ctx2[64 * g:64 * g + 64], ctx_in.rearrange("(b s) d -> s b d", s=S)).then_inc(ctx_loaded, 16)
            sp.dma_start(cst[:], cst_in).then_inc(ctx_loaded, 16)
            sp.dma_start(r_raw[:], router_w).then_inc(r_loaded, 16)
            with sp.Fori(0, NE // 2) as i:
                for par in range(2):
                    sp.wait_ge(raw_used, 2 * i + par + 1)
                    for m, w in enumerate((gate_w, up_w, down_w)):
                        sp.dma_start(raw[par][:, m, :].rearrange("p (c h) -> p c h", h=w.shape[2]),
                                     w[bass.ds(2 * i + par, 1)].rearrange("a (c p) h -> p (a c) h", p=P)).then_inc(raw_loaded[par], 16)

            def load_fold(u, par):
                for dst, src in ((f_wq, wq.rearrange("(h k) i -> k h i", k=KD)[:, bass.ds(2 * u, 2), :]),
                                 (f_kcq, w_kc_q.rearrange("h k q -> k h q")[:, bass.ds(2 * u, 2), :]),
                                 (f_wo, wo.rearrange("(c o) n -> o c n", o=P)[:, :, bass.ds(2 * KD * u, 2 * KD)]),
                                 (f_kv, w_kc_kv.rearrange("h k d -> k h d")[:, bass.ds(2 * u, 2), :]),
                                 (f_qr, w_qr.rearrange("(u c p) r -> u p c r", c=3, p=P)[bass.ds(u, 1)].rearrange("a p c r -> p (a c) r")),
                                 (f_kr, w_kr[bass.ds(P * u, P), :])):
                    sp.dma_start(dst[par][:], src).then_inc(f_loaded[par], 16)

            sp.wait_ge(tern_ready, 3 * NE)
            for par in range(2):
                load_fold(par, par)
            sp.wait_ge(xrow_ready, 1)
            sp.dma_start(x_rows.rearrange("(t p) d -> p t d", p=P), xrow[:].bitcast(U32)).then_inc(xrow_stored, 16)
            for par in range(2):
                sp.sem_inc(y_stored[par], 16)
            with sp.Fori(0, NBLK // 2) as i:
                for par in range(2):
                    sp.wait_ge(y_copied, 2 * i + par + 2)
                    sp.dma_start(y_rows[bass.ds((2 * i + par) * P, P), :], y[par][:]).then_inc(y_stored[par], 16)
            sp.wait_ge(x2_ready, NT)
            for c, (dst, src) in enumerate(((w_raw, weight.rearrange("(c p) i -> p c i", p=P)), (o_scale, scale), (rd_raw, router_d))):
                sp.dma_start(dst[:], src).then_inc(d_loaded, 16)
            with sp.Fori(1, NU // 2) as i:
                for par in range(2):
                    sp.wait_ge(V_ready, 2 * i + par + 1)
                    load_fold(2 * i + par, par)
            def load_masks(g):
                sp.dma_start(m_raw[g % 4][:], masks[4 * g:4 * g + 4].rearrange("e (c p) i -> p e c i", p=P)).then_inc(m_loaded[g % 4], 16)

            for g in range(4):
                load_masks(g)
            for g in range(4, 8):
                sp.wait_ge(m_turned, 4 * (g - 3) + 4)
                load_masks(g)
            rows = n_rows.rearrange("(t p) d -> p t d", p=P)
            sp.wait_ge(x3_ready, NT)
            sp.dma_start(rows[:, :, H:], X[:]).then_inc(n_stored, 16)
            sp.wait_ge(XW_ready, NT)
            sp.dma_start(rows[:, :, 0:H], XN[:]).then_inc(n_stored, 16)

        @block.gpsimd
        def _(pool):
            link = Chain(pool, pool_chain)
            link(pool.memset(ident[:], 0.0))
            pool.affine_select(out=ident[:], in_=ident[:], compare_op=ALU.not_equal, fill=1.0, base=0,
                               pattern=[[-1, P]], channel_multiplier=1).then_inc(consts_built, 1)
            pool.memset(ones[:], 1.0).then_inc(consts_built, 1)
            pool.wait_ge(ctx_loaded, 64)
            for g in range(2):
                pool.tensor_tensor(v_all[:, :, :, g, 0:HD], ctx2[:].rearrange("p b (k d) -> p b k d", d=HD),
                                   cst[:, 2 + g:3 + g, None, None].to_broadcast([P, 2 * NT, NKV, HD]), ALU.mult).then_inc(v_all_ready, 1)
                pool.tensor_copy(v_all[:, :, :, g, HD], cst[:, 2 + g:3 + g, None].to_broadcast([P, 2 * NT, NKV])).then_inc(v_all_ready, 1)
            link(pool.memset(negsel[:], 0.0))
            for s in range(3):
                link(pool.affine_select(out=negsel[32 * s:32 * s + 32], in_=negsel[32 * s:32 * s + 32],
                                        compare_op=ALU.not_equal, fill=-1.0, base=0,
                                        pattern=[[-2, NPAIR], [-1, 2], [0, S]], channel_multiplier=1))
            pool.nop().then_inc(negsel_built, 1)
            pool.memset(ones_b[:], 1.0).then_inc(bconsts_built, 1)
            link(pool.memset(identf[:], 0.0))
            pool.affine_select(out=identf[:], in_=identf[:], compare_op=ALU.not_equal, fill=1.0, base=0,
                               pattern=[[-1, P]], channel_multiplier=1).then_inc(bconsts_built, 1)
            link(pool.memset(before[:], 0.0))
            pool.affine_select(out=before[:], in_=before[:], compare_op=ALU.is_ge, fill=1.0, base=0,
                               pattern=[[-1, P]], channel_multiplier=1).then_inc(bconsts_built, 1)
            link(pool.memset(before_e[:], 0.0))
            pool.affine_select(out=before_e[:], in_=before_e[:], compare_op=ALU.is_ge, fill=1.0, base=0,
                               pattern=[[-1, NE_D]], channel_multiplier=1).then_inc(bconsts_built, 1)
            link(pool.memset(mask_m[:], 1.0))
            link(pool.memset(mask_m[0:64, P:P + 64], 0.0))
            link(pool.memset(mask_m[64:P, 64:P], 0.0))
            for dst, src in ((kvr2[:], ctx2[:]), (kvr[:, :, 0, :], ctxn[:])):
                n = src.shape[1]
                r = rot[:, 0:n, :]
                cos = cst[:, None, C_KCOS:C_KCOS + S].to_broadcast([P, n, S])
                sin = cst[:, None, C_KSIN:C_KSIN + S].to_broadcast([P, n, S])
                link(pool.tensor_tensor(dst, src, cos, ALU.mult))
                link(pool.tensor_tensor(r[:, :, 0:32], src[:, :, 32:64], sin[:, :, 0:32], ALU.mult))
                link(pool.tensor_tensor(r[:, :, 32:64], src[:, :, 0:32], sin[:, :, 32:64], ALU.mult))
                link(pool.tensor_tensor(dst, dst, r, ALU.add))
            pool.tensor_copy(kvr[:, :, 1, :], kvr[:, :, 0, :]).then_inc(kv_rotated, 1)
            pool.wait_ge(xrow_stored, 16)
            pool.wait_ge(owner_ready, 1)
            for j in range(NBLK):
                if j >= 4:
                    pool.wait_ge(xgT_ready, j - 2)
                    pool.wait_ge(gathered[j % 4], 16 * (j // 4))
                pool.indirect_dma_start(out=xg[j % 4][:].bitcast(U32), out_offset=None, in_=x_rows,
                                        in_offset=bass.IndirectOffsetOnAxis(ap=RB.owner[:, j:j + 1], axis=0)).then_inc(gathered[j % 4], 16)
            for par in range(2):
                pool.wait_ge(y_stored[par], 16 * (NBLK // 2) + 16)
            for t in range(NT):
                for k in range(2):
                    c = k * NT + t
                    pool.indirect_dma_start(out=yg[:, t, k, :], out_offset=None, in_=y_rows,
                                            in_offset=bass.IndirectOffsetOnAxis(ap=RB.y_index[:, c:c + 1], axis=0)).then_inc(y_back[t], 16)
            pool.wait_ge(n_stored, 32)
            pool.wait_ge(owner_ready, 2)
            for b in range(NT):
                pool.indirect_dma_start(out=dg[:, b, :], out_offset=None, in_=n_rows,
                                        in_offset=bass.IndirectOffsetOnAxis(ap=RD.owner[:, b:b + 1], axis=0)).then_inc(d_gathered[b], 16)
            pool.wait_ge(z_added, NPAIR_D + 4)
            for b in range(NT):
                pool.indirect_dma_start(out=out, out_offset=bass.IndirectOffsetOnAxis(ap=RD.owner[:, b:b + 1], axis=0),
                                        in_=dg[:, b, H:], in_offset=None).then_inc(out_stored, 16)
            pool.wait_ge(out_stored, 16 * NT)

        @block.tensor
        def _(pe):
            pe.sem_inc(turned, 6)
            pe.sem_inc(scores_ready, 8)
            pe.sem_inc(probs_used, 8)
            pe.sem_inc(tern_turned, 6)
            pe.sem_inc(w_total, 2)
            pe.wait_ge(consts_built, 1)

            def turn(t, par, units=(0, 1, 2)):
                pe.wait_ge(parts_ready, t + 1)
                k = k_parts[par][:].rearrange("p k a g d -> p k (a g d)")
                q = q_parts[par][:].rearrange("p r a e -> p r (a e)")
                for u in units:
                    src = (k, q[:, 0:8, :], q[:, 8:16, :])[u]
                    T = bank[u % 2].bitcast(BF16)
                    if u == 2:
                        pe.wait_ge(k_unturned, t + 1)
                    elif not isinstance(t, int) or t:
                        pe.wait_ge(tern_done, 3 * t + u - 1)
                    for j in range(8):
                        mm = pe.transpose(T[0:KROWS, j * P:(j + 1) * P], src[:, j, :], ident[:])
                    mm.then_inc(turned, 1)

            def natural(t, par):
                pe.wait_ge(k_unturned, t + 1)
                pe.wait_ge(q_unturned, 2 * t + 4)
                for q in range(4):
                    pe.wait_ge(nat_read, 4 * t + q + 1)
                    for j in range(4):
                        for b in range(2):
                            r = 4 * q + j
                            mm = pe.matmul(bank[2 + q % 2][64 * b:64 * b + 64, j * P:(j + 1) * P],
                                           qT[par][:, r * P + 64 * b:r * P + 64 * b + 64],
                                           kT[par][:, r // 2, b, :, :].rearrange("p g s -> p (g s)"), start=True, stop=True)
                    mm.then_inc(nat_ready, 1)

            def turn_max(t):
                pe.wait_ge(mx_ready, t + 1)
                if not isinstance(t, int) or t:
                    pe.wait_ge(w_rec_ready, t + 1)
                pe.transpose(bank[6].bitcast(BF16)[0:96, 0:P], mx_parts[:].rearrange("p a h -> p (a h)"),
                             ident[:]).then_inc(mx_turned, 1)

            def total(e, par):
                pe.wait_ge(w_summed, e + 1)
                pe.matmul(bank[6][:, 64:67], ones[:], w_sum[par][:], start=True, stop=True).then_inc(w_total, 1)

            def turn_weights(e, par, m, after_queries=True):
                pe.wait_ge(tern_ready, 3 * e + m + 1)
                if m < 2 and after_queries:
                    pe.wait_ge(q_unturned, 2 * e + m + 7)
                else:
                    pe.wait_ge(tern_done, 3 * e + (6, 5, 7)[m])
                B = bank[1 - m % 2].bitcast(BF16)
                for c in range(4 if m < 2 else 2):
                    for k in range(2 if m < 2 else 4):
                        src = tern[par][:, m, (c * 2 + k if m < 2 else c * 4 + k) * P:][:, 0:P]
                        o = k * FF + c * P if m < 2 else k * H + c * P
                        mm = pe.transpose(B[:, o:o + P], src, ident[:])
                mm.then_inc(tern_turned, 1)

            def attend(t, par, units):
                pe.wait_ge(mxT_ready, t + 1)
                for q in units:
                    if q == 0:
                        total(t, par)
                    if q < 4:
                        B = bank[4 + q % 2]
                        pe.wait_ge(probs_ready, 4 * t + q + 1)
                        for j in range(4):
                            for b in range(2):
                                r = 4 * q + j
                                o = B[:, (2 * j + b) * 64:(2 * j + b) * 64 + 64]
                                pe.matmul(o, kT[par][:, r // 2, b, :, :].rearrange("p g s -> p (g s)"),
                                          qT[par][:, r * P + 64 * b:r * P + 64 * b + 64], start=True, stop=False)
                                mm = pe.matmul(o, negsel[:, r, :, :].rearrange("p g s -> p (g s)"),
                                               mxT[par][:, 64 * b:64 * b + 64], start=False, stop=True)
                        mm.then_inc(scores_ready, 1)
                    if q == 1:
                        pe.wait_ge(att_read, t + 1)
                        pe.wait_ge(v_ready, t + 1)
                    if q >= 1:
                        pe.wait_ge(probs_ready, 4 * t + q + 2)
                        for j in range(4):
                            for b in range(2):
                                r = 4 * (q - 1) + j
                                mm = pe.matmul(bank[7][64 * b:64 * b + 64, r * 18:r * 18 + 18],
                                               pT[q - 1][:, (2 * j + b) * 64:(2 * j + b) * 64 + 64],
                                               v_blk[par][:, b, r // 2, :, :].rearrange("p g e -> p (g e)"), start=True, stop=True)
                        mm.then_inc(probs_used, 1)

            def tile(t, par, first=False):
                turn(t + 1, 1 - par, (0, 1))
                attend(t, par, (0,))
                turn(t + 1, 1 - par, (2,))
                attend(t, par, (1,))
                if not first:
                    turn_weights(t - 1, 1 - par, 0)
                natural(t + 1, 1 - par)
                if not first:
                    turn_weights(t - 1, 1 - par, 1)
                attend(t, par, (2, 3, 4))
                if not first:
                    turn_weights(t - 1, 1 - par, 2)
                turn_max(t + 1)

            turn(0, 0)
            natural(0, 0)
            turn_max(0)
            pe.wait_ge(negsel_built, 1)
            pe.wait_ge(consts_built, 2)
            tile(0, 0, first=True)
            with pe.Fori(0, NT // 2 - 1) as i:
                tile(2 * i + 1, 1)
                tile(2 * i + 2, 0)
            attend(NT - 1, 1, (0, 1))
            turn_weights(NT - 2, 0, 0, after_queries=False)
            attend(NT - 1, 1, (2, 3, 4))
            for m in (1, 2):
                turn_weights(NT - 2, 0, m, after_queries=False)
            for m in range(3):
                turn_weights(NT - 1, 1, m, after_queries=False)

            pe.wait_ge(bconsts_built, 4)
            pe.wait_ge(x1_ready, NT)

            pe.wait_ge(r_loaded, 16)
            for k in range(2):
                mm = pe.transpose(bank[3][:, k * NE:(k + 1) * NE], r_raw[:, k * P:(k + 1) * P], identf[0:NE, 0:NE])
            mm.then_inc(r_turned, 1)
            pe.wait_ge(XN_ready, 1)
            for h in range(NT // 2):
                for k in range(2):
                    for t in range(2):
                        mm = pe.transpose(bank[4 + h % 4][:, (2 * k + t) * P:(2 * k + t + 1) * P],
                                          XN[:, 2 * h + t, k * P:(k + 1) * P], identf[:])
                mm.then_inc(XN_turned, 1)
            pe.wait_ge(r_ready, 1)
            for t in range(NT):
                pe.wait_ge(XNT_ready, t // 2 + 1)
                for k in range(2):
                    mm = pe.matmul(bank[3][:, 64 + t * NE:64 + (t + 1) * NE], XNT[:, k, t * P:(t + 1) * P], rT[:, k, :],
                                   start=k == 0, stop=k == 1)
            mm.then_inc(logits_ready, 1)
            pe.wait_ge(hot_ready, 1)
            count(pe, RB, bank[4])
            sort(pe, RB, bank[5], 1)

            pe.wait_ge(block_e_ready, 1)
            pe.wait_ge(owner_ready, 1)
            pe.sem_inc(h_turned, 2)

            def turn_rows(j, q, r):
                pe.wait_ge(gathered[r], 16 * q + 16)
                pe.wait_ge(xgT_ready, j + 1)
                for k in range(2):
                    mm = pe.transpose(bank[0].bitcast(BF16)[:, k * P:(k + 1) * P], xg[r][:, k * P:(k + 1) * P], ident[:])
                mm.then_inc(xg_turned, 1)

            def expert_of(j):
                return pe.value_load(block_ei[0:1, bass.ds(j, 1)], min_val=0, max_val=NE - 1)

            def gate_up(j, par, e):
                pe.wait_ge(xgT_ready, j + 2)
                pe.wait_ge(hid_done, j + 1)
                for k in range(2):
                    for m in range(2):
                        mm = pe.matmul(bank[1 + 2 * m + par][:], xgT[par][:, k * P:(k + 1) * P],
                                       WGU[:, bass.ds(e, 1), k, m, :].rearrange("p a i -> p (a i)"), start=k == 0, stop=k == 1)
                mm.then_inc(gu_ready, 1)

            def turn_hidden(j, par):
                pe.wait_ge(hq_ready, j + 1)
                pe.wait_ge(hT_ready, j + 1)
                for k in range(4):
                    mm = pe.transpose(bank[5].bitcast(BF16)[:, k * P:(k + 1) * P], hid_q[par][:, k * P:(k + 1) * P], ident[:])
                mm.then_inc(h_turned, 1)

            def down(j, par, e):
                pe.wait_ge(hT_ready, j + 2)
                pe.wait_ge(y_copied, j + 1)
                for k in range(4):
                    mm = pe.matmul(bank[6][:, 0:H], hidT[par][:, k * P:(k + 1) * P],
                                   WD[:, bass.ds(e, 1), k, :].rearrange("p a o -> p (a o)"), start=k == 0, stop=k == 3)
                mm.then_inc(y_ready, 1)

            for j in range(4):
                turn_rows(j, 0, j)
                if j:
                    gate_up(j - 1, (j - 1) % 2, expert_of(j - 1))
            with pe.Fori(0, NBLK // 4 - 1) as i:
                for r in range(4):
                    j = 4 * i + r
                    e_up, e_down = expert_of(j + 3), expert_of(j)
                    turn_hidden(j, r % 2)
                    turn_rows(j + 4, i + 1, r)
                    gate_up(j + 3, (r + 1) % 2, e_up)
                    down(j, r % 2, e_down)
            for j in range(NBLK - 4, NBLK):
                e_down = expert_of(j)
                turn_hidden(j, j % 2)
                if j + 3 < NBLK:
                    gate_up(j + 3, (j + 1) % 2, expert_of(j + 3))
                down(j, j % 2, e_down)

            pe.sem_inc(V_ready, 2)
            pe.sem_inc(keyed, 2)
            pe.sem_inc(s_ready, 1)
            pe.sem_inc(c_ready, 1)
            pe.wait_ge(kv_rotated, 1)
            pe.wait_ge(y_copied, NBLK + 1)
            for t in range(NT):
                mm = pe.transpose(bank[4 + t // 4][:, (t % 4) * P:(t % 4 + 1) * P], kvr[:, t].rearrange("p a d -> p (a d)"), identf[:])
            mm.then_inc(kv_turned, 1)
            pe.wait_ge(kvrT_ready, 2)

            def fold(u, q, par):
                pe.wait_ge(f_loaded[par], 96 * q + 96)
                for c in range(2):
                    pe.wait_ge(s_less, 2 * u + 1 + c)
                    for h in range(2):
                        mm = pe.matmul(bank[4 + c][:, h * QD:(h + 1) * QD], f_wq[par][:, h, c * P:(c + 1) * P],
                                       f_kcq[par][:, h, :], start=True, stop=True)
                    mm.then_inc(A_ready, 1)
                pe.wait_ge(roped_ready, NUNIT * u + 2)
                for h in range(2):
                    for c in range(2):
                        mm = pe.transpose(bank[0][:, h * H + c * P:h * H + (c + 1) * P], f_wo[par][:, c, h * KD:(h + 1) * KD], identf[:])
                mm.then_inc(wo_turned, 1)
                for c in range(3):
                    pe.transpose(bank[1][0:S, c * P:(c + 1) * P], f_qr[par][:, c, :], identf[:])
                pe.transpose(bank[1][0:S, 3 * P:4 * P], f_kr[par][:], identf[:]).then_inc(qr_turned, 1)
                pe.wait_ge(qrT_ready, 2 * u + 2)
                pe.wait_ge(woT_done, u + 1)
                for h in range(2):
                    mm = pe.matmul(bank[2][h * S:(h + 1) * S, 0:H], f_kv[par][:, h, :], woT[:, h, :], start=True, stop=True)
                mm.then_inc(V_ready, 1)
                pe.wait_ge(qrwT_done, u + 1)
                for r in range(2):
                    for c, (at, n) in enumerate(((0, 64), (64, 128), (192, 64))):
                        k0 = 64 if c == 2 else 0
                        mm = pe.matmul(bank[3][:, r * 2 * P + at:r * 2 * P + at + n],
                                       qrwT[:, r, :, :].rearrange("p h q -> p (h q)")[:, c * P:(c + 1) * P],
                                       krT[:, k0:k0 + n], start=True, stop=True)
                mm.then_inc(M_ready, 1)

            def rotated(u, par):
                pe.wait_ge(A_split, u + 1)
                pe.wait_ge(woT_done, u + 1)
                pe.wait_ge(qrwT_done, u + 1)

                def project(n):
                    c, g = UNITS[n]
                    pe.wait_ge(roped_ready, NUNIT * u + n + 1)
                    terms = ((AW_hi[par], XNT_hi), (AW_hi[par], XNT_lo), (AW_lo[par], XNT_hi))
                    for k in range(2):
                        for i, (a, b) in enumerate(terms):
                            mm = pe.matmul(bank[g][:], a[:, k, c * P:(c + 1) * P], b[:, k, g * 512:(g + 1) * 512],
                                           start=k == 0 and i == 0, stop=k == 1 and i == 2)
                    mm.then_inc(q_ready, 1)

                def to_keys_outer(g):
                    pe.wait_ge(roped_ready, NUNIT * u + 2 + g + 3)
                    for r in range(2):
                        for h, n, at in ((0, g, 0), (1, 2 + g, 192)):
                            pe.matmul(bank[2 + g][h * S:(h + 1) * S, :], MW[par][:, r, at:at + S], roped[n][:, r, :],
                                      start=r == 0, stop=False, skip_group_check=True)

                def to_keys_middle(g):
                    pe.wait_ge(roped_ready, NUNIT * u + 4 + g + 3)
                    for r in range(2):
                        mm = pe.matmul(bank[2 + g][:], MW[par][:, r, 64:192], roped[4 + g][:, r, :],
                                       start=False, stop=r == 1, skip_group_check=True)
                    mm.then_inc(keyed, 1)

                for n in range(4):
                    project(n)
                pe.wait_ge(V_done, u + 1)
                pe.wait_ge(M_done, u + 1)
                to_keys_outer(0)
                project(4)
                to_keys_outer(1)
                project(5)
                to_keys_middle(0)
                to_keys_middle(1)

            def scores(u, last=False):
                pe.wait_ge(qrT_ready, 2 * u + 4)
                pe.wait_ge(A_done, 2 * u + (2 if last else 4))
                pe.sem_inc(pe_waited, 1)
                for b in range(2 * NT):
                    for h in range(2):
                        mm = pe.matmul(bank[4 + h][64 * (b % 2):64 * (b % 2) + 64, (b // 2) * S:(b // 2 + 1) * S],
                                       qrT[h * S:(h + 1) * S, b * S:(b + 1) * S], kvrT[h * S:(h + 1) * S, b * S:(b + 1) * S],
                                       start=True, stop=True)
                mm.then_inc(s_ready, 1)

            def turn_probs(u):
                pe.wait_ge(prob_ready, 2 * u + 2)
                for t in range(NT):
                    if t % 4 == 0:
                        pe.wait_ge(ctxT_ready, 2 * u + t // 4 + 1)
                    mm = pe.transpose(bank[6 + t // 4][:, (t % 4) * P:(t % 4 + 1) * P], prob[:, t].rearrange("p h l -> p (h l)"), identf[:])
                    if t % 4 == 3:
                        mm.then_inc(prob_turned, 1)

            def contexts(u):
                pe.wait_ge(probT_ready, 2 * u + 2)
                pe.sem_inc(pe_waited, 1)
                for n in range(2 * NT):
                    for h in range(2):
                        b = (n + NT * h) % (2 * NT)
                        mm = pe.matmul(bank[6 + b // NT][h * S:(h + 1) * S, (b % NT) * S:(b % NT + 1) * S], kvr2[h * S:(h + 1) * S, b, :],
                                       probT[h * S:(h + 1) * S, b * S:(b + 1) * S], start=True, stop=True)
                mm.then_inc(c_ready, 1)

            fold(0, 0, 0)
            pe.wait_ge(V_done, 1)
            pe.wait_ge(M_done, 1)
            pe.wait_ge(XN_ready, 2)
            for h in range(NT // 2):
                for k in range(2):
                    for t in range(2):
                        mm = pe.transpose(bank[h][:, (2 * k + t) * P:(2 * k + t + 1) * P],
                                          XN[:, 2 * h + t, k * P:(k + 1) * P], identf[:])
                mm.then_inc(XN_turned, 1)
            pe.wait_ge(XNT_split, NT // 2)
            rotated(0, 0)
            fold(1, 0, 1)
            scores(0)
            with pe.Fori(0, NU // 2 - 1) as i:
                for u, q, par in ((2 * i + 1, i + 1, 1), (2 * i + 2, i + 1, 0)):
                    rotated(u, par)
                    turn_probs(u - 1)
                    fold(u + 1, q, 1 - par)
                    scores(u)
                    contexts(u - 1)
            rotated(NU - 1, 1)
            turn_probs(NU - 2)
            pe.wait_ge(s_less, 2 * (NU - 1) + 4)
            scores(NU - 1, last=True)
            contexts(NU - 2)
            turn_probs(NU - 1)
            contexts(NU - 1)
            pe.wait_ge(ctxT_ready, 2 * NU + 2)
            pe.wait_ge(w_scaled_d, 1)
            for c in range(2):
                for k in range(2):
                    mm = pe.transpose(bank[4][:, k * H + c * P:k * H + (c + 1) * P], w_raw[:, c, k * P:(k + 1) * P], identf[:])
            for k in range(2):
                mm = pe.transpose(bank[5][:, k * NE_D:(k + 1) * NE_D], rd_raw[:, k * P:(k + 1) * P], identf[0:NE_D, 0:NE_D])
            mm.then_inc(w_turned_d, 1)
            pe.sem_inc(m_turned, 4)
            pe.wait_ge(rdT_ready, 1)

            def turn_masks(e, slot, rounds):
                pe.wait_ge(m_loaded[slot // 4], 16 * rounds)
                pe.wait_ge(WE_ready, e + 1)
                for c in range(2):
                    for k in range(2):
                        mm = pe.transpose(bank[4 + slot % 4][:, k * H + c * P:k * H + (c + 1) * P],
                                          m_raw[slot // 4][:, slot % 4, c, k * P:(k + 1) * P], identf[:])
                mm.then_inc(m_turned, 1)

            for t in range(NT):
                for u in range(NU):
                    mm = pe.matmul(bank[t // 2][:, (t % 2) * H:(t % 2 + 1) * H], ctxT[:, u, t * P:(t + 1) * P], VW[:, u, :],
                                   start=u == 0, stop=u == NU - 1)
                if t % 2:
                    mm.then_inc(o_ready, 1)
                for e in (2 * t, 2 * t + 1):
                    turn_masks(e, e, 1)

            for e in range(4):
                turn_masks(16 + e, e, 2)
            pe.wait_ge(XN_ready, 3)
            for h in range(NT // 2):
                for k in range(2):
                    for t in range(2):
                        mm = pe.transpose(bank[h][:, (2 * k + t) * P:(2 * k + t + 1) * P],
                                          XN[:, 2 * h + t, k * P:(k + 1) * P], identf[:])
                mm.then_inc(XN_turned, 1)
            for e in range(4, 8):
                turn_masks(16 + e, e, 2)
            for t in range(NT):
                pe.wait_ge(XNT_ready, NT + t // 2 + 1)
                for k in range(2):
                    mm = pe.matmul(bank[0][:, t * NE_D:(t + 1) * NE_D], XNT[:, k, t * P:(t + 1) * P], rdT[:, k, :],
                                   start=k == 0, stop=k == 1)
            mm.then_inc(logits_ready, 1)
            pe.wait_ge(hot_ready, 2)
            for t in range(NT):
                pe.matmul(bank[3][0:NE_D, 0:1], RD.hot_b[:, t, :], ones_b[:, 0:1], start=t == 0, stop=t == NT - 1)
            count(pe, RD, bank[1])
            for i in range(2):
                if i:
                    sort(pe, RD, bank[2], 2)
                pe.wait_ge(ecol_ready, i + 1)
                pe.matmul(bank[3][0:NE_D, i + 1:i + 2], before_e[:], ecol[:, 6 * i:6 * i + 1], start=True, stop=True).then_inc(ecol_summed, 1)
            pe.wait_ge(ecol_ready, 3)
            for v in range(4):
                mm = pe.matmul(bank[3][:, 64 + v * NPAIR_D:64 + (v + 1) * NPAIR_D], pair_v[:, v, :], pair_hot[:, 1, :], start=True, stop=True)
            mm.then_inc(ecol_summed, 1)
            for e in range(8, 16):
                turn_masks(16 + e, e, 2)
                if e == 11:
                    pe.wait_ge(owner_ready, 2)
                    for b in range(NT):
                        pe.wait_ge(d_gathered[b], 16)
                        if b >= 2:
                            pe.wait_ge(dgT_ready, b - 1)
                        for k in range(2):
                            mm = pe.transpose(bank[b % 2][:, k * P:(k + 1) * P], dg[:, b, k * P:(k + 1) * P], identf[:])
                        mm.then_inc(dg_turned, 1)
            pe.wait_ge(WE_ready, NE_D + 4)
            pe.wait_ge(pairs_ready, 1)
            pe.sem_inc(z_ready, 4)
            def experts_of(g):
                return pe.value_load(pair_ei[0:1, bass.ds(g, 1)], min_val=0, max_val=(1 << E_BITS * PACK) - 1)

            with pe.Fori(0, NPAIR_D // 8) as i:
                packs = [experts_of(8 // PACK * i + g) for g in range(8 // PACK)]
                for r in range(8):
                    e = (packs[r // PACK] >> (E_BITS * (r % PACK))) & (NE_D - 1)
                    j = 8 * i + r
                    pe.wait_ge(pT_ready, j + 1)
                    pe.wait_ge(z_added, j + 1)
                    for k in range(2):
                        mm = pe.matmul(bank[4 + r % 4][:, 0:H], pT_d[r % 4][:, k * P:(k + 1) * P],
                                       WE[:, bass.ds(e, 1), k, :].rearrange("p a o -> p (a o)"), start=k == 0, stop=k == 1)
                    mm.then_inc(z_ready, 1)

        @block.scalar
        def _(act):
            act.sem_inc(probs_ready, 2)
            act.sem_inc(q_unturned, 2)

            def unturn(t, par, u):
                act.wait_ge(scores_ready, 4 * t + 4)
                act.wait_ge(turned, 3 * t + u + 7)
                c = (u - 1) * 8 * P
                act.activation(qT[par][:, c:c + 8 * P], bank[u % 2].bitcast(BF16)[0:KROWS, 0:8 * P],
                               ACT.Copy).then_inc(q_unturned, 1)

            def exp(t, q):
                act.wait_ge(scores_ready, 4 * t + q + 9)
                act.wait_ge(probs_used, 4 * t + q + 5)
                act.activation(pT[q][:], bank[4 + q % 2][:], ACT.Exp).then_inc(probs_ready, 1)

            def over_mean(e, par, m):
                act.wait_ge(w_rec_ready, e + 2)
                act.activation(raw[par][:, m, :], raw[par][:, m, :], ACT.Identity, scale=w_rec[par][:, m:m + 1],
                               bias=magic[:]).then_inc(w_scaled, 1)

            def magnitudes(e, h, par):
                act.wait_ge(raw_loaded[par], 48 * h + 48)
                act.wait_ge(w_total, e + 1)
                for m in range(3):
                    ins = act.activation(w_junk[:, m, :], raw[par][:, m, :], ACT.Abs, accum_out=w_sum[par][:, m:m + 1])
                ins.then_inc(w_summed, 1)

            act.wait_ge(magic_set, 1)
            magnitudes(0, 0, 0)
            def tile(t, par, h=None):
                if h is not None:
                    unturn(t + 1, 1 - par, 1)
                exp(t, 0)
                if h is not None:
                    unturn(t + 1, 1 - par, 2)
                over_mean(t, par, 0)
                exp(t, 1)
                over_mean(t, par, 1)
                over_mean(t, par, 2)
                exp(t, 2)
                exp(t, 3)
                if h is not None:
                    magnitudes(t + 1, h, 1 - par)

            unturn(0, 0, 1)
            unturn(0, 0, 2)
            tile(0, 0, 0)
            with act.Fori(0, NT // 2 - 1) as i:
                tile(2 * i + 1, 1, i + 1)
                tile(2 * i + 2, 0, i + 1)
            tile(NT - 1, 1)
            act.wait_ge(r_turned, 1)
            act.activation(rT[:].rearrange("p k e -> p (k e)"), bank[3][:, 0:2 * NE], ACT.Copy).then_inc(r_ready, 1)
            for h in range(NT // 2):
                act.wait_ge(XN_turned, h + 1)
                act.activation(XNT[:, :, 2 * h * P:2 * (h + 1) * P], bank[4 + h % 4][:].rearrange("p (k n) -> p k n", k=2),
                               ACT.Copy).then_inc(XNT_ready, 1)
            act.wait_ge(xs_ready, 1)
            for t in range(NT):
                act.activation(xq32[:, t, :], XN[:, t, :], ACT.Identity, scale=row_max[:, 1, t:t + 1], bias=magic[:]).then_inc(xq_ready, 1)
            act.wait_ge(gap_ready, 1)
            act.activation(gate[:, 1, :], gate[:, 0, :], ACT.Exp).then_inc(gate_exp, 1)
            act.sem_inc(xgT_ready, 1)
            act.sem_inc(hT_ready, 1)
            act.sem_inc(y_copied, 1)

            def rows(j, par, r):
                act.wait_ge(xg_turned, j + 1)
                act.activation(hs[r][:, 0:1], xg[r][:, H:H + 2].bitcast(F32), ACT.Copy, scale=block_w[:, 0, bass.ds(j, 1)])
                act.activation(xgT[par][:], bank[0].bitcast(BF16)[:, 0:H], ACT.Copy).then_inc(xgT_ready, 1)

            def relus(j, par):
                act.wait_ge(gu_ready, j + 1)
                act.wait_ge(hid_done, j + 1)
                act.activation(relu[par][:], bank[1 + par][:], ACT.Relu).then_inc(relu_ready, 1)

            def hidden_scaled(j, r):
                act.wait_ge(h_scale_ready, j + 1)
                act.activation(hid[r][:], hid[r][:], ACT.Identity, scale=hs[r][:, 4:5], bias=magic[:]).then_inc(hid_scaled, 1)

            def hidden_rows(j, par):
                act.wait_ge(h_turned, j + 3)
                act.activation(hidT[par][:], bank[5].bitcast(BF16)[:, 0:FF], ACT.Copy).then_inc(hT_ready, 1)

            def outputs(j, h, par, r):
                act.wait_ge(y_ready, j + 1)
                act.wait_ge(y_stored[par], 16 * h + 16)
                act.activation(y[par][:], bank[6][:, 0:H], ACT.Copy, scale=hs[r][:, 5:6]).then_inc(y_copied, 1)

            act.wait_ge(block_w_ready, 1)
            for j in range(4):
                rows(j, j % 2, j)
                if j:
                    relus(j - 1, (j - 1) % 2)
                if j == 2:
                    hidden_scaled(0, 0)
            with act.Fori(0, NBLK // 4 - 1) as i:
                for r in range(4):
                    j = 4 * i + r
                    hidden_scaled(j + 1, (r + 1) % 4)
                    hidden_rows(j, r % 2)
                    rows(j + 4, r % 2, r)
                    relus(j + 3, (r + 1) % 2)
                    outputs(j, 2 * i + r // 2, r % 2, r)
            for j in range(NBLK - 4, NBLK):
                if j + 1 < NBLK:
                    hidden_scaled(j + 1, (j + 1) % 4)
                hidden_rows(j, j % 2)
                if j + 3 < NBLK:
                    relus(j + 3, (j + 1) % 2)
                outputs(j, j // 2, j % 2, j % 4)

            act.wait_ge(kv_turned, 1)
            for h in range(2):
                act.activation(kvrT[:, h * 512:(h + 1) * 512], bank[4 + h][:], ACT.Copy).then_inc(kvrT_ready, 1)
            act.sem_inc(qrT_ready, 2)
            act.sem_inc(ctxT_ready, 2)

            def fold(u, par):
                for c in range(2):
                    act.wait_ge(A_ready, 2 * u + c + 1)
                    act.activation(AW[par][:, c, :], bank[4 + c][:, 0:2 * QD], ACT.Copy).then_inc(A_done, 1)
                act.wait_ge(wo_turned, u + 1)
                act.activation(woT[:].rearrange("p h o -> p (h o)"), bank[0][:], ACT.Copy).then_inc(woT_done, 1)
                act.wait_ge(V_ready, u + 3)
                act.activation(VW[:, bass.ds(u, 1), :].rearrange("p a o -> p (a o)"), bank[2][:, 0:H], ACT.Copy).then_inc(V_done, 1)

            def exps(u):
                for h in range(2):
                    act.wait_ge(s_less, 2 * u + h + 5)
                    act.activation(prob[:, :, h, :], prob[:, :, h, :], ACT.Exp).then_inc(s_exp, 1)

            def queries(u):
                for g in range(2):
                    act.wait_ge(keyed, 2 * u + g + 3)
                    act.wait_ge(s_ready, u + 1)
                    act.activation(qrT[:, g * 512:(g + 1) * 512], bank[2 + g][:], ACT.Copy).then_inc(qrT_ready, 1)

            def probs(u):
                for g in range(2):
                    act.wait_ge(prob_turned, 2 * u + g + 1)
                    act.wait_ge(c_ready, u + 1)
                    act.activation(probT[:, g * 512:(g + 1) * 512], bank[6 + g][:], ACT.Copy).then_inc(probT_ready, 1)

            def contexts(u):
                act.wait_ge(c_ready, u + 2)
                for g in range(2):
                    act.activation(ctxT[:, bass.ds(u, 1), g * 512:(g + 1) * 512].rearrange("p a n -> p (a n)"), bank[6 + g][:],
                                   ACT.Copy).then_inc(ctxT_ready, 1)

            fold(0, 0)
            for h in range(NT // 2):
                act.wait_ge(XN_turned, NT // 2 + h + 1)
                act.activation(XNT_hi[:, :, 2 * h * P:2 * (h + 1) * P], bank[h][:].rearrange("p (k n) -> p k n", k=2),
                               ACT.Copy).then_inc(XNT_ready, 1)
            queries(0)
            fold(1, 1)
            exps(0)
            with act.Fori(0, NU // 2 - 1) as i:
                for u, par in ((2 * i + 1, 1), (2 * i + 2, 0)):
                    queries(u)
                    probs(u - 1)
                    fold(u + 1, 1 - par)
                    exps(u)
                    contexts(u - 1)
            queries(NU - 1)
            probs(NU - 2)
            exps(NU - 1)
            contexts(NU - 2)
            probs(NU - 1)
            contexts(NU - 1)

            act.wait_ge(w_turned_d, 1)
            act.activation(rdT[:].rearrange("p k e -> p (k e)"), bank[5][:, 0:2 * NE_D], ACT.Copy).then_inc(rdT_ready, 1)
            for h in range(NT // 2):
                act.wait_ge(XN_turned, NT + h + 1)
                act.activation(XNT[:, :, 2 * h * P:2 * (h + 1) * P], bank[h][:].rearrange("p (k n) -> p k n", k=2),
                               ACT.Copy).then_inc(XNT_ready, 1)
            act.wait_ge(less_ready, 1)
            act.activation(l_exp[:], l_exp[:], ACT.Exp).then_inc(l_exp_ready, 1)
            act.wait_ge(top_w_ready, 1)
            for t in range(NT):
                act.activation(XN[:, t, :], XN[:, t, :], ACT.Copy, scale=top_w[:, 1, t:t + 1]).then_inc(XW_ready, 1)
            for b in range(NT):
                act.wait_ge(dg_turned, b + 1)
                act.activation(dgT[:, b, :], bank[b % 2][:, 0:2 * P], ACT.Copy).then_inc(dgT_ready, 1)
            act.wait_ge(pairs_ready, 1)
            act.wait_ge(dgT_ready, NT)
            def blocks_of(g):
                return act.value_load(pair_bi[0:1, bass.ds(g, 1)], min_val=0, max_val=(1 << B_BITS * PACK) - 1)

            with act.Fori(0, NPAIR_D // 8) as i:
                packs = [blocks_of(8 // PACK * i + g) for g in range(8 // PACK)]
                for r in range(8):
                    b = (packs[r // PACK] >> (B_BITS * (r % PACK))) & (NT - 1)
                    act.wait_ge(z_ready, 8 * i + r + 1)
                    act.activation(pT_d[r % 4][:], dgT[:, bass.ds(b, 1), :].rearrange("p a n -> p (a n)"), ACT.Copy).then_inc(pT_ready, 1)

        @block.vector
        def _(dve):
            link = Chain(dve, dve_chain)
            dve.sem_inc(nat_read, 2)
            dve.sem_inc(att_read, 1)
            dve.memset(magic[:], MAGIC).then_inc(magic_set, 1)

            def statistics(tiles):
                for t in tiles:
                    ins = dve.bn_stats(stats[:, t, :], X[:, t, :])
                link(ins)

            def aggregate():
                for t in range(NT):
                    ins = dve.bn_aggr(mv[:, t, :], stats[:, t, :])
                link(ins)
                link(dve.tensor_scalar(var[:], mv[:, :, 1], EPS, None, ALU.add))
                inverse_root(dve, link)

            dve.sem_inc(raw_used, 2)
            dve.sem_inc(w_rec_ready, 1)
            dve.sem_inc(tern_done, 6)
            dve.wait_ge(x_loaded, 16)
            statistics(range(NT))
            aggregate()
            link(dve.tensor_scalar(rstd[:], rstd[:], Q_SCALE, None, ALU.mult))
            dve.wait_ge(ctx_loaded, 64)
            link(dve.tensor_copy(k_split[:, :, 0, :], ctxn[:]))
            link(dve.tensor_tensor(k_rest[:], ctxn[:], k_split[:, :, 0, :], ALU.subtract))
            link(dve.tensor_copy(k_split[:, :, 1, :], k_rest[:]))
            link(dve.tensor_tensor(k_split[:, :, 2, :], k_rest[:], k_split[:, :, 1, :], ALU.subtract))
            for term, part in enumerate((0, 1, 2, 0, 1, 0)):
                for g in range(2):
                    ins = dve.tensor_copy(k_all[:, :, :, term, g, :],
                                          k_split[:, :, part, :].rearrange("p t (k d) -> p t k d", d=HD))
            link(ins)

            def parts(t, par):
                Q = q_parts[par]
                qv = qn[:].rearrange("p (r e) -> p r e", e=2 * HD)
                qr = q_rest[:].rearrange("p (r e) -> p r e", e=2 * HD)
                link(dve.tensor_scalar(qn[:], row(X, t), row(mv, t)[:, 0:1], rstd[:, bass.ds(t, 1)], ALU.subtract, ALU.mult))
                dve.wait_ge(turned, 3 * t + 3)
                link(dve.tensor_copy(Q[:, :, 0, :], qv))
                link(dve.tensor_tensor(qr, qv, Q[:, :, 0, :], ALU.subtract))
                link(dve.tensor_copy(Q[:, :, 3, :], qr))
                dve.tensor_copy(Q[:, :, 1, :], Q[:, :, 0, :])
                dve.tensor_copy(Q[:, :, 2, :], Q[:, :, 0, :])
                dve.tensor_copy(Q[:, :, 4, :], Q[:, :, 3, :])
                dve.tensor_copy(k_parts[par][:].rearrange("p k a g d -> p (k a g d)"),
                                k_all[:, bass.ds(t, 1)].rearrange("p t k a g d -> p (t k a g d)"))
                dve.tensor_tensor(Q[:, :, 5, :], qr, Q[:, :, 3, :], ALU.subtract).then_inc(parts_ready, 1)

            def values(t, par):
                dve.tensor_copy(v_blk[par][:].rearrange("p b k g e -> p (b k g e)"),
                                v_all[:, bass.ds(2 * t, 2)].rearrange("p b k g e -> p (b k g e)")).then_inc(v_ready, 1)

            def unturn(t, par):
                dve.wait_ge(scores_ready, 4 * t + 4)
                dve.wait_ge(turned, 3 * t + 7)
                T = bank[0].bitcast(BF16)[0:KROWS, 0:8 * P].rearrange("p (k b s) -> p k b s", b=2, s=S)
                for g in range(2):
                    ins = dve.tensor_scalar(kT[par][:, :, :, g, :], T, cst[0:KROWS, g:g + 1], None, ALU.mult)
                ins.then_inc(k_unturned, 1)

            def maxima(t):
                for q in range(4):
                    dve.wait_ge(nat_ready, 4 * t + q + 1)
                    dve.tensor_reduce(mx[:, 8 * q:8 * q + 8], bank[2 + q % 2][:].rearrange("p (h s) -> p h s", s=S),
                                      AX.X, ALU.max).then_inc(nat_read, 1)
                dve.wait_ge(nat_read, 4 * t + 6)
                link(dve.tensor_copy(mx_parts[:, 0, :], mx[:]))
                link(dve.tensor_tensor(mx_rest[:, 0, :], mx[:], mx_parts[:, 0, :], ALU.subtract))
                link(dve.tensor_copy(mx_parts[:, 1, :], mx_rest[:, 0, :]))
                dve.tensor_tensor(mx_parts[:, 2, :], mx_rest[:, 0, :], mx_parts[:, 1, :], ALU.subtract).then_inc(mx_ready, 1)

            def unturn_max(t, par):
                dve.wait_ge(mx_turned, t + 1)
                dve.tensor_copy(mxT[par][:], bank[6].bitcast(BF16)[0:96, 0:P]).then_inc(mxT_ready, 1)

            def add_att(t):
                dve.wait_ge(probs_used, 4 * t + 12)
                o = bank[7][:, 0:NPAIR * 18].rearrange("p (h e) -> p h e", e=HD + 1)
                link(dve.reciprocal(den_rec[:], o[:, :, HD]))
                dve.tensor_tensor(att[:].rearrange("p (h d) -> p h d", d=HD), o[:, :, 0:HD],
                                  den_rec[:, :, None].to_broadcast([P, 32, HD]), ALU.mult).then_inc(att_read, 1)
                dve.wait_ge(att_read, t + 2)
                dve.tensor_tensor(row(X, t), row(X, t), att[:], ALU.add).then_inc(x1_ready, 1)

            def mean(e, par):
                dve.wait_ge(w_total, e + 3)
                link(dve.tensor_scalar(w_sum2[:], bank[6][:, 64:67], 1.0 / (FF * H), EPS, ALU.mult, ALU.max))
                dve.tensor_copy(w_mean[:, bass.ds(e, 1), :].rearrange("p a m -> p (a m)"), w_sum2[:])
                dve.reciprocal(w_rec[par][:], w_sum2[:]).then_inc(w_rec_ready, 1)

            def ternary(e, par):
                for m in range(3):
                    dve.wait_ge(w_scaled, 3 * e + m + 1)
                    dve.wait_ge(tern_turned, 3 * e + m + 1)
                    dve.tensor_scalar(tern[par][:, m, :], raw[par][:, m, :], MAGIC, 1.0, ALU.subtract, ALU.min).then_inc(tern_ready, 1)
                dve.wait_ge(tern_ready, 3 * e + 3)
                dve.sem_inc(raw_used, 1)

            def unturn_weights(e, m):
                dve.wait_ge(tern_turned, 3 * e + m + 7)
                src = bank[1 - m % 2].bitcast(BF16)[:]
                if m < 2:
                    dst = WGU[:, bass.ds(e, 1), :, m, :].rearrange("p a k i -> p (a k) i")
                    src = src.rearrange("p (k i) -> p k i", k=2)
                else:
                    dst = WD[:, bass.ds(e, 1)].rearrange("p a k o -> p (a k o)")
                dve.tensor_scalar(dst, src, -1.0, None, ALU.max).then_inc(tern_done, 1)

            def tile(t, par, first=False, ahead=True):
                unturn(t + 1, 1 - par)
                mean(t, par)
                if not first:
                    ternary(t - 1, 1 - par)
                maxima(t + 1)
                if not first:
                    unturn_weights(t - 1, 0)
                    unturn_weights(t - 1, 1)
                if ahead:
                    parts(t + 2, par)
                unturn_max(t + 1, 1 - par)
                if not first:
                    unturn_weights(t - 1, 2)
                add_att(t)
                if ahead:
                    values(t + 2, par)

            parts(0, 0)
            unturn(0, 0)
            parts(1, 1)
            maxima(0)
            dve.wait_ge(v_all_ready, 4)
            values(0, 0)
            values(1, 1)
            unturn_max(0, 0)
            tile(0, 0, first=True)
            with dve.Fori(0, NT // 2 - 2) as i:
                link.enter(i, 18)
                tile(2 * i + 1, 1)
                tile(2 * i + 2, 0)
                link.leave(NT // 2 - 2, 18)
            tile(NT - 3, 1)
            tile(NT - 2, 0, ahead=False)
            mean(NT - 1, 1)
            ternary(NT - 2, 0)
            unturn_weights(NT - 2, 0)
            dve.wait_ge(x1_ready, NT - 1)
            statistics(range(NT - 1))
            add_att(NT - 1)
            for m in (1, 2):
                unturn_weights(NT - 2, m)
            ternary(NT - 1, 1)
            for m in range(3):
                unturn_weights(NT - 1, m)

            def normalise():
                aggregate()
                for t in range(NT):
                    ins = dve.tensor_scalar(XN[:, t, :], X[:, t, :], mv[:, t, 0:1], rstd[:, t:t + 1], ALU.subtract, ALU.mult)
                ins.then_inc(XN_ready, 1)

            dve.wait_ge(x1_ready, NT)
            statistics([NT - 1])
            normalise()
            dve.wait_ge(XN_ready, 1)
            link(dve.tensor_reduce(row_max[:, 0, :], XN[:], AX.X, ALU.max, apply_absolute_value=True))
            link(dve.tensor_scalar(row_max[:, 0, :], row_max[:, 0, :], EPS, 1.0 / QMAX, ALU.max, ALU.mult))
            dve.reciprocal(row_max[:, 1, :], row_max[:, 0, :]).then_inc(xs_ready, 1)
            link(dve.tensor_tensor(row_max[:, 2, :], row_max[:, 0, :], row_max[:, 0, :], ALU.mult))
            link(dve.tensor_tensor(xrow[:, :, H:H + 2].bitcast(F32).rearrange("p t a -> p (t a)"),
                                   row_max[:, 2, :], row_max[:, 0, :], ALU.mult))

            dve.wait_ge(xq_ready, NT)
            dve.tensor_scalar(xrow[:, :, 0:H], xq32[:], MAGIC, None, ALU.subtract).then_inc(xrow_ready, 1)

            dve.wait_ge(logits_ready, 1)
            link(dve.tensor_copy(RB.logits[:].rearrange("p t e -> p (t e)"), bank[3][:, 64:64 + NT * NE]))
            best(dve, link, RB)
            dve.tensor_tensor(gate[:, 0, :], RB.top[:, :, 1], RB.top[:, :, 0], ALU.subtract).then_inc(gap_ready, 1)
            mark(dve, link, RB)
            dve.tensor_tensor(RB.hot_b[:], RB.hot[:, 0], RB.hot[:, 1], ALU.add).then_inc(hot_ready, 1)
            dve.wait_ge(gate_exp, 1)
            link(dve.tensor_scalar(gate[:, 0, :], gate[:, 1, :], 1.0, None, ALU.add))
            link(dve.reciprocal(gate[:, 0, :], gate[:, 0, :]))
            link(dve.tensor_tensor(gate[:, 1, :], gate[:, 1, :], gate[:, 0, :], ALU.mult))
            dve.wait_ge(counted, 1)
            link(dve.tensor_copy(RB.base[:].rearrange("p t e -> p (t e)"), bank[4][:, 0:NT * NE]))
            link(dve.tensor_scalar(RB.counts_i[:, 0, :], bank[4][:, NT * NE:NT * NE + NE], float(P - 1), None, ALU.add))
            link(dve.tensor_scalar(RB.counts_i[:, 0, :], RB.counts_i[:, 0, :], 7, None, ALU.arith_shift_right))
            n_blocks, upto, start = (RB.counts[:, i, :] for i in range(3))
            link(dve.tensor_copy(n_blocks, RB.counts_i[:, 0, :]))
            link(dve.tensor_tensor_scan(upto, ones[:, 0:NE], n_blocks, 0.0, ALU.mult, ALU.add))
            link(dve.tensor_tensor(start, upto, n_blocks, ALU.subtract))
            link(dve.tensor_scalar(start, start, float(P), None, ALU.mult))
            positions(dve, link, RB, start, 1, bank[5])
            link(dve.tensor_tensor(below[:], upto[:, None, :].to_broadcast([P, NBLK, NE]),
                                   cst[:, C_IOTA:C_IOTA + NBLK, None].to_broadcast([P, NBLK, NE]), ALU.is_le))
            link(dve.tensor_reduce(block_e[:], below[:], AX.X, ALU.add))
            link(dve.tensor_scalar(block_e[:], block_e[:], float(NE - 1), None, ALU.min))
            dve.tensor_copy(block_ei[:], block_e[:]).then_inc(block_e_ready, 1)
            link(dve.tensor_tensor(w_prod[:, 0, :], w_mean[:, :, 0], w_mean[:, :, 0], ALU.mult))
            link(dve.tensor_tensor(w_prod[:, 0, :], w_prod[:, 0, :], w_mean[:, :, 1], ALU.mult))
            link(dve.tensor_scalar(w_prod[:, 1, :], w_mean[:, :, 2], 1.0 / QMAX, None, ALU.mult))
            link(dve.tensor_tensor(below[:], block_e[:, :, None].to_broadcast([P, NBLK, NE]),
                                   cst[:, None, C_IOTA:C_IOTA + NE].to_broadcast([P, NBLK, NE]), ALU.is_equal))
            for k in range(2):
                link(dve.tensor_tensor(below2[:], below[:], w_prod[:, k:k + 1, :].to_broadcast([P, NBLK, NE]), ALU.mult))
                link(dve.tensor_reduce(block_w[:, k, :], below2[:], AX.X, ALU.add))
            dve.sem_inc(block_w_ready, 1)

            dve.sem_inc(hid_done, 2)

            def hidden(j, r):
                par, h = r % 2, hs[r]
                if not isinstance(j, int) or j >= 4:
                    dve.wait_ge(hq_ready, j - 3)
                dve.wait_ge(relu_ready, j + 1)
                link(dve.scalar_tensor_tensor(hid[r][:], bank[1 + par][:], 0.0, relu[par][:], ALU.max, ALU.mult))
                dve.tensor_tensor(hid[r][:], hid[r][:], bank[3 + par][:], ALU.mult).then_inc(hid_done, 1)
                dve.wait_ge(hid_done, j + 3)
                link(dve.tensor_reduce(h[:, 1:2], hid[r][:], AX.X, ALU.max, apply_absolute_value=True))
                link(dve.tensor_scalar(h[:, 2:3], h[:, 1:2], h[:, 0:1], EPS, ALU.mult, ALU.max))
                link(dve.reciprocal(h[:, 3:4], h[:, 2:3]))
                dve.tensor_scalar(h[:, 5:6], h[:, 2:3], block_w[:, 1, bass.ds(j, 1)], None, ALU.mult)
                dve.tensor_scalar(h[:, 4:5], h[:, 3:4], h[:, 0:1], QMAX, ALU.mult, ALU.mult).then_inc(h_scale_ready, 1)

            def integers(j, par, r):
                dve.wait_ge(hid_scaled, j + 1)
                dve.wait_ge(h_turned, j + 1)
                dve.tensor_scalar(hid_q[par][:], hid[r][:], MAGIC, None, ALU.subtract).then_inc(hq_ready, 1)

            for j in range(4):
                hidden(j, j)
                if j:
                    integers(j - 1, (j - 1) % 2, j - 1)
            with dve.Fori(1, NBLK // 4) as i:
                link.enter(i - 1, 16)
                for r in range(4):
                    hidden(4 * i + r, r)
                    integers(4 * i + r - 1, (r - 1) % 2, (r - 1) % 4)
                link.leave(NBLK // 4 - 1, 16)
            integers(NBLK - 1, (NBLK - 1) % 2, (NBLK - 1) % 4)

            dve.sem_inc(roped_ready, 2)
            dve.sem_inc(s_less, 4)

            def split(hi, lo, src):
                link(dve.tensor_copy(hi[:], src[:]))
                return dve.tensor_tensor(lo[:], src[:], hi[:].bitcast(F32), ALU.subtract)

            def fold(u, par):
                dve.wait_ge(qr_turned, u + 1)
                T = bank[1][0:S, 0:3 * P].rearrange("p (h a q) -> p h a q", h=2, a=2)
                dve.tensor_copy(qrwT[:, 0, :, :].rearrange("p h q -> p (h q)"), bank[1][0:S, 0:3 * P])
                for a in range(2):
                    dve.tensor_copy(qrwT[:, 1, :, :].rearrange("p h (a q) -> p h a q", a=2)[:, :, a, :], T[:, :, 1 - a, :])
                dve.tensor_copy(krT[:], bank[1][0:S, 3 * P:4 * P]).then_inc(qrwT_done, 1)
                dve.wait_ge(A_done, 2 * u + 2)
                split(AW_hi[par], AW_lo[par], AW[par]).then_inc(A_split, 1)
                dve.wait_ge(M_ready, u + 1)
                dve.tensor_tensor(MW[par][:], bank[3][:].rearrange("p (r n) -> p r n", r=2),
                                  mask_m[:, None, :].to_broadcast([P, 2, 2 * P]), ALU.mult).then_inc(M_done, 1)

            def rope(u, n):
                c, g = UNITS[n]
                dve.wait_ge(q_ready, NUNIT * u + n + 1)
                dve.wait_ge(keyed, 2 * u + 2)
                src = bank[g][:].rearrange("p (b s) -> p b s", s=S)
                for r in range(2):
                    at = C_QCOS + (2 * c + r) * S
                    ins = dve.tensor_tensor(roped[n][:, r, :].rearrange("p (b s) -> p b s", s=S), src,
                                            cst[:, None, at:at + S].to_broadcast([P, 8, S]), ALU.mult)
                ins.then_inc(roped_ready, 1)

            def less_max(u, h):
                dve.wait_ge(s_ready, u + 2)
                dve.wait_ge(prob_turned, 2 * u + 0) if not isinstance(u, int) or u else None
                src = bank[4 + h][:].rearrange("p (t l) -> p t l", l=S)
                link(dve.tensor_reduce(s_stat[:, h, 0, :], src, AX.X, ALU.max))
                dve.tensor_tensor(prob[:, :, h, :], src, s_stat[:, h, 0, :, None].to_broadcast([P, NT, S]), ALU.subtract).then_inc(s_less, 1)

            def by_sum(u, h):
                dve.wait_ge(s_exp, 2 * u + h + 1)
                link(dve.tensor_reduce(s_stat[:, h, 1, :], prob[:, :, h, :], AX.X, ALU.add))
                link(dve.reciprocal(s_stat[:, h, 2, :], s_stat[:, h, 1, :]))
                dve.tensor_tensor(prob[:, :, h, :], prob[:, :, h, :], s_stat[:, h, 2, :, None].to_broadcast([P, NT, S]), ALU.mult).then_inc(prob_ready, 1)

            fold(0, 0)
            for t in range(NT):
                dve.wait_ge(y_back[t], 32)
                link(dve.scalar_tensor_tensor(X[:, t, :], yg[:, t, 0, :], gate[:, 0, t:t + 1], X[:, t, :], ALU.mult, ALU.add))
                dve.scalar_tensor_tensor(X[:, t, :], yg[:, t, 1, :], gate[:, 1, t:t + 1], X[:, t, :],
                                         ALU.mult, ALU.add).then_inc(x2_ready, 1)
                dve.wait_ge(x2_ready, t + 1)
                link(dve.bn_stats(stats[:, t, :], X[:, t, :]))
            normalise()
            for h in range(NT // 2):
                dve.wait_ge(XNT_ready, NT // 2 + h + 1)
                dve.tensor_tensor(XNT_lo[:, :, 2 * h * P:2 * (h + 1) * P], bank[h][:].rearrange("p (k n) -> p k n", k=2),
                                  XNT_hi[:, :, 2 * h * P:2 * (h + 1) * P].bitcast(F32), ALU.subtract).then_inc(XNT_split, 1)
            for n in range(NUNIT):
                rope(0, n)
            fold(1, 1)

            def pair(u):
                for h in range(2):
                    less_max(u - 1, h)
                for h in range(2):
                    by_sum(u - 1, h)
                for n in range(NUNIT):
                    rope(u, n)

            with dve.Fori(0, NU // 2 - 1) as i:
                link.enter(i, 14)
                for u, par in ((2 * i + 1, 1), (2 * i + 2, 0)):
                    pair(u)
                    fold(u + 1, 1 - par)
                link.leave(NU // 2 - 1, 14)
            pair(NU - 1)
            for h in range(2):
                less_max(NU - 1, h)
            for h in range(2):
                by_sum(NU - 1, h)
            dve.wait_ge(d_loaded, 48)
            link(dve.tensor_scalar(w_raw[:], w_raw[:], 2.0, MAGIC, ALU.mult, ALU.add))
            link(dve.tensor_scalar(w_raw[:], w_raw[:], MAGIC, 1.0, ALU.subtract, ALU.min))
            link(dve.tensor_scalar(w_raw[:], w_raw[:], -1.0, None, ALU.max))
            dve.tensor_tensor(w_raw[:], w_raw[:], o_scale[:, :, None].to_broadcast([P, 2, H]), ALU.mult).then_inc(w_scaled_d, 1)
            dve.wait_ge(w_turned_d, 1)
            link(dve.tensor_copy(wT[:].rearrange("p k o -> p (k o)"), bank[4][:]))
            dve.sem_inc(WE_ready, 4)

            def mask(e, r):
                dve.wait_ge(m_turned, e + 5)
                dve.tensor_tensor(WE[:, bass.ds(e, 1)].rearrange("p a k o -> p (a k o)"), bank[4 + r][:],
                                  wT[:].rearrange("p k o -> p (k o)"), ALU.mult).then_inc(WE_ready, 1)

            for h in range(NT // 2):
                for r in range(2):
                    mask(4 * h + r, r)
                dve.wait_ge(o_ready, h + 1)
                for t in range(2):
                    dve.tensor_tensor(X[:, 2 * h + t, :], X[:, 2 * h + t, :], bank[h][:, t * H:(t + 1) * H], ALU.add).then_inc(x3_ready, 1)
                dve.wait_ge(x3_ready, 2 * h + 2)
                statistics((2 * h, 2 * h + 1))
                for r in range(2, 4):
                    mask(4 * h + r, r)
            normalise()
            for e in range(8):
                mask(NE_D // 2 + e, e % 4)
            dve.wait_ge(logits_ready, 2)
            link(dve.tensor_copy(RD.logits[:].rearrange("p t e -> p (t e)"), bank[0][:, 0:NT * NE_D]))
            best(dve, link, RD)
            dve.tensor_tensor(l_exp[:], RD.logits[:], RD.top[:, :, 0:1].to_broadcast([P, NT, NE_D]), ALU.subtract).then_inc(less_ready, 1)
            mark(dve, link, RD)
            dve.tensor_copy(RD.hot_b[:], RD.hot[:, 0]).then_inc(hot_ready, 1)
            dve.wait_ge(l_exp_ready, 1)
            link(dve.tensor_reduce(top_w[:, 0, :], l_exp[:], AX.X, ALU.add))
            dve.reciprocal(top_w[:, 1, :], top_w[:, 0, :]).then_inc(top_w_ready, 1)
            dve.wait_ge(counted, 2)
            def col(n, m=1):
                return ecol[:, n:n + m]

            dve.tensor_copy(col(0), bank[3][0:NE_D, 0:1]).then_inc(ecol_ready, 1)
            link(dve.tensor_copy(RD.base[:].rearrange("p t e -> p (t e)"), bank[1][:, 0:NT * NE_D]))
            n_tok, end, start = (RD.counts[:, i, :] for i in range(3))
            link(dve.tensor_copy(n_tok, bank[1][:, NT * NE_D:NT * NE_D + NE_D]))
            link(dve.tensor_tensor_scan(end, ones[:, 0:NE_D], n_tok, 0.0, ALU.mult, ALU.add))
            link(dve.tensor_tensor(start, end, n_tok, ALU.subtract))
            positions(dve, link, RD, start, 2, bank[2])
            dve.wait_ge(ecol_summed, 1)
            link(dve.tensor_copy(col(1), bank[3][0:NE_D, 1:2]))
            link(dve.tensor_tensor(col(2), col(1), col(0), ALU.add))
            link(dve.tensor_copy(ecol_i[:, 0:1], col(1)))
            link(dve.tensor_scalar(ecol_i[:, 1:2], col(2), -1.0, None, ALU.add))
            link(dve.tensor_scalar(ecol_i[:], ecol_i[:], 7, None, ALU.arith_shift_right))
            link(dve.tensor_copy(col(3, 2), ecol_i[:]))
            link(dve.tensor_scalar(col(5), col(0), 1.0, None, ALU.min))
            link(dve.tensor_tensor(col(6), col(4), col(3), ALU.subtract))
            link(dve.scalar_tensor_tensor(col(6), col(6), 1.0, col(5), ALU.add, ALU.mult))
            dve.sem_inc(ecol_ready, 1)
            for v, src in enumerate((None, col(1), col(2), cst[0:NE_D, C_ROW:C_ROW + 1])):
                if v:
                    dve.tensor_scalar(pair_v[:, v, :], ones[0:NE_D, :], src, None, ALU.mult)
            dve.wait_ge(ecol_summed, 2)
            link(dve.tensor_copy(col(7), bank[3][0:NE_D, 2:3]))
            link(dve.tensor_tensor(col(8), col(7), col(6), ALU.add))
            link(dve.tensor_tensor(col(9), col(3), col(7), ALU.subtract))
            dve.tensor_scalar(pair_v[:, 0, :], ones[0:NE_D, :], col(9), None, ALU.mult)
            iota = cst[:, C_IOTA:C_IOTA + NPAIR_D]
            link(dve.tensor_scalar(pair_hot[:, 0, :], iota[0:NE_D], col(7), None, ALU.is_ge))
            dve.scalar_tensor_tensor(pair_hot[:, 1, :], iota[0:NE_D], col(8), pair_hot[:, 0, :], ALU.is_lt, ALU.mult).then_inc(ecol_ready, 1)
            dve.wait_ge(ecol_summed, 3)
            link(dve.tensor_copy(pairs[:, 0:4, :].rearrange("p v j -> p (v j)"), bank[3][:, 64:64 + 4 * NPAIR_D]))
            blk, lo, hi, expert, row_p, mask_lo, mask_d, block = (pairs[:, i, :] for i in range(8))
            link(dve.tensor_tensor(blk, blk, iota, ALU.add))
            link(dve.tensor_scalar(row_p, blk, float(P), cst[:, C_ROW:C_ROW + 1], ALU.mult, ALU.add))
            link(dve.tensor_tensor(mask_lo, row_p, lo, ALU.is_ge))
            link(dve.tensor_tensor(mask_d, row_p, hi, ALU.is_lt))
            link(dve.tensor_tensor(mask_d, mask_d, mask_lo, ALU.mult))
            link(dve.tensor_scalar(block, blk, 0.0, float(NT - 1), ALU.max, ALU.min))
            for half, (value, bits, out) in enumerate(((expert, E_BITS, pair_ei), (block, B_BITS, pair_bi))):
                of = value.rearrange("p (g r) -> p g r", r=PACK)
                total = of[:, :, 0]
                for r in range(1, PACK):
                    into = packed[:, half, :] if r < PACK - 1 else out[:]
                    link(dve.scalar_tensor_tensor(into, of[:, :, r], float(1 << bits * r), total, ALU.mult, ALU.add))
                    total = into
            dve.sem_inc(pairs_ready, 1)
            for e in range(3 * NE_D // 4, NE_D):
                mask(e, e % 4)
            dve.sem_inc(z_added, 4)
            for b in range(NT):
                dve.wait_ge(d_gathered[b], 16)
            def blocks_of(g):
                return dve.value_load(pair_bi[0:1, bass.ds(g, 1)], min_val=0, max_val=(1 << B_BITS * PACK) - 1)

            with dve.Fori(0, NPAIR_D // 8) as i:
                packs = [blocks_of(8 // PACK * i + g) for g in range(8 // PACK)]
                for r in range(8):
                    b = (packs[r // PACK] >> (B_BITS * (r % PACK))) & (NT - 1)
                    j = 8 * i + r
                    at = dg[:, bass.ds(b, 1), H:].rearrange("p a o -> p (a o)")
                    dve.wait_ge(z_ready, j + 5)
                    dve.wait_ge(z_added, j + 4)
                    dve.scalar_tensor_tensor(at, bank[4 + r % 4][:, 0:H], mask_d[:, bass.ds(j, 1)], at, ALU.mult, ALU.add).then_inc(z_added, 1)


def constants():
    c = np.zeros((P, C_W), np.float32)
    p = np.arange(P)
    for g in range(2):
        c[:, g] = (p // HD) % 2 == g
        c[:, 2 + g] = p // S == g
    c[:, C_IOTA:C_IOTA + P] = np.arange(P)
    c[:, C_ROW] = p
    c[:, C_TILE:C_TILE + NT] = P * np.arange(NT)
    pos = np.arange(S, dtype=np.float32)

    def angles(dim):
        inv = np.float32(1.0) / np.float32(10000.0) ** (np.arange(0, dim, 2, dtype=np.float32) / np.float32(dim))
        a = np.repeat(pos[:, None] * inv[None, :], 2, axis=-1).astype(np.float32)
        return np.cos(a), np.sin(a)

    cos, sin = angles(S)
    sin = np.concatenate([-sin[:, :S // 2], sin[:, S // 2:]], axis=1)
    c[:, C_KCOS:C_KCOS + S] = cos[p % S]
    c[:, C_KSIN:C_KSIN + S] = sin[p % S]
    cos, sin = angles(QD)
    sin = np.concatenate([sin[:, QD // 2:], -sin[:, :QD // 2]], axis=1)
    for ch in range(3):
        f = (ch * P + p) % QD
        for r, table in enumerate((cos, sin)):
            at = C_QCOS + (2 * ch + r) * S
            c[:, at:at + S] = table[:, f].T
    return c


LAYOUTS = {
    "x": (NT * P, H), "ctx_512": (NT * P, S), "constants": (P, C_W),
    "L0_ffn_router_w": (NE, H), "L0_ffn_gate_w": (NE, FF, H), "L0_ffn_up_w": (NE, FF, H), "L0_ffn_down_w": (NE, H, FF),
    "L1_xattn_Wq": (NH * KD, H), "L1_xattn_w_kc_q": (NH, KD, QD), "L1_xattn_w_kc_kv": (NH, KD, S),
    "L1_xattn_W_qr": (NH * QD, S), "L1_xattn_W_kr": (NH * S, S), "L1_xattn_Wo": (H, NH * KD),
    "L1_ffn_weight": (H, H), "L1_ffn_scale": (P, 2), "L1_ffn_expert_masks": (NE_D, H, H), "L1_ffn_router_w": (NE_D, H),
}


def kernel(**inputs):
    import concourse.bacc as bacc
    from concourse.bass_utils import run_bass_kernel_spmd

    inputs = dict(inputs, constants=constants())
    inputs["L1_ffn_scale"] = np.asarray(inputs["L1_ffn_scale"]).reshape(2, P).T
    nc = bacc.Bacc("TRN2", target_bir_lowering=False, num_devices=1)
    arrays, args = {}, []
    for name, shape in LAYOUTS.items():
        a = np.ascontiguousarray(np.asarray(inputs[name]).reshape(shape))
        arrays[f"in_{name}_dram"] = a
        args.append(nc.dram_tensor(f"in_{name}_dram", a.shape, mybir.dt.from_np(a.dtype), kind="ExternalInput").ap())
    args.append(nc.dram_tensor("out_0_dram", (NT * P, H), F32, kind="ExternalOutput").ap())
    build(nc, *args)
    result = run_bass_kernel_spmd(nc, [arrays], core_ids=[0])
    return result.results[0]["out_0_dram"].reshape(2 * NT, S, H)
```
